# Optimizing a Trainium2 kernel written in Bass

```python
import numpy as np
import jax
import jax.numpy as jnp

def _softmax(x, axis=-1):
    return jax.nn.softmax(x, axis=axis)

def _gelu(x):
    return jax.nn.gelu(x, approximate=True)

def _silu(x):
    return jax.nn.silu(x)

def _sigmoid(x):
    return jax.nn.sigmoid(x)

def _layernorm(x, axis=-1, eps=1e-05):
    m = jnp.mean(x, axis=axis, keepdims=True)
    v = jnp.var(x, axis=axis, keepdims=True)
    return (x - m) / jnp.sqrt(v + eps)

def _scatter_add(tgt, idx, src, axis=0):
    return tgt.at[idx].add(src)

def _segment_sum(src, seg, n):
    return jax.ops.segment_sum(src, seg, n)
kernel_name = 'mk_hybrid_d2_jaxref_r8_116744'

def setup_inputs(seed: int=0):
    np.random.seed(seed)
    _w = jnp.asarray

    def _L0_attn_a_setup():
        import jax, jax.numpy as jnp
        import numpy as np
        EMBED_DIM = 128
        NUM_HEADS = 16
        HEAD_DIM = EMBED_DIM // NUM_HEADS
        NUM_FEATS = 32
        YAT_EPS = 0.1
        BATCH = 4
        SEQ = 512

        def _spherical_features(x, projection):
            x_norm = x / (jnp.linalg.norm(x, axis=-1, keepdims=True) + 1e-08)
            proj = jnp.einsum('bhsd,hfd->bhsf', x_norm, projection)
            return jax.nn.relu(proj) + YAT_EPS
        key = jax.random.key(seed)
        ks = jax.random.split(key, 6)
        s = 1.0 / np.sqrt(EMBED_DIM)
        return {'x': jax.random.normal(ks[0], (BATCH, SEQ, EMBED_DIM), jnp.float32), 'Wq': jax.random.normal(ks[1], (EMBED_DIM, EMBED_DIM), jnp.float32) * s, 'bq': jnp.zeros((EMBED_DIM,), jnp.float32), 'Wk': jax.random.normal(ks[2], (EMBED_DIM, EMBED_DIM), jnp.float32) * s, 'bk': jnp.zeros((EMBED_DIM,), jnp.float32), 'Wv': jax.random.normal(ks[3], (EMBED_DIM, EMBED_DIM), jnp.float32) * s, 'bv': jnp.zeros((EMBED_DIM,), jnp.float32), 'Wo': jax.random.normal(ks[4], (EMBED_DIM, EMBED_DIM), jnp.float32) * s, 'bo': jnp.zeros((EMBED_DIM,), jnp.float32), 'projection': jax.random.normal(ks[5], (NUM_HEADS, NUM_FEATS, HEAD_DIM), jnp.float32)}
    _L0_attn_a_in = _L0_attn_a_setup()

    def _L0_attn_b_setup():
        import jax, jax.numpy as jnp
        import numpy as np
        B, S, D = (4, 256, 128)
        F = 4 * D
        E = 8
        K = 2
        key = jax.random.key(seed)
        ks = jax.random.split(key, 4)
        s = 0.02
        return {'h_t': jax.random.normal(ks[0], (B, S, D), jnp.float32), 'gate_w': jax.random.normal(ks[1], (D, E), jnp.float32) * s, 'gate_b': jnp.zeros((E,), jnp.float32), 'w1': jax.random.normal(ks[2], (E, D, F), jnp.float32) * s, 'b1': jnp.zeros((E, F), jnp.float32), 'w2': jax.random.normal(ks[3], (E, F, D), jnp.float32) * s, 'b2': jnp.zeros((E, D), jnp.float32)}
    _L0_attn_b_in = _L0_attn_b_setup()

    def _L0_ffn_setup():
        import jax, jax.numpy as jnp
        import numpy as np
        DIM = 128

        def _reference_tuple_inner(x, W_r, W_k, W_v, mu_r, mu_k):
            B, T, C = x.shape
            x_prev = jnp.concatenate([jnp.zeros((B, 1, C), x.dtype), x[:, :-1, :]], axis=1)
            xr = mu_r * x + (1.0 - mu_r) * x_prev
            xk = mu_k * x + (1.0 - mu_k) * x_prev
            r = jax.nn.sigmoid(jnp.einsum('btc,dc->btd', xr, W_r))
            k = jnp.einsum('btc,dc->btd', xk, W_k)
            k_act = jnp.square(jax.nn.relu(k))
            out = r * jnp.einsum('btc,dc->btd', k_act, W_v)
            new_state = x[:, -1, :]
            return (out, new_state)
        key = jax.random.key(seed)
        ks = jax.random.split(key, 6)
        B, T, C = (8, 256, DIM)
        x = jax.random.normal(ks[0], (B, T, C), dtype=jnp.float32)
        s = 1.0 / np.sqrt(C)
        W_r = jax.random.uniform(ks[1], (C, C), jnp.float32, -s, s)
        W_k = jax.random.uniform(ks[2], (C, C), jnp.float32, -s, s)
        W_v = jax.random.uniform(ks[3], (C, C), jnp.float32, -s, s)
        mu_r = jax.random.uniform(ks[4], (C,), jnp.float32)
        mu_k = jax.random.uniform(ks[5], (C,), jnp.float32)
        return {'x': x, 'W_r': W_r, 'W_k': W_k, 'W_v': W_v, 'mu_r': mu_r, 'mu_k': mu_k}
    _L0_ffn_in = _L0_ffn_setup()

    def _L1_attn_a_setup():
        import jax, jax.numpy as jnp
        import numpy as np
        D_MODEL = 128
        NUM_HEADS = 16
        HEAD_DIM = D_MODEL // NUM_HEADS
        D_FF = 512
        EPS = 1e-05

        def layer_norm(x, gamma, beta):
            mu = jnp.mean(x, axis=-1, keepdims=True)
            var = jnp.mean((x - mu) ** 2, axis=-1, keepdims=True)
            return (x - mu) * jax.lax.rsqrt(var + EPS) * gamma + beta

        def apply_rope(t):
            S, d = (t.shape[-2], t.shape[-1])
            inv_freq = 1.0 / 10000.0 ** (jnp.arange(0, d, 2, dtype=jnp.float32) / d)
            angles = jnp.arange(S, dtype=jnp.float32)[:, None] * inv_freq[None, :]
            sin, cos = (jnp.sin(angles), jnp.cos(angles))
            tp = t.reshape(*t.shape[:-1], d // 2, 2)
            t0, t1 = (tp[..., 0], tp[..., 1])
            rot = jnp.stack([t0 * cos - t1 * sin, t0 * sin + t1 * cos], axis=-1)
            return rot.reshape(t.shape)
        key = jax.random.key(seed)
        ks = jax.random.split(key, 18)
        s = 0.02
        d, f = (D_MODEL, D_FF)
        return {'x': jax.random.normal(ks[0], (2, 256, d), dtype=jnp.float32), 'Wq': jax.random.normal(ks[1], (d, d), dtype=jnp.float32) * s, 'bq': jnp.zeros((d,), jnp.float32), 'Wk': jax.random.normal(ks[2], (d, d), dtype=jnp.float32) * s, 'bk': jnp.zeros((d,), jnp.float32), 'Wv': jax.random.normal(ks[3], (d, d), dtype=jnp.float32) * s, 'bv': jnp.zeros((d,), jnp.float32), 'Wo': jax.random.normal(ks[4], (d, d), dtype=jnp.float32) * s, 'bo': jnp.zeros((d,), jnp.float32), 'W1': jax.random.normal(ks[5], (d, f), dtype=jnp.float32) * s, 'b1': jnp.zeros((f,), jnp.float32), 'W2': jax.random.normal(ks[6], (f, d), dtype=jnp.float32) * s, 'b2': jnp.zeros((d,), jnp.float32), 'g1': jnp.ones((d,), jnp.float32), 'beta1': jnp.zeros((d,), jnp.float32), 'g2': jnp.ones((d,), jnp.float32), 'beta2': jnp.zeros((d,), jnp.float32)}
    _L1_attn_a_in = _L1_attn_a_setup()

    def _L1_attn_b_setup():
        import jax, jax.numpy as jnp
        import numpy as np
        B, T, V, C, NB = (8, 256, 128, 128, 32)
        key = jax.random.key(seed)
        ks = jax.random.split(key, 6)
        x = jax.random.normal(ks[0], (B, T, V), jnp.float32)
        basis = jax.random.normal(ks[1], (V, 2 * NB), jnp.float32)
        q_coeffs = jax.random.normal(ks[2], (C, 2 * NB), jnp.float32) * 0.02
        k_coeffs = jax.random.normal(ks[3], (C, 2 * NB), jnp.float32) * 0.02
        v_coeffs = jax.random.normal(ks[4], (C, 2 * NB), jnp.float32) * 0.02
        o_coeffs = jax.random.normal(ks[5], (C, 2 * NB), jnp.float32) * 0.02
        decay = jnp.float32(0.95)
        out_scale = jnp.float32(0.1)
        return {'x': x, 'basis': basis, 'q_coeffs': q_coeffs, 'k_coeffs': k_coeffs, 'v_coeffs': v_coeffs, 'o_coeffs': o_coeffs, 'decay': decay, 'out_scale': out_scale}
    _L1_attn_b_in = _L1_attn_b_setup()

    def _L1_ffn_setup():
        import jax, jax.numpy as jnp
        import numpy as np
        D_MODEL = 128
        D_HIDDEN = 512
        NUM_EXPERTS = 8
        B, T = (2, 256)
        key = jax.random.key(seed)
        ks = jax.random.split(key, 8)
        s = 0.02
        x = jax.random.normal(ks[0], (B, T, D_MODEL), dtype=jnp.float32)
        Wg = jax.random.normal(ks[1], (D_MODEL, NUM_EXPERTS), dtype=jnp.float32) * s
        bg = jnp.zeros((NUM_EXPERTS,), dtype=jnp.float32)
        W1 = jax.random.normal(ks[2], (NUM_EXPERTS, D_MODEL, D_HIDDEN), dtype=jnp.float32) * s
        b1 = jnp.zeros((NUM_EXPERTS, D_HIDDEN), dtype=jnp.float32)
        W2 = jax.random.normal(ks[3], (NUM_EXPERTS, D_HIDDEN, D_MODEL), dtype=jnp.float32) * s
        b2 = jnp.zeros((NUM_EXPERTS, D_MODEL), dtype=jnp.float32)
        return {'x': x, 'Wg': Wg, 'bg': bg, 'W1': W1, 'b1': b1, 'W2': W2, 'b2': b2}
    _L1_ffn_in = _L1_ffn_setup()
    _d = {'L0_attn_a_x': _L0_attn_a_in['x'], 'L0_attn_a_Wq': _L0_attn_a_in['Wq'], 'L0_attn_a_bq': _L0_attn_a_in['bq'], 'L0_attn_a_Wk': _L0_attn_a_in['Wk'], 'L0_attn_a_bk': _L0_attn_a_in['bk'], 'L0_attn_a_Wv': _L0_attn_a_in['Wv'], 'L0_attn_a_bv': _L0_attn_a_in['bv'], 'L0_attn_a_Wo': _L0_attn_a_in['Wo'], 'L0_attn_a_bo': _L0_attn_a_in['bo'], 'L0_attn_a_projection': _L0_attn_a_in['projection'], 'L0_attn_b_gate_w': _L0_attn_b_in['gate_w'], 'L0_attn_b_gate_b': _L0_attn_b_in['gate_b'], 'L0_attn_b_w1': _L0_attn_b_in['w1'], 'L0_attn_b_b1': _L0_attn_b_in['b1'], 'L0_attn_b_w2': _L0_attn_b_in['w2'], 'L0_attn_b_b2': _L0_attn_b_in['b2'], 'L0_ffn_W_r': _L0_ffn_in['W_r'], 'L0_ffn_W_k': _L0_ffn_in['W_k'], 'L0_ffn_W_v': _L0_ffn_in['W_v'], 'L0_ffn_mu_r': _L0_ffn_in['mu_r'], 'L0_ffn_mu_k': _L0_ffn_in['mu_k'], 'L1_attn_a_Wq': _L1_attn_a_in['Wq'], 'L1_attn_a_bq': _L1_attn_a_in['bq'], 'L1_attn_a_Wk': _L1_attn_a_in['Wk'], 'L1_attn_a_bk': _L1_attn_a_in['bk'], 'L1_attn_a_Wv': _L1_attn_a_in['Wv'], 'L1_attn_a_bv': _L1_attn_a_in['bv'], 'L1_attn_a_Wo': _L1_attn_a_in['Wo'], 'L1_attn_a_bo': _L1_attn_a_in['bo'], 'L1_attn_a_W1': _L1_attn_a_in['W1'], 'L1_attn_a_b1': _L1_attn_a_in['b1'], 'L1_attn_a_W2': _L1_attn_a_in['W2'], 'L1_attn_a_b2': _L1_attn_a_in['b2'], 'L1_attn_a_g1': _L1_attn_a_in['g1'], 'L1_attn_a_beta1': _L1_attn_a_in['beta1'], 'L1_attn_a_g2': _L1_attn_a_in['g2'], 'L1_attn_a_beta2': _L1_attn_a_in['beta2'], 'L1_attn_b_basis': _L1_attn_b_in['basis'], 'L1_attn_b_q_coeffs': _L1_attn_b_in['q_coeffs'], 'L1_attn_b_k_coeffs': _L1_attn_b_in['k_coeffs'], 'L1_attn_b_v_coeffs': _L1_attn_b_in['v_coeffs'], 'L1_attn_b_o_coeffs': _L1_attn_b_in['o_coeffs'], 'L1_attn_b_decay': _L1_attn_b_in['decay'], 'L1_attn_b_out_scale': _L1_attn_b_in['out_scale'], 'L1_ffn_Wg': _L1_ffn_in['Wg'], 'L1_ffn_bg': _L1_ffn_in['bg'], 'L1_ffn_W1': _L1_ffn_in['W1'], 'L1_ffn_b1': _L1_ffn_in['b1'], 'L1_ffn_W2': _L1_ffn_in['W2'], 'L1_ffn_b2': _L1_ffn_in['b2']}
    _x0 = _d['L0_attn_a_x']
    _d['L0_attn_a_x'] = jax.random.normal(jax.random.fold_in(jax.random.key(seed), 1), (2, 1024, 128), dtype=_x0.dtype)
    del _x0
    return _d

def reference(L0_attn_a_x, L0_attn_a_Wq, L0_attn_a_bq, L0_attn_a_Wk, L0_attn_a_bk, L0_attn_a_Wv, L0_attn_a_bv, L0_attn_a_Wo, L0_attn_a_bo, L0_attn_a_projection, L0_attn_b_gate_w, L0_attn_b_gate_b, L0_attn_b_w1, L0_attn_b_b1, L0_attn_b_w2, L0_attn_b_b2, L0_ffn_W_r, L0_ffn_W_k, L0_ffn_W_v, L0_ffn_mu_r, L0_ffn_mu_k, L1_attn_a_Wq, L1_attn_a_bq, L1_attn_a_Wk, L1_attn_a_bk, L1_attn_a_Wv, L1_attn_a_bv, L1_attn_a_Wo, L1_attn_a_bo, L1_attn_a_W1, L1_attn_a_b1, L1_attn_a_W2, L1_attn_a_b2, L1_attn_a_g1, L1_attn_a_beta1, L1_attn_a_g2, L1_attn_a_beta2, L1_attn_b_basis, L1_attn_b_q_coeffs, L1_attn_b_k_coeffs, L1_attn_b_v_coeffs, L1_attn_b_o_coeffs, L1_attn_b_decay, L1_attn_b_out_scale, L1_ffn_Wg, L1_ffn_bg, L1_ffn_W1, L1_ffn_b1, L1_ffn_W2, L1_ffn_b2):

    def _L0_attn_a_ref(x, Wq, bq, Wk, bk, Wv, bv, Wo, bo, projection):
        import jax, jax.numpy as jnp
        import numpy as np
        EMBED_DIM = 128
        NUM_HEADS = 16
        HEAD_DIM = EMBED_DIM // NUM_HEADS
        NUM_FEATS = 32
        YAT_EPS = 0.1
        BATCH = 4
        SEQ = 512

        def _spherical_features(x, projection):
            x_norm = x / (jnp.linalg.norm(x, axis=-1, keepdims=True) + 1e-08)
            proj = jnp.einsum('bhsd,hfd->bhsf', x_norm, projection)
            return jax.nn.relu(proj) + YAT_EPS
        b, s, _ = x.shape

        def heads(t):
            return jnp.transpose(t.reshape(b, s, NUM_HEADS, HEAD_DIM), (0, 2, 1, 3))
        Q = heads(x @ Wq + bq)
        K = heads(x @ Wk + bk)
        V = heads(x @ Wv + bv)
        Qp = _spherical_features(Q, projection)
        Kp = _spherical_features(K, projection)
        KV = jnp.einsum('bhsf,bhsd->bhfd', Kp, V)
        QKV = jnp.einsum('bhsf,bhfd->bhsd', Qp, KV)
        K_sum = jnp.sum(Kp, axis=2)
        normalizer = jnp.einsum('bhsf,bhf->bhs', Qp, K_sum)[..., None]
        normalizer = jnp.maximum(normalizer, 1e-06)
        out = QKV / normalizer
        out = jnp.transpose(out, (0, 2, 1, 3)).reshape(b, s, EMBED_DIM)
        return out @ Wo + bo

    def _L0_attn_b_ref(h_t, gate_w, gate_b, w1, b1, w2, b2):
        import jax, jax.numpy as jnp
        import numpy as np
        B, S, D = (4, 256, 128)
        F = 4 * D
        E = 8
        K = 2
        Bb, Ss, Dd = h_t.shape
        x = h_t.reshape(Bb * Ss, Dd)
        logits = x @ gate_w + gate_b
        probs = jax.nn.softmax(logits, axis=1)
        topw, topi = jax.lax.top_k(probs, K)
        topw = topw / topw.sum(axis=-1, keepdims=True)
        topw = topw.astype(h_t.dtype)
        hid = jax.nn.gelu(jnp.einsum('nd,edf->enf', x, w1) + b1[:, None, :])
        out = jnp.einsum('enf,efd->end', hid, w2) + b2[:, None, :]
        sel = topi[None, :, :] == jnp.arange(E)[:, None, None]
        ew = jnp.where(sel, topw[None, :, :], 0.0).sum(axis=-1)
        tmask = jnp.any(sel, axis=-1).astype(h_t.dtype)
        final = (out * ew[..., None] * tmask[..., None]).sum(axis=0)
        return final.reshape(Bb, Ss, Dd)

    def _L0_ffn_ref(x, W_r, W_k, W_v, mu_r, mu_k):
        import jax, jax.numpy as jnp
        import numpy as np
        DIM = 128

        def _reference_tuple_inner(x, W_r, W_k, W_v, mu_r, mu_k):
            B, T, C = x.shape
            x_prev = jnp.concatenate([jnp.zeros((B, 1, C), x.dtype), x[:, :-1, :]], axis=1)
            xr = mu_r * x + (1.0 - mu_r) * x_prev
            xk = mu_k * x + (1.0 - mu_k) * x_prev
            r = jax.nn.sigmoid(jnp.einsum('btc,dc->btd', xr, W_r))
            k = jnp.einsum('btc,dc->btd', xk, W_k)
            k_act = jnp.square(jax.nn.relu(k))
            out = r * jnp.einsum('btc,dc->btd', k_act, W_v)
            new_state = x[:, -1, :]
            return (out, new_state)
        return _reference_tuple_inner(x, W_r, W_k, W_v, mu_r, mu_k)[0]

    def _L1_attn_a_ref(x, Wq, bq, Wk, bk, Wv, bv, Wo, bo, W1, b1, W2, b2, g1, beta1, g2, beta2):
        import jax, jax.numpy as jnp
        import numpy as np
        D_MODEL = 128
        NUM_HEADS = 16
        HEAD_DIM = D_MODEL // NUM_HEADS
        D_FF = 512
        EPS = 1e-05

        def layer_norm(x, gamma, beta):
            mu = jnp.mean(x, axis=-1, keepdims=True)
            var = jnp.mean((x - mu) ** 2, axis=-1, keepdims=True)
            return (x - mu) * jax.lax.rsqrt(var + EPS) * gamma + beta

        def apply_rope(t):
            S, d = (t.shape[-2], t.shape[-1])
            inv_freq = 1.0 / 10000.0 ** (jnp.arange(0, d, 2, dtype=jnp.float32) / d)
            angles = jnp.arange(S, dtype=jnp.float32)[:, None] * inv_freq[None, :]
            sin, cos = (jnp.sin(angles), jnp.cos(angles))
            tp = t.reshape(*t.shape[:-1], d // 2, 2)
            t0, t1 = (tp[..., 0], tp[..., 1])
            rot = jnp.stack([t0 * cos - t1 * sin, t0 * sin + t1 * cos], axis=-1)
            return rot.reshape(t.shape)
        B, S, d = x.shape
        H, hd = (NUM_HEADS, HEAD_DIM)
        x_norm = layer_norm(x, g1, beta1)
        q = (x_norm @ Wq + bq).reshape(B, S, H, hd).transpose(0, 2, 1, 3)
        k = (x_norm @ Wk + bk).reshape(B, S, H, hd).transpose(0, 2, 1, 3)
        v = (x_norm @ Wv + bv).reshape(B, S, H, hd).transpose(0, 2, 1, 3)
        q = apply_rope(q)
        k = apply_rope(k)
        q = q * (1.0 / jnp.sqrt(jnp.float32(hd)))
        scores = jnp.einsum('bhqd,bhkd->bhqk', q, k)
        attn = jax.nn.softmax(scores, axis=-1)
        out = jnp.einsum('bhqk,bhkd->bhqd', attn, v)
        out = out.transpose(0, 2, 1, 3).reshape(B, S, d)
        attn_out = out @ Wo + bo
        x = x + attn_out
        x_norm2 = layer_norm(x, g2, beta2)
        ffn = jax.nn.relu(x_norm2 @ W1 + b1) @ W2 + b2
        return x + ffn

    def _L1_attn_b_ref(x, basis, q_coeffs, k_coeffs, v_coeffs, o_coeffs, decay, out_scale):
        import jax, jax.numpy as jnp
        import numpy as np
        B, T, V, C, NB = (8, 256, 128, 128, 32)
        q_w = jax.nn.softmax(basis @ q_coeffs.T, axis=0)
        k_w = jax.nn.softmax(basis @ k_coeffs.T, axis=0)
        v_w = jax.nn.softmax(basis @ v_coeffs.T, axis=0)
        o_w = basis @ o_coeffs.T
        q = x @ q_w
        k = x @ k_w
        v = x @ v_w
        d = jax.nn.sigmoid(decay)
        M0 = jnp.zeros((x.shape[0], q_w.shape[1], q_w.shape[1]), x.dtype)

        def step(M, qkv_t):
            q_t, k_t, v_t = qkv_t
            retrieved = jnp.einsum('bc,bcd->bd', q_t, M)
            M_new = d * M + jnp.einsum('bc,bd->bcd', k_t, v_t)
            return (M_new, retrieved)
        qT = jnp.swapaxes(q, 0, 1)
        kT = jnp.swapaxes(k, 0, 1)
        vT = jnp.swapaxes(v, 0, 1)
        _, rs = jax.lax.scan(step, M0, (qT, kT, vT))
        retrieved = jnp.swapaxes(rs, 0, 1)
        return retrieved @ o_w.T * out_scale

    def _L1_ffn_ref(x, Wg, bg, W1, b1, W2, b2):
        import jax, jax.numpy as jnp
        import numpy as np
        D_MODEL = 128
        D_HIDDEN = 512
        NUM_EXPERTS = 8
        B, T = (2, 256)
        gate_logits = jnp.einsum('btd,de->bte', x, Wg) + bg
        gate_scores = jax.nn.softmax(gate_logits, axis=-1)
        top1_idx = jnp.argmax(gate_scores, axis=-1)
        top1_mask = jax.nn.one_hot(top1_idx, NUM_EXPERTS, dtype=x.dtype)
        top1_weight = jnp.sum(gate_scores * top1_mask, axis=-1, keepdims=True)
        h = jax.nn.silu(jnp.einsum('btd,edh->bteh', x, W1) + b1)
        o = jnp.einsum('bteh,ehd->bted', h, W2) + b2
        y = jnp.sum(o * top1_mask[..., None], axis=2) * top1_weight
        return y
    x = L0_attn_a_x
    x = x + _L0_attn_a_ref(_layernorm(x, axis=-1), L0_attn_a_Wq, L0_attn_a_bq, L0_attn_a_Wk, L0_attn_a_bk, L0_attn_a_Wv, L0_attn_a_bv, L0_attn_a_Wo, L0_attn_a_bo, L0_attn_a_projection)
    x = x + _L0_ffn_ref(_layernorm(x, axis=-1), L0_ffn_W_r, L0_ffn_W_k, L0_ffn_W_v, L0_ffn_mu_r, L0_ffn_mu_k)
    x = x + _L0_attn_b_ref(_layernorm(x, axis=-1), L0_attn_b_gate_w, L0_attn_b_gate_b, L0_attn_b_w1, L0_attn_b_b1, L0_attn_b_w2, L0_attn_b_b2)
    x = x + _L0_ffn_ref(_layernorm(x, axis=-1), L0_ffn_W_r, L0_ffn_W_k, L0_ffn_W_v, L0_ffn_mu_r, L0_ffn_mu_k)
    x = x + _L1_attn_a_ref(_layernorm(x, axis=-1), L1_attn_a_Wq, L1_attn_a_bq, L1_attn_a_Wk, L1_attn_a_bk, L1_attn_a_Wv, L1_attn_a_bv, L1_attn_a_Wo, L1_attn_a_bo, L1_attn_a_W1, L1_attn_a_b1, L1_attn_a_W2, L1_attn_a_b2, L1_attn_a_g1, L1_attn_a_beta1, L1_attn_a_g2, L1_attn_a_beta2)
    x = x + _L1_ffn_ref(_layernorm(x, axis=-1), L1_ffn_Wg, L1_ffn_bg, L1_ffn_W1, L1_ffn_b1, L1_ffn_W2, L1_ffn_b2)
    x = x + _L1_attn_b_ref(_layernorm(x, axis=-1), L1_attn_b_basis, L1_attn_b_q_coeffs, L1_attn_b_k_coeffs, L1_attn_b_v_coeffs, L1_attn_b_o_coeffs, L1_attn_b_decay, L1_attn_b_out_scale)
    x = x + _L1_ffn_ref(_layernorm(x, axis=-1), L1_ffn_Wg, L1_ffn_bg, L1_ffn_W1, L1_ffn_b1, L1_ffn_W2, L1_ffn_b2)
    return x

_drawn_inputs = setup_inputs


def setup_inputs(seed=0):
    import zlib

    import numpy as np

    out = dict(_drawn_inputs(seed))
    spreads = {'L0_attn_a_bq': (0.0, 0.8),
     'L0_attn_a_bk': (0.0, 0.8),
     'L0_attn_a_bv': (0.0, 0.1),
     'L0_attn_a_bo': (0.0, 0.1),
     'L0_attn_b_gate_b': (0.0, 0.1),
     'L0_attn_b_b1': (0.0, 0.457),
     'L0_attn_b_b2': (0.0, 0.1),
     'L1_attn_a_bq': (0.0, 0.8),
     'L1_attn_a_bk': (0.0, 0.8),
     'L1_attn_a_bv': (0.0, 0.712),
     'L1_attn_a_bo': (0.0, 0.1),
     'L1_attn_a_b1': (0.0, 0.49),
     'L1_attn_a_b2': (0.0, 0.1),
     'L1_attn_a_g1': (1.0, 0.6),
     'L1_attn_a_beta1': (0.0, 0.8),
     'L1_attn_a_g2': (1.0, 0.6),
     'L1_attn_a_beta2': (0.0, 0.8),
     'L1_ffn_bg': (0.0, 0.527),
     'L1_ffn_b1': (0.0, 0.8),
     'L1_ffn_b2': (0.0, 0.444)}
    factors = {'L0_ffn_mu_r': 3.045,
     'L1_attn_a_Wq': 8.0,
     'L1_attn_a_Wk': 8.0,
     'L1_attn_a_Wv': 8.0,
     'L1_attn_a_Wo': 4.618,
     'L1_attn_b_basis': 8.0,
     'L1_attn_b_q_coeffs': 8.0,
     'L1_attn_b_k_coeffs': 8.0,
     'L1_attn_b_v_coeffs': 8.0,
     'L1_attn_b_o_coeffs': 8.0,
     'L1_ffn_Wg': 2.93,
     'L1_ffn_W1': 6.217,
     'L1_ffn_W2': 5.623}
    for name, (base, spread) in spreads.items():
        noise = np.random.default_rng([zlib.crc32(name.encode()), seed]).standard_normal(out[name].shape)
        drawn = base * np.exp(spread * noise) if base else spread * noise
        out[name] = jnp.asarray(drawn.astype(out[name].dtype))
    for name, factor in factors.items():
        out[name] = (out[name] * factor).astype(out[name].dtype)
    return out
```

```python
from contextlib import ExitStack

import numpy as np

import concourse.bass as bass
from concourse import mybir

P = 128
F32 = mybir.dt.float32
F16 = mybir.dt.float16
BF16 = mybir.dt.bfloat16
I32 = mybir.dt.int32
ALU = mybir.AluOpType
ACT = mybir.ActivationFunctionType
AX = mybir.AxisListType

B, S, D = 2, 1024, 128
N = B * S
T = N // P
TB = T // B
H, HD = 16, 8
FEAT = 32
NE = 8
FF = 512
FC = FF // P
ARENA = 28608
HG = 4
NG = H // HG




class Turn:

    def __init__(self, bank, before):
        self.bank, self.before = bank, before


class Core:

    def __init__(self, nc, ctx):
        self.nc, self.ctx = nc, ctx
        self.psum = ctx.enter_context(nc.psum_tensor("psum", [P, 8, 512], F32))
        self.filled = [self.sem(f"bank{i}_filled") for i in range(8)]
        self.emptied = [self.sem(f"bank{i}_emptied") for i in range(8)]
        self.uses = [0] * 8
        self.next_bank = 0
        self.vector_steps = self.sem("vector_steps")
        self.scalar_steps = self.sem("scalar_steps")
        self.pool_steps = self.sem("pool_steps")
        self.variance = self.sem("ln_variance")
        self.root = self.sem("ln_root")
        self.eps = self.sb("eps", [P, 1])
        self.eps_in = self.sem("eps_in")
        self.norms_v = self.norms_s = 0
        self.steps = {"v": 0, "s": 0, "p": 0}
        self.x = self.sb("x", [P, T, D])
        self.xn = self.sb("xn", [P, T, D])
        self.xnT = self.sb("xnT", [P, B, 1 + S])
        self.expert_w = self.sb("expert_w", [P, 2 * NE * FF])
        self.arena = self.sb("arena", [P, ARENA])
        self.stats = self.sb("stats", [P, T, 6])
        self.ln = self.sb("ln_small", [P, 8, T])

    def sem(self, name):
        return self.ctx.enter_context(self.nc.semaphore(name))

    def sb(self, name, shape, dt=F32):
        return self.ctx.enter_context(self.nc.sbuf_tensor(name, shape, dt))

    def turns(self, n):
        out = []
        for _ in range(n):
            b = self.next_bank
            out.append(Turn(b, self.uses[b]))
            self.uses[b] += 1
            self.next_bank = (b + 1) % 8
        return out

    def claim(self, pe, turn):
        if turn.before:
            pe.wait_ge(self.emptied[turn.bank], turn.before)

    def result(self, eng, turn):
        eng.wait_ge(self.filled[turn.bank], turn.before + 1)

    def moved(self, eng, turn):
        eng.wait_ge(self.emptied[turn.bank], turn.before + 1)

    def vstep(self, ins):
        self.steps["v"] += 1
        ins.then_inc(self.vector_steps, 1)
        self.nc.vector.wait_ge(self.vector_steps, self.steps["v"])

    def vmark(self, ins):
        self.steps["v"] += 1
        ins.then_inc(self.vector_steps, 1)

    def vsync(self):
        self.nc.vector.wait_ge(self.vector_steps, self.steps["v"])

    def pstep(self, ins):
        self.steps["p"] += 1
        ins.then_inc(self.pool_steps, 1)
        self.nc.gpsimd.wait_ge(self.pool_steps, self.steps["p"])

    def sstep(self, ins):
        self.steps["s"] += 1
        ins.then_inc(self.scalar_steps, 1)
        self.nc.scalar.wait_ge(self.scalar_steps, self.steps["s"])


def carve(core, at, shape, dt=F32):
    n = int(np.prod(shape))
    words = n * mybir.dt.size(dt) // 4 if False else (n // 2 if dt in (F16, BF16) else n)
    assert at + words <= ARENA, (at, words)
    v = core.arena[:, at:at + words]
    if dt is not F32:
        v = v.bitcast(dt)
    if len(shape) > 1:
        names = [f"d{i}" for i in range(len(shape))]
        v = v.rearrange(f"p ({' '.join(names)}) -> p {' '.join(names)}", **dict(zip(names[1:], shape[1:])))
    return v, at + words


def layer_norm(core, src, out, b):
    nc, ln = core.nc, core.ln
    t0, t1 = b * TB, (b + 1) * TB
    for t in range(t0, t1):
        core.vmark(nc.vector.bn_stats(core.stats[:, t, :], src[:, t, :]))
    core.vsync()
    st = core.stats
    me, mo = st[:, t0:t1, 1], st[:, t0:t1, 4]
    me2, mo2 = st[:, t0:t1, 2], st[:, t0:t1, 5]
    mean, diff, m2, var, rstd = (ln[:, i, t0:t1] for i in range(5))
    core.vmark(nc.vector.tensor_tensor(mean, me, mo, ALU.add))
    core.vmark(nc.vector.tensor_tensor(diff, me, mo, ALU.subtract))
    core.vstep(nc.vector.tensor_tensor(m2, me2, mo2, ALU.add))
    core.vmark(nc.vector.tensor_scalar(mean, mean, 0.5, None, ALU.mult))
    core.vstep(nc.vector.scalar_tensor_tensor(out=var, in0=diff, scalar=0.25, in1=diff, op0=ALU.mult, op1=ALU.mult))
    nc.vector.scalar_tensor_tensor(out=var, in0=m2, scalar=1.0 / D, in1=var, op0=ALU.mult,
                                   op1=ALU.add).then_inc(core.variance, 1)
    core.norms_v += 1
    nc.vector.wait_ge(core.root, core.norms_v)
    core.vstep(nc.vector.reciprocal(rstd, rstd))
    core.vstep(nc.vector.tensor_tensor(out[:, t0:t1, :], src[:, t0:t1, :],
                                       mean.unsqueeze(2).to_broadcast([P, TB, D]), ALU.subtract))
    return nc.vector.tensor_tensor(out[:, t0:t1, :], out[:, t0:t1, :],
                                   rstd.unsqueeze(2).to_broadcast([P, TB, D]), ALU.mult)


def deviation(core, b, eps=1e-5):
    ln, tiles = core.ln, slice(b * TB, (b + 1) * TB)
    core.norms_s += 1
    core.nc.scalar.wait_ge(core.variance, core.norms_s)
    core.nc.scalar.activation(ln[:, 4, tiles], ln[:, 3, tiles], ACT.Sqrt, bias=core.eps[:, 0:1]).then_inc(core.root, 1)


def transpose_tiles(core, pe, turn, pieces, identity):
    core.claim(pe, turn)
    for i, piece in enumerate(pieces):
        last = core.nc.tensor.transpose(core.psum[:, turn.bank, i * P:(i + 1) * P], piece, identity)
    last.then_inc(core.filled[turn.bank], 1)


class LinearAttention:

    def __init__(self, core, w):
        self.core, self.w = core, w
        s = core.sem
        self.normed = s("la_normed")
        self.ones = s("la_ones")
        self.squared = s("la_squared")
        self.sums = s("la_sums")
        self.norms = s("la_norms")
        self.unit = s("la_unit")
        self.qfeat_in = s("la_qfeat")
        self.att_in = s("la_att")
        self.bias_in = s("la_bias")
        at = 0
        self.qkv, at = carve(core, at, [T, 400])
        self.sq, _ = carve(core, at, [B, TB, 256])
        self.att, at = carve(core, at, [T, D])
        self.attT, at = carve(core, at, [N])
        self.qT, at = carve(core, at, [2, N])
        self.kfeat, at = carve(core, at, [TB, H * FEAT])
        self.qfeat, at = carve(core, at, [NG, N])
        self.kv, at = carve(core, at, [B, NG, D + H])
        self.rn, at = carve(core, at, [B, TB, 2 * H])
        self.den, at = carve(core, at, [2, 2, H])
        self.t = []
        for b in range(B):
            self.t.append({"xT": core.turns(2), "qkv": core.turns(8)})
        for b in range(B):
            self.t[b].update(qkT=core.turns(4), kfeat=core.turns(8), qfeat=core.turns(8))
            self.t[b].update(kv=core.turns(2), out=core.turns(4))
            self.t[b].update(attT=core.turns(2), wo=core.turns(2))

    def tensor(self, pe):
        core, w, nc = self.core, self.w, self.core.nc
        ps = core.psum
        for b in range(B):
            pe.wait_ge(self.normed, b + 1)
            if b == 0:
                pe.wait_ge(w.first_in, w.first_all)
            for g, turn in enumerate(self.t[b]["xT"]):
                t = b * TB + 4 * g
                transpose_tiles(core, pe, turn, [core.xn[:, t + i, :] for i in range(4)], w.ident[:, :])
            for i, turn in enumerate(self.t[b]["qkv"]):
                core.claim(pe, turn)
                core.moved(pe, self.t[b]["xT"][i // 4])
                nc.tensor.matmul(ps[:, turn.bank, 0:384], core.xnT[:, b, 1 + i * P:1 + (i + 1) * P],
                                 w.la_wqkv[:, :], start=True, stop=True).then_inc(core.filled[turn.bank], 1)
        for b in range(B):
            tb = self.t[b]
            pe.wait_ge(self.unit, b + 1)
            for g, turn in enumerate(tb["qkT"]):
                t, c = b * TB + 4 * (g % 2), D * (g // 2)
                transpose_tiles(core, pe, turn, [self.qkv[:, t + i, c:c + D] for i in range(4)], w.ident[:, :])
            if b == 0:
                pe.wait_ge(w.proj_in, 1)
            for i, turn in enumerate(tb["kfeat"]):
                core.claim(pe, turn)
                core.moved(pe, tb["qkT"][2 + i // 4])
                nc.tensor.matmul(ps[:, turn.bank, :], self.qT[:, 1, b * S + i * P:b * S + (i + 1) * P],
                                 w.proj[:, :, :], start=True, stop=True).then_inc(core.filled[turn.bank], 1)
            for i, turn in enumerate(tb["qfeat"]):
                c, half = i // 2, i % 2
                core.claim(pe, turn)
                nc.tensor.matmul(ps[:, turn.bank, :], w.proj[:, HG * c:HG * c + HG, :],
                                 self.qT[:, 0, b * S + 512 * half:b * S + 512 * (half + 1)],
                                 start=True, stop=True).then_inc(core.filled[turn.bank], 1)
            if b == 0:
                pe.wait_ge(self.ones, 1)
            for r, turn in enumerate(tb["kv"]):
                core.claim(pe, turn)
                for c in (2 * r, 2 * r + 1):
                    for i in range(TB):
                        if c == 0:
                            core.moved(pe, tb["kfeat"][i])
                        last = nc.tensor.matmul(ps[:, turn.bank, (c % 2) * 144:(c % 2 + 1) * 144],
                                                self.kfeat[:, i, c * P:(c + 1) * P],
                                                self.qkv[:, b * TB + i, 256:400],
                                                start=(i == 0), stop=(i == TB - 1))
                last.then_inc(core.filled[turn.bank], 1)
            core.moved(pe, tb["kv"][0])
            core.moved(pe, tb["kv"][1])
            pe.wait_ge(self.qfeat_in, 8 * b + 8)
            for r, turn in enumerate(tb["out"]):
                core.claim(pe, turn)
                for j in range(2):
                    t = b * TB + 2 * r + j
                    for c in range(NG):
                        last = nc.tensor.matmul(ps[:, turn.bank, j * 144:(j + 1) * 144],
                                                self.qfeat[:, c, t * P:(t + 1) * P], self.kv[:, b, c, :],
                                                start=(c == 0), stop=(c == NG - 1))
                last.then_inc(core.filled[turn.bank], 1)
            for g, turn in enumerate(tb["attT"]):
                t = b * TB + 4 * g
                core.moved(pe, tb["out"][2 * g])
                core.moved(pe, tb["out"][2 * g + 1])
                transpose_tiles(core, pe, turn, [self.att[:, t + i, :] for i in range(4)], w.ident[:, :])
            for g, turn in enumerate(tb["wo"]):
                core.claim(pe, turn)
                core.moved(pe, tb["attT"][g])
                for i in range(4):
                    t = b * TB + 4 * g + i
                    last = nc.tensor.matmul(ps[:, turn.bank, i * D:(i + 1) * D], self.attT[:, t * P:(t + 1) * P],
                                            w.la_wo[:, :], start=True, stop=True)
                last.then_inc(core.filled[turn.bank], 1)

    def scalar(self, act):
        core, nc = self.core, self.core.nc
        ps = core.psum
        act.wait_ge(core.eps_in, 1)
        for b in range(B):
            deviation(core, b)
        for b in range(B):
            for g, turn in enumerate(self.t[b]["xT"]):
                core.result(act, turn)
                nc.scalar.copy(core.xnT[:, b, 1 + 512 * g:1 + 512 * (g + 1)],
                               ps[:, turn.bank, :]).then_inc(core.emptied[turn.bank], 1)
        for b in range(B):
            for turn in self.t[b]["qkv"]:
                core.moved(act, turn)
            nc.scalar.activation(self.sq[:, b, :, :], self.qkv[:, b * TB:(b + 1) * TB, 0:256],
                                 ACT.Square).then_inc(self.squared, 1)
            act.wait_ge(self.sums, b + 1)
            nc.scalar.activation(self.rn[:, b, :, :], self.rn[:, b, :, :], ACT.Sqrt).then_inc(self.norms, 1)
        for b in range(B):
            for g, turn in enumerate(self.t[b]["qkT"]):
                at = b * S + 512 * (g % 2)
                core.result(act, turn)
                nc.scalar.copy(self.qT[:, g // 2, at:at + 512],
                               ps[:, turn.bank, :]).then_inc(core.emptied[turn.bank], 1)
            for i, turn in enumerate(self.t[b]["qfeat"]):
                at = b * S + 512 * (i % 2)
                core.result(act, turn)
                nc.scalar.activation(self.qfeat[:, i // 2, at:at + 512], ps[:, turn.bank, :],
                                     ACT.Relu).then_inc(core.emptied[turn.bank], 1)
            for g, turn in enumerate(self.t[b]["attT"]):
                at = b * S + 512 * g
                core.result(act, turn)
                nc.scalar.copy(self.attT[:, at:at + 512],
                               ps[:, turn.bank, :]).then_inc(core.emptied[turn.bank], 1)

    def vector(self, dve):
        core, w, nc = self.core, self.w, self.core.nc
        ps, v = core.psum, self.core.nc.vector
        dve.wait_ge(w.x_in, 16 * B)
        for b in range(B):
            layer_norm(core, core.x, core.xn, b).then_inc(self.normed, 1)
        dve.wait_ge(w.first_in, w.first_all)
        v.tensor_tensor(w.proj[:, :, :], w.proj_rows[:, :].unsqueeze(1).to_broadcast([P, H, FEAT]),
                        w.head_mask[:, :].unsqueeze(2).to_broadcast([P, H, FEAT]),
                        ALU.mult).then_inc(w.proj_in, 1)
        v.tensor_copy(w.ident16[:, :], w.ident[:, :]).then_inc(w.ident16_in, 1)
        w.e0.split_biases(dve)
        w.e1.split_biases(dve)
        for b in range(B):
            for i, turn in enumerate(self.t[b]["qkv"]):
                core.result(dve, turn)
                v.tensor_tensor(self.qkv[:, b * TB + i, 0:384], ps[:, turn.bank, 0:384], w.la_bqkv[:, :],
                                ALU.add).then_inc(core.emptied[turn.bank], 1)
            dve.wait_ge(self.squared, b + 1)
            rn = self.rn[:, b, :, :]
            v.tensor_reduce(rn, self.sq[:, b, :, :].rearrange("p t (h d) -> p t h d", d=HD), AX.X,
                            ALU.add).then_inc(self.sums, 1)
            dve.wait_ge(self.norms, b + 1)
            core.vstep(v.tensor_scalar(rn, rn, 1e-8, None, ALU.add))
            core.vstep(v.reciprocal(rn, rn))
            qk = self.qkv[:, b * TB:(b + 1) * TB, 0:256].rearrange("p t (h d) -> p t h d", d=HD)
            v.tensor_tensor(qk, qk, rn.unsqueeze(3).to_broadcast([P, TB, 2 * H, HD]),
                            ALU.mult).then_inc(self.unit, 1)
        for b in range(B):
            tb = self.t[b]
            for i, turn in enumerate(tb["kfeat"]):
                core.result(dve, turn)
                v.tensor_scalar(self.kfeat[:, i, :], ps[:, turn.bank, :], 0.0, 0.1, ALU.max,
                                ALU.add).then_inc(core.emptied[turn.bank], 1)
            for r, turn in enumerate(tb["kv"]):
                core.result(dve, turn)
                v.tensor_tensor(self.kv[:, b, 2 * r:2 * r + 2, :],
                                ps[:, turn.bank, 0:288].rearrange("p (c n) -> p c n", c=2),
                                w.kv_mask[:, 2 * r:2 * r + 2, :], ALU.mult).then_inc(core.emptied[turn.bank], 1)
            for r, turn in enumerate(tb["out"]):
                t = b * TB + 2 * r
                core.result(dve, turn)
                view = ps[:, turn.bank, 0:288].rearrange("p (j n) -> p j n", j=2)
                den = self.den[:, r % 2, :, :]
                core.vstep(v.tensor_scalar(den, view[:, :, D:], 1e-6, None, ALU.max))
                core.vstep(v.reciprocal(den, den))
                v.tensor_tensor(self.att[:, t:t + 2, :].rearrange("p j (h d) -> p j h d", d=HD),
                                view[:, :, 0:D].rearrange("p j (h d) -> p j h d", d=HD),
                                den.unsqueeze(3).to_broadcast([P, 2, H, HD]),
                                ALU.mult).then_inc(core.emptied[turn.bank], 1)
            dve.wait_ge(self.bias_in, b + 1)
            for g, turn in enumerate(tb["wo"]):
                t = b * TB + 4 * g
                core.result(dve, turn)
                xs = core.x[:, t:t + 4, :]
                v.tensor_tensor(xs, xs, ps[:, turn.bank, :].rearrange("p (t d) -> p t d", d=D),
                                ALU.add).then_inc(core.emptied[turn.bank], 1)
        for b in range(B):
            for turn in self.t[b]["wo"]:
                core.moved(dve, turn)

    def gpsimd(self, pool):
        core, w, nc = self.core, self.w, self.core.nc
        nc.gpsimd.memset(self.qkv[:, :, 384:400], 1.0).then_inc(self.ones, 1)
        pool.wait_ge(w.first_in, w.first_all)
        for b in range(B):
            pool.wait_ge(self.normed, b + 1)
            xs = core.x[:, b * TB:(b + 1) * TB, :]
            nc.gpsimd.tensor_tensor(xs, xs, w.la_bo[:, :].unsqueeze(1).to_broadcast([P, TB, D]),
                                    ALU.add).then_inc(self.bias_in, 1)
        for b in range(B):
            for i, turn in enumerate(self.t[b]["qfeat"]):
                at = b * S + 512 * (i % 2)
                core.moved(pool, turn)
                q = self.qfeat[:, i // 2, at:at + 512]
                nc.gpsimd.tensor_scalar(q, q, 0.1, None, ALU.add).then_inc(self.qfeat_in, 1)


class ChannelMix:

    def __init__(self, core, w, name):
        self.core, self.w = core, w
        s = core.sem
        self.normed = s(name + "_normed")
        self.xk_in = s(name + "_xk")
        self.xr_in = s(name + "_xr")
        self.act_in = s(name + "_act")
        at = 0
        self.dx, at = carve(core, at, [B, S])
        self.xk, at = carve(core, at, [B, S])
        self.xr, at = carve(core, at, [B, S])
        self.kact, at = carve(core, at, [N])
        self.gate, at = carve(core, at, [T, D])
        self.prod, at = carve(core, at, [T, D])
        self.t = [{"xT": core.turns(2)} for b in range(B)]
        for b in range(B):
            self.t[b].update(k=core.turns(2), r=core.turns(2))
        for b in range(B):
            self.t[b].update(v=core.turns(2))

    def tensor(self, pe):
        core, w, nc = self.core, self.w, self.core.nc
        ps = core.psum
        for b in range(B):
            pe.wait_ge(self.normed, b + 1)
            for g, turn in enumerate(self.t[b]["xT"]):
                t = b * TB + 4 * g
                transpose_tiles(core, pe, turn, [core.xn[:, t + i, :] for i in range(4)], w.ident[:, :])
        pe.wait_ge(w.cm_in, w.cm_all)
        for b in range(B):
            pe.wait_ge(self.xk_in, b + 1)
            for g, turn in enumerate(self.t[b]["k"]):
                core.claim(pe, turn)
                nc.tensor.matmul(ps[:, turn.bank, :], w.cm_wkT[:, :], self.xk[:, b, 512 * g:512 * (g + 1)],
                                 start=True, stop=True).then_inc(core.filled[turn.bank], 1)
            pe.wait_ge(self.xr_in, b + 1)
            for g, turn in enumerate(self.t[b]["r"]):
                core.claim(pe, turn)
                for i in range(4):
                    at = (4 * g + i) * P
                    last = nc.tensor.matmul(ps[:, turn.bank, i * D:(i + 1) * D], self.xr[:, b, at:at + P],
                                            w.cm_wrT[:, :], start=True, stop=True)
                last.then_inc(core.filled[turn.bank], 1)
        for b in range(B):
            for g, turn in enumerate(self.t[b]["v"]):
                core.claim(pe, turn)
                pe.wait_ge(self.act_in, 2 * b + g + 1)
                for i in range(4):
                    at = b * S + (4 * g + i) * P
                    last = nc.tensor.matmul(ps[:, turn.bank, i * D:(i + 1) * D], self.kact[:, at:at + P],
                                            w.cm_wvT[:, :], start=True, stop=True)
                last.then_inc(core.filled[turn.bank], 1)

    def scalar(self, act):
        core, nc = self.core, self.core.nc
        ps = core.psum
        for b in range(B):
            deviation(core, b)
        for b in range(B):
            for g, turn in enumerate(self.t[b]["xT"]):
                core.result(act, turn)
                nc.scalar.copy(core.xnT[:, b, 1 + 512 * g:1 + 512 * (g + 1)],
                               ps[:, turn.bank, :]).then_inc(core.emptied[turn.bank], 1)
        for b in range(B):
            for g, turn in enumerate(self.t[b]["k"]):
                k = self.kact[:, b * S + 512 * g:b * S + 512 * (g + 1)]
                core.result(act, turn)
                nc.scalar.activation(k, ps[:, turn.bank, :], ACT.Relu).then_inc(core.emptied[turn.bank], 1)
                core.moved(act, turn)
                nc.scalar.activation(k, k, ACT.Square).then_inc(self.act_in, 1)
            for g, turn in enumerate(self.t[b]["r"]):
                t = b * TB + 4 * g
                core.result(act, turn)
                nc.scalar.activation(self.gate[:, t:t + 4, :],
                                     ps[:, turn.bank, :].rearrange("p (t d) -> p t d", d=D),
                                     ACT.Sigmoid).then_inc(core.emptied[turn.bank], 1)

    def vector(self, dve):
        core, w, nc = self.core, self.w, self.core.nc
        ps, v = core.psum, self.core.nc.vector
        for b in range(B):
            layer_norm(core, core.x, core.xn, b).then_inc(self.normed, 1)
        dve.wait_ge(w.cm_in, w.cm_all)
        dve.wait_ge(w.zero_column, 1)
        for b in range(B):
            for turn in self.t[b]["xT"]:
                core.moved(dve, turn)
            now, before = core.xnT[:, b, 1:1 + S], core.xnT[:, b, 0:S]
            core.vstep(v.tensor_tensor(self.dx[:, b, :], now, before, ALU.subtract))
            v.scalar_tensor_tensor(out=self.xk[:, b, :], in0=self.dx[:, b, :], scalar=w.cm_mu[:, 0:1], in1=before,
                                   op0=ALU.mult, op1=ALU.add).then_inc(self.xk_in, 1)
            v.scalar_tensor_tensor(out=self.xr[:, b, :], in0=self.dx[:, b, :], scalar=w.cm_mu[:, 1:2], in1=before,
                                   op0=ALU.mult, op1=ALU.add).then_inc(self.xr_in, 1)
        for b in range(B):
            for g, turn in enumerate(self.t[b]["v"]):
                t = b * TB + 4 * g
                core.moved(dve, self.t[b]["r"][g])
                core.result(dve, turn)
                prod, xs = self.prod[:, t:t + 4, :], core.x[:, t:t + 4, :]
                v.tensor_tensor(prod, ps[:, turn.bank, :].rearrange("p (t d) -> p t d", d=D),
                                self.gate[:, t:t + 4, :], ALU.mult).then_inc(core.emptied[turn.bank], 1)
                core.moved(dve, turn)
                core.vmark(v.tensor_tensor(xs, xs, prod, ALU.add))
        core.vsync()


class Weights:

    def __init__(self, core, a):
        self.core, self.a = core, a
        s, sb = core.sem, core.sb
        self.x_in, self.first_in, self.cm_in = s("x_in"), s("first_in"), s("cm_in")
        self.proj_in, self.zero_column = s("proj_in"), s("zero_column")
        self.ident = sb("ident", [P, P])
        self.la_wqkv = sb("la_wqkv", [P, 3, D])
        self.la_bqkv = sb("la_bqkv", [P, 3 * D])
        self.la_wo, self.la_bo = sb("la_wo", [P, D]), sb("la_bo", [P, D])
        self.proj_rows, self.proj = sb("proj_rows", [P, FEAT]), sb("proj", [P, H, FEAT])
        self.head_mask, self.kv_mask = sb("head_mask", [P, H]), sb("kv_mask", [P, NG, D + H])
        self.cm_wkT, self.cm_wrT, self.cm_wvT = (sb(f"cm_w{n}T", [P, D]) for n in "krv")
        self.cm_mu = sb("cm_mu", [P, 2])
        self.before, self.ones = sb("before", [P, P]), sb("ones", [P, P])
        self.expert_ids, self.not_first = sb("expert_ids", [P, NE]), sb("not_first", [P, NE * T])
        self.tile_starts = sb("tile_starts", [1, 40])
        self.ones_rows = sb("ones_rows", [3, P], BF16)
        self.ones_rows_in = s("ones_rows_in")
        self.cleared = s("cleared")
        self.sorted_clear = s("sorted_clear")
        self.zeros = core.arena[:, ARENA - 1280:ARENA]
        self.sorted_x = core.nc.dram_tensor("sorted_x", (39 * P, D), F32).ap()
        self.sorted_y = core.nc.dram_tensor("sorted_y", (39 * P, D), F32).ap()
        self.sorted_clear_all = 16 * 4
        self.sa_in, self.ident16_in = s("sa_in"), s("ident16_in")
        self.ident16 = sb("ident16", [P, P], F16)
        self.sa_wqkv, self.sa_bqkv = sb("sa_wqkv", [P, 3, D]), sb("sa_bqkv", [P, 3 * D])
        self.sa_wo, self.sa_bo, self.sa_b2 = sb("sa_wo", [P, D]), sb("sa_bo", [P, D]), sb("sa_b2", [P, D])
        self.sa_w1, self.sa_b1, self.sa_w2 = sb("sa_w1", [P, FF]), sb("sa_b1", [P, FC]), sb("sa_w2", [P, FC, D])
        self.sa_affine = sb("sa_affine", [P, 4])
        self.rope = sb("rope", [P, 2, TB, HD // 2])
        self.sa_all = 16 * 15
        self.bias_rows = sb("bias_rows", [3, NE * FF + NE * D], BF16)
        self.e0 = ExpertWeights(core, self, "e0")
        self.e1 = ExpertWeights(core, self, "e1")
        self.first_all, self.cm_all = 16 * 9, 16 * 9

    def sync(self, sp, mw):
        core, a = self.core, self.a
        xv = a["L0_attn_a_x"].rearrange("b (t p) d -> b p t d", p=P)
        for b in range(B):
            sp.dma_start(core.x[:, b * TB:(b + 1) * TB, :], xv[b]).then_inc(self.x_in, 16)
        mw.load(sp)
        sp.dma_start(self.ones[:, :], a["c_ones"]).then_inc(mw.loaded, 16)
        sp.dma_start(self.ident[:, :], a["c_ident"]).then_inc(mw.loaded, 16)
        loads = [(self.la_wqkv[:, i, :], a["L0_attn_a_W" + n]) for i, n in enumerate("qkv")]
        loads += [(self.la_bqkv[:, :], a["L0_attn_a_bqkv"].partition_broadcast(P))]
        loads += [(self.proj_rows[:, :], a["L0_attn_a_proj"]), (self.head_mask[:, :], a["c_head_mask"]),
                  (self.kv_mask[:, :, :], a["c_kv_mask"]), (self.la_wo[:, :], a["L0_attn_a_Wo"]),
                  (self.la_bo[:, :], a["L0_attn_a_bo"].partition_broadcast(P))]
        self.first_all = 16 * len(loads)
        for out, src in loads:
            sp.dma_start(out, src).then_inc(self.first_in, 16)
        for out, src in [(self.before[:, :], a["c_before"]),
                         (self.expert_ids[:, :], a["c_expert_ids"].partition_broadcast(P)),
                         (self.not_first[:, :], a["c_not_first"].partition_broadcast(P)),
                         (self.tile_starts[:, :], a["c_tile_starts"].partition_broadcast(1))]:
            sp.dma_start(out, src).then_inc(self.cm_in, 16)
        for n in "krv":
            sp.dma_start({"k": self.cm_wkT, "r": self.cm_wrT, "v": self.cm_wvT}[n][:, :],
                         a[f"L0_ffn_W_{n}T"]).then_inc(self.cm_in, 16)
        for i, n in enumerate("kr"):
            sp.dma_start(self.cm_mu[:, i:i + 1], a["L0_ffn_mu_" + n].rearrange("(p a) -> p a", a=1)).then_inc(self.cm_in, 16)
        sp.wait_ge(self.cleared, 1)
        for j in range(0, 39, 10):
            n = min(10, 39 - j)
            sp.dma_start(self.sorted_x[j * P:(j + n) * P, :].rearrange("(p t) d -> p (t d)", p=P),
                         self.zeros[:, 0:n * D]).then_inc(self.sorted_clear, 16)
        self.e0.load_small(sp)
        self.e1.load_small(sp)
        self.e0.load_big(sp)
        col = "(p a) -> p a"
        loads = [(self.sa_wqkv[:, i, :], a["L1_attn_a_W" + n]) for i, n in enumerate("qkv")]
        loads += [(self.sa_bqkv[:, :], a["L1_attn_a_bqkv"].partition_broadcast(P)),
                  (self.sa_wo[:, :], a["L1_attn_a_Wo"]), (self.sa_bo[:, :], a["L1_attn_a_bo"].partition_broadcast(P)),
                  (self.sa_b2[:, :], a["L1_attn_a_b2"].partition_broadcast(P)), (self.sa_w1[:, :], a["L1_attn_a_W1"]),
                  (self.sa_b1[:, :], a["L1_attn_a_b1_cols"]),
                  (self.sa_w2[:, :, :], a["L1_attn_a_W2"].rearrange("(c p) d -> p c d", p=P)),
                  (self.rope[:, :, :, :], a["c_rope"])]
        loads += [(self.sa_affine[:, i:i + 1], a["L1_attn_a_" + n].rearrange(col, a=1))
                  for i, n in enumerate(("g1", "beta1", "g2", "beta2"))]
        for out, src in loads:
            sp.dma_start(out, src).then_inc(self.sa_in, 16)
        self.e0.bias_to_rows(sp)

    def gpsimd(self, pool):
        g = self.core.nc.gpsimd
        g.memset(self.core.eps[:, :], 1e-5).then_inc(self.core.eps_in, 1)
        g.memset(self.zeros, 0.0).then_inc(self.cleared, 1)
        g.memset(self.ones_rows[:, :], 1.0).then_inc(self.ones_rows_in, 1)
        g.memset(self.core.xnT[:, :, 0:1], 0.0).then_inc(self.zero_column, 1)


class ExpertWeights:

    W2 = NE * FF

    def __init__(self, core, w, name):
        self.core, self.w, self.name = core, w, name
        s, sb = core.sem, core.sb
        self.gate, self.gate_b = sb(name + "_gate", [P, NE]), sb(name + "_gate_b", [P, NE])
        self.bias_wide = sb(name + "_bias_wide", [P, 40])
        self.bias_rest = sb(name + "_bias_rest", [P, 40])
        self.bias_parts = sb(name + "_bias_parts", [P, 3, 40], BF16)
        self.bias_rows = w.bias_rows
        self.small_in = s(name + "_small_in")
        self.big_in = s(name + "_big_in")
        self.parts_in = s(name + "_bias_parts_in")
        self.rows_in = s(name + "_bias_rows_in")
        self.small_all, self.big_all, self.rows_all = 16 * 4, 16 * 2 * NE, 16 * 6

    def load_small(self, sp):
        a, n = self.core_inputs()
        loads = [(self.gate[:, :], a[n["gate"]]), (self.gate_b[:, :], a[n["gate_b"]].partition_broadcast(P)),
                 (self.bias_wide[:, 0:32], a[n["b1"]].rearrange("e (q c) -> (e q) c", c=32)),
                 (self.bias_wide[:, 32:40], a[n["b2"]].rearrange("e (q c) -> (e q) c", c=8))]
        for out, src in loads:
            sp.dma_start(out, src).then_inc(self.small_in, 16)

    def load_big(self, sp):
        a, n = self.core_inputs()
        ew = self.core.expert_w
        for e in range(NE):
            sp.dma_start(ew[:, e * FF:(e + 1) * FF], a[n["w1"]][e]).then_inc(self.big_in, 16)
            sp.dma_start(ew[:, self.W2 + e * FF:self.W2 + (e + 1) * FF].rearrange("p (c d) -> p c d", d=D),
                         a[n["w2"]][e].rearrange("(c p) d -> p c d", p=P)).then_inc(self.big_in, 16)

    def bias_to_rows(self, sp):
        sp.wait_ge(self.parts_in, 3)
        for k in range(3):
            sp.dma_start(self.bias_rows[k:k + 1, 0:NE * FF], self.bias_parts[:, k, 0:32]).then_inc(self.rows_in, 16)
            sp.dma_start(self.bias_rows[k:k + 1, NE * FF:], self.bias_parts[:, k, 32:40]).then_inc(self.rows_in, 16)

    def split_biases(self, dve):
        core, v = self.core, self.core.nc.vector
        dve.wait_ge(self.small_in, self.small_all)
        parts, rest = self.bias_parts, self.bias_rest
        v.tensor_copy(parts[:, 0, :], self.bias_wide[:, :]).then_inc(self.parts_in, 1)
        dve.wait_ge(self.parts_in, 1)
        core.vstep(v.tensor_tensor(rest[:, :], self.bias_wide[:, :], parts[:, 0, :], ALU.subtract))
        v.tensor_copy(parts[:, 1, :], rest[:, :]).then_inc(self.parts_in, 1)
        dve.wait_ge(self.parts_in, 2)
        v.tensor_tensor(parts[:, 2, :], rest[:, :], parts[:, 1, :], ALU.subtract).then_inc(self.parts_in, 1)

    def core_inputs(self):
        if self.name == "e0":
            return self.w.a, {"gate": "L0_attn_b_gate_w", "gate_b": "L0_attn_b_gate_b", "w1": "L0_attn_b_w1",
                              "b1": "L0_attn_b_b1", "w2": "L0_attn_b_w2", "b2": "L0_attn_b_b2"}
        return self.w.a, {"gate": "L1_ffn_Wg", "gate_b": "L1_ffn_bg", "w1": "L1_ffn_W1",
                          "b1": "L1_ffn_b1", "w2": "L1_ffn_W2", "b2": "L1_ffn_b2"}


class Experts:

    def __init__(self, core, w, ew, name, top, func):
        self.core, self.w, self.ew, self.top, self.func = core, w, ew, top, func
        self.tiles = tiles = N * top // P + NE - 1
        assert tiles % 2 == 1
        s, sb = core.sem, core.sb
        self.normed = s(name + "_normed")
        self.shifted = s(name + "_shifted")
        self.exps = s(name + "_exps")
        self.chosen = s(name + "_chosen")
        self.slots_in = s(name + "_slots")
        self.scattered = s(name + "_scattered")
        self.tile_in = [s(f"{name}_tile_in{i}") for i in range(2)]
        self.stored = s(name + "_stored")
        self.gathered = [s(f"{name}_gathered{i}") for i in range(4)]
        at = 0
        c = carve
        self.probs, at = c(core, at, [T, NE])
        self.top_p, at = c(core, at, [2, T])
        self.tmp, at = c(core, at, [T, NE])
        self.hot, at = c(core, at, [2, T, NE])
        self.both, at = c(core, at, [T, NE])
        self.r1, at = c(core, at, [T])
        self.tot, at = c(core, at, [NE, T])
        self.incl, at = c(core, at, [NE, T])
        self.cnt, at = c(core, at, [4, NE])
        self.cnt_i, at = c(core, at, [NE], I32)
        self.pos, at = c(core, at, [T, NE])
        self.slot, at = c(core, at, [2, T], I32)
        self.over, at = c(core, at, [40, NE])
        self.tile_w, at = c(core, at, [40])
        self.tile_off, at = c(core, at, [40], I32)
        self.tile_off2, at = c(core, at, [40], I32)
        self.xg, at = c(core, at, [2, D])
        self.xgT, at = c(core, at, [2, P])
        self.h, at = c(core, at, [2, FF])
        self.hT, at = c(core, at, [2, FC, P])
        self.y, at = c(core, at, [tiles, D])
        self.yg, at = c(core, at, [top, T, D])
        self.store_plan = [(j, 8) for j in range(0, tiles - 7, 8)] + [(tiles - 7, 4), (tiles - 3, 3)]
        assert sum(n for _, n in self.store_plan) == tiles
        self.xT = core.turns(4)
        (self.logits,) = core.turns(1)
        (self.ranks,) = core.turns(1)
        self.base = list(core.uses)
        assert min(self.base) > 0
        for i in range(8):
            core.uses[i] += (tiles + 1 - i % 2) // 2
        self.xs, self.ys = w.sorted_x, w.sorted_y

    def claim(self, eng, k, p, m):
        eng.wait_ge(self.core.emptied[2 * k + p], m + self.base[2 * k + p])

    def result(self, eng, k, p, m):
        eng.wait_ge(self.core.filled[2 * k + p], m + (self.base[2 * k + p] + 1))

    def moved(self, eng, k, p, m):
        eng.wait_ge(self.core.emptied[2 * k + p], m + (self.base[2 * k + p] + 1))

    def used_before(self, eng, k, p, m):
        eng.wait_ge(self.core.filled[2 * k + p], m + self.base[2 * k + p])

    def over_tiles(self, eng, step, lag):
        first = 2 * ((lag + 3) // 2)
        last = first + 2 * ((self.tiles - first) // 2)
        for s in range(first):
            step(s, s % 2, s // 2)
        with eng.Fori(first // 2, last // 2) as m:
            for p in range(2):
                step(None, p, m)
        for s in range(last, self.tiles + lag):
            step(s, s % 2, s // 2)

    def sync(self, sp):
        sp.wait_ge(self.scattered, 16 * self.top * T)

        def load(s, p, m):
            if s is None or s >= 2:
                self.used_before(sp, 0, p, m)
            row = m * (2 * P) + p * P
            src = self.xs[row:row + P, :] if s is not None else self.xs[bass.ds(row, P), :]
            sp.dma_start(self.xg[:, p, :], src).then_inc(self.tile_in[p], 16)

        self.over_tiles(sp, load, 0)
        for j, n in self.store_plan:
            for t in (j + n - 2, j + n - 1):
                if t >= 0:
                    self.moved(sp, 3, t % 2, t // 2)
            sp.dma_start(self.ys[j * P:(j + n) * P, :].rearrange("(t p) d -> p t d", p=P),
                         self.y[:, j:j + n, :]).then_inc(self.stored, 16)

    def gpsimd(self, pool):
        core = self.core
        pool.wait_ge(self.slots_in, 1)
        pool.wait_ge(self.w.sorted_clear, self.w.sorted_clear_all)
        for k in range(self.top):
            for t in range(T):
                pool.indirect_dma_start(out=self.xs[:, :],
                                        out_offset=bass.IndirectOffsetOnAxis(ap=self.slot[:, k, t:t + 1], axis=0),
                                        in_=core.xn[:, t, :], in_offset=None).then_inc(self.scattered, 16)
        pool.wait_ge(self.stored, 16 * len(self.store_plan))
        for t in range(T):
            for k in range(self.top):
                pool.indirect_dma_start(out=self.yg[:, k, t, :], out_offset=None, in_=self.ys[:, :],
                                        in_offset=bass.IndirectOffsetOnAxis(ap=self.slot[:, k, t:t + 1], axis=0)
                                        ).then_inc(self.gathered[t // 4], 16)

    def tensor(self, pe):
        core, w, nc = self.core, self.w, self.core.nc
        ps = core.psum
        for g, turn in enumerate(self.xT):
            pe.wait_ge(self.normed, g // 2 + 1)
            transpose_tiles(core, pe, turn, [core.xn[:, 4 * g + i, :] for i in range(4)], w.ident[:, :])
        pe.wait_ge(self.ew.small_in, self.ew.small_all)
        core.claim(pe, self.logits)
        for t in range(T):
            if t % 4 == 0:
                core.moved(pe, self.xT[t // 4])
            b, i = t // TB, t % TB
            last = nc.tensor.matmul(ps[:, self.logits.bank, t * NE:(t + 1) * NE],
                                    core.xnT[:, b, 1 + i * P:1 + (i + 1) * P], self.ew.gate[:, :],
                                    start=True, stop=True)
        last.then_inc(core.filled[self.logits.bank], 1)
        pe.wait_ge(self.chosen, 1)
        core.claim(pe, self.ranks)
        both = self.both.rearrange("p t e -> p (t e)")
        nc.tensor.matmul(ps[:, self.ranks.bank, 0:P], w.before[:, :], both, start=True, stop=True)
        nc.tensor.matmul(ps[:, self.ranks.bank, P:2 * P], w.ones[:, :], both, start=True,
                         stop=True).then_inc(core.filled[self.ranks.bank], 1)
        pe.wait_ge(self.ew.big_in, self.ew.big_all)
        pe.wait_ge(self.ew.rows_in, self.ew.rows_all)
        pe.wait_ge(self.slots_in, 3)
        pe.wait_ge(w.ones_rows_in, 1)
        ew, brows = core.expert_w, self.ew.bias_rows

        def first_column(tile):
            return pe.value_load(self.tile_off[0:1, tile], min_val=0, max_val=(NE - 1) * FF)

        def step(s, p, m):
            def live(lag):
                return s is None or 0 <= s - lag < self.tiles
            q = 1 - p
            mq = m - q if s is not None or q else m
            if live(0):
                pe.wait_ge(self.tile_in[p], 16 * m + 16)
                self.claim(pe, 0, p, m)
                nc.tensor.transpose(ps[:, p, 0:P], self.xg[:, p, :], w.ident[:, :]).then_inc(core.filled[p], 1)
            if live(1):
                tile = 2 * mq + q
                at = first_column(slice(tile, tile + 1) if s is not None else bass.ds(tile, 1))
                self.moved(pe, 0, q, mq)
                self.claim(pe, 1, q, mq)
                nc.tensor.matmul(ps[:, 2 + q, :], self.xgT[:, q, :], ew[:, bass.ds(at, FF)], start=True, stop=False)
                nc.tensor.matmul(ps[:, 2 + q, :], w.ones_rows[:, :], brows[:, bass.ds(at, FF)], start=False,
                                 stop=True).then_inc(core.filled[2 + q], 1)
            if live(2):
                self.moved(pe, 1, p, m - 1)
                self.claim(pe, 2, p, m - 1)
                for c in range(FC):
                    last = nc.tensor.transpose(ps[:, 4 + p, c * P:(c + 1) * P], self.h[:, p, c * P:(c + 1) * P],
                                               w.ident[:, :])
                last.then_inc(core.filled[4 + p], 1)
            if live(3):
                tile = 2 * (mq - 1) + q
                at = first_column(slice(tile, tile + 1) if s is not None else bass.ds(tile, 1))
                self.moved(pe, 2, q, mq - 1)
                self.claim(pe, 3, q, mq - 1)
                for c in range(FC):
                    nc.tensor.matmul(ps[:, 6 + q, 0:D], self.hT[:, q, c, :],
                                     ew[:, bass.ds(at + (self.ew.W2 + c * D), D)], start=(c == 0), stop=False)
                quarter = pe.value_load(self.tile_off2[0:1, slice(tile, tile + 1) if s is not None else bass.ds(tile, 1)],
                                        min_val=0, max_val=(NE - 1) * D)
                nc.tensor.matmul(ps[:, 6 + q, 0:D], w.ones_rows[:, :], brows[:, bass.ds(quarter + NE * FF, D)],
                                 start=False, stop=True).then_inc(core.filled[6 + q], 1)

        self.over_tiles(pe, step, 3)

    def scalar(self, act):
        core, nc = self.core, self.core.nc
        ps = core.psum
        for b in range(B):
            deviation(core, b)
        for g, turn in enumerate(self.xT):
            core.result(act, turn)
            nc.scalar.copy(core.xnT[:, g // 2, 1 + 512 * (g % 2):1 + 512 * (g % 2 + 1)],
                           ps[:, turn.bank, :]).then_inc(core.emptied[turn.bank], 1)
        act.wait_ge(self.shifted, 1)
        nc.scalar.activation(self.probs, self.probs, ACT.Exp).then_inc(self.exps, 1)

        def step(s, p, m):
            def live(lag):
                return s is None or 0 <= s - lag < self.tiles
            q = 1 - p
            mq = m - q
            if live(0):
                if s is None or s >= 2:
                    self.used_before(act, 1, p, m)
                self.result(act, 0, p, m)
                nc.scalar.copy(self.xgT[:, p, :], ps[:, p, 0:P]).then_inc(core.emptied[p], 1)
            if live(1):
                if s is None or s >= 3:
                    self.used_before(act, 2, q, mq)
                self.result(act, 1, q, mq)
                nc.scalar.activation(self.h[:, q, :], ps[:, 2 + q, :], self.func).then_inc(core.emptied[2 + q], 1)

        self.over_tiles(act, step, 1)

    def vector(self, dve):
        core, w, nc = self.core, self.w, self.core.nc
        ps, v = core.psum, self.core.nc.vector
        for b in range(B):
            layer_norm(core, core.x, core.xn, b).then_inc(self.normed, 1)
        pr, tmp, r1 = self.probs, self.tmp, self.r1

        def per_tile(a):
            return a.unsqueeze(2).to_broadcast([P, T, NE])

        gate_b = self.ew.gate_b[:, :].unsqueeze(1).to_broadcast([P, T, NE])
        ids = w.expert_ids[:, :].unsqueeze(1).to_broadcast([P, T, NE])
        dve.wait_ge(self.ew.small_in, self.ew.small_all)
        core.result(dve, self.logits)
        v.tensor_tensor(pr, ps[:, self.logits.bank, 0:T * NE].rearrange("p (t e) -> p t e", e=NE), gate_b,
                        ALU.add).then_inc(core.emptied[self.logits.bank], 1)
        core.moved(dve, self.logits)
        core.vstep(v.tensor_reduce(r1, pr, AX.X, ALU.max))
        v.tensor_tensor(pr, pr, per_tile(r1), ALU.subtract).then_inc(self.shifted, 1)
        dve.wait_ge(self.exps, 1)
        core.vstep(v.tensor_reduce(r1, pr, AX.X, ALU.add))
        core.vstep(v.reciprocal(r1, r1))
        core.vstep(v.tensor_tensor(pr, pr, per_tile(r1), ALU.mult))
        for k in range(self.top):
            best, hot = self.top_p[:, k, :], self.hot[:, k, :, :]
            core.vstep(v.tensor_reduce(best, pr, AX.X, ALU.max))
            core.vstep(v.tensor_tensor(tmp, pr, per_tile(best), ALU.is_equal))
            core.vstep(v.tensor_tensor(tmp, tmp, ids, ALU.mult))
            core.vstep(v.tensor_reduce(r1, tmp, AX.X, ALU.min))
            core.vstep(v.tensor_tensor(hot, per_tile(r1), ids, ALU.is_equal))
            if k + 1 < self.top:
                core.vstep(v.scalar_tensor_tensor(out=pr, in0=hot, scalar=-2.0, in1=pr, op0=ALU.mult, op1=ALU.add))
        if self.top == 2:
            v.tensor_tensor(self.both, self.hot[:, 0, :, :], self.hot[:, 1, :, :], ALU.add).then_inc(self.chosen, 1)
            core.vstep(v.tensor_tensor(r1, self.top_p[:, 0, :], self.top_p[:, 1, :], ALU.add))
            core.vstep(v.reciprocal(r1, r1))
            core.vstep(v.tensor_tensor(self.top_p, self.top_p, r1.unsqueeze(1).to_broadcast([P, 2, T]), ALU.mult))
        else:
            v.tensor_copy(self.both, self.hot[:, 0, :, :]).then_inc(self.chosen, 1)
        totals = ps[:, self.ranks.bank, P:2 * P].rearrange("p (t e) -> p e t", e=NE)
        ranks = ps[:, self.ranks.bank, 0:P].rearrange("p (t e) -> p t e", e=NE)
        cnt = self.cnt
        core.result(dve, self.ranks)
        core.vstep(v.tensor_copy(self.tot, totals))
        flat = "p e t -> p (e t)"
        core.vstep(v.tensor_tensor_scan(self.incl.rearrange(flat), w.not_first[:, :], self.tot.rearrange(flat), 0.0,
                                        ALU.mult, ALU.add))
        core.vstep(v.tensor_scalar(self.cnt_i, self.incl[:, :, T - 1], float(P - 1), None, ALU.add))
        core.vstep(v.tensor_scalar(self.cnt_i, self.cnt_i, 7, 7, ALU.logical_shift_right, ALU.logical_shift_left))
        core.vstep(v.tensor_copy(cnt[:, 0, :], self.cnt_i))
        core.vstep(v.tensor_tensor_scan(cnt[:, 1, :], w.ones[:, 0:NE], cnt[:, 0, :], 0.0, ALU.mult, ALU.add))
        core.vstep(v.tensor_tensor(cnt[:, 2, :], cnt[:, 1, :], cnt[:, 0, :], ALU.subtract))
        core.vstep(v.tensor_tensor(self.incl, self.incl, self.tot, ALU.subtract))
        core.vstep(v.tensor_tensor(self.incl, self.incl, cnt[:, 2, :].unsqueeze(2).to_broadcast([P, NE, T]), ALU.add))
        v.tensor_tensor(self.pos, ranks, self.incl.rearrange("p e t -> p t e"),
                        ALU.add).then_inc(core.emptied[self.ranks.bank], 1)
        core.moved(dve, self.ranks)
        for k in range(self.top):
            core.vstep(v.tensor_tensor(tmp, self.hot[:, k, :, :], self.pos, ALU.mult))
            core.vstep(v.tensor_reduce(r1, tmp, AX.X, ALU.add))
            if k + 1 < self.top:
                core.vstep(v.tensor_copy(self.slot[:, k, :], r1))
        v.tensor_copy(self.slot[:, self.top - 1, :], r1).then_inc(self.slots_in, 1)
        n = self.tiles
        over, off = self.over[0:1, 0:n, :], self.tile_w[0:1, 0:n]
        core.vstep(v.tensor_tensor(over, w.tile_starts[0:1, 0:n].unsqueeze(2).to_broadcast([1, n, NE]),
                                   cnt[0:1, 1, :].unsqueeze(1).to_broadcast([1, n, NE]), ALU.is_ge))
        core.vstep(v.tensor_reduce(off, over, AX.X, ALU.add))
        v.tensor_scalar(self.tile_off[0:1, 0:n], off, float(NE - 1), float(FF), ALU.min,
                        ALU.mult).then_inc(self.slots_in, 1)
        v.tensor_scalar(self.tile_off2[0:1, 0:n], off, float(NE - 1), float(D), ALU.min,
                        ALU.mult).then_inc(self.slots_in, 1)

        def step(s, p, m):
            def live(lag):
                return s is None or 0 <= s - lag < self.tiles
            q = 1 - p
            mq = m - q
            if live(0):
                if s is None or s >= 2:
                    self.used_before(dve, 3, p, m)
                self.result(dve, 2, p, m)
                v.tensor_copy(self.hT[:, p, :, :], ps[:, 4 + p, :].rearrange("p (c t) -> p c t", t=P)
                              ).then_inc(core.emptied[4 + p], 1)
            if live(1):
                tile = 2 * mq + q
                self.result(dve, 3, q, mq)
                y = self.y[:, tile, :] if s is not None else self.y[:, bass.ds(tile, 1), :]
                v.tensor_copy(y, ps[:, 6 + q, 0:D] if s is not None else ps[:, 6 + q, 0:D].unsqueeze(1)
                              ).then_inc(core.emptied[6 + q], 1)

        self.over_tiles(dve, step, 1)
        for g in range(4):
            ts = slice(4 * g, 4 * g + 4)
            dve.wait_ge(self.gathered[g], 16 * 4 * self.top)
            for k in range(self.top):
                yg = self.yg[:, k, ts, :]
                core.vstep(v.tensor_tensor(yg, yg, self.top_p[:, k, ts].unsqueeze(2).to_broadcast([P, 4, D]), ALU.mult))
                core.vstep(v.tensor_tensor(core.x[:, ts, :], core.x[:, ts, :], yg, ALU.add))


class SoftmaxAttention:

    SHIFT = 256.0

    def __init__(self, core, w):
        self.core, self.w = core, w
        s = core.sem
        self.outer_normed = s("sa_outer_normed")
        self.normed = s("sa_normed")
        self.rotated = s("sa_rotated")
        self.split_in = s("sa_split")
        self.pads = s("sa_pads")
        self.cleared = s("sa_cleared")
        self.masked_q = [s(f"sa_masked_q{i}") for i in range(2)]
        self.masked_k = [s(f"sa_masked_k{i}") for i in range(2)]
        self.ring_in = s("sa_ring_in")
        self.ring_out = s("sa_ring_out")
        self.max_in = s("sa_max_in")
        self.score_in = s("sa_score_in")
        self.prob_in = s("sa_prob_in")
        self.wave_in = s("sa_wave_in")
        self.sum_out = s("sa_sum_out")
        self.value_in = s("sa_value_in")
        self.att_in = s("sa_att")
        self.u2_in = s("sa_u2")
        self.bias_in = s("sa_bias")
        self.x_in = s("sa_x")
        self.ln2 = s("sa_ln2")
        c, at = carve, 0
        self.qT, at = c(core, at, [NG, N], F16)
        self.kT, at = c(core, at, [NG, N], F16)
        self.qM, at = c(core, at, [2, HG, S], F16)
        self.kM, mid = c(core, at, [2, HG, S], F16)
        self.qs, _ = c(core, at, [T, H, 32], F16)
        self.prob, _ = c(core, mid, [2, HG, 512])
        self.ks, at = c(core, mid, [T, H, 32], F16)
        self.v, at = c(core, at, [T, D])
        self.vs, at = c(core, at, [2, TB, HG, 32])
        self.qT2, at = c(core, at, [2, S], F16)
        self.m4, at = c(core, at, [TB, P], F16)
        self.mx, at = c(core, at, [TB, HG])
        self.n1, _ = c(core, 0, [T, D])
        ew = core.expert_w
        self.qk = ew[:, 0:T * 256].rearrange("p (t c) -> p t c", t=T)
        self.rot = ew[:, T * 256:2 * T * 256].rearrange("p (t c) -> p t c", t=T)
        self.rtmp, _ = c(core, at, [2, TB * 2 * H * HD // 2])
        self.oT = ew[:, :].rearrange("p (g n) -> p g n", g=NG)
        at = 0
        self.att, at = c(core, at, [T, D])
        self.attT, at = c(core, at, [N])
        self.n2, at = c(core, at, [T, D])
        self.hid, at = c(core, at, [FC, N])
        self.den, at = c(core, at, [2, H])
        self.t = []
        for b in range(B):
            self.t.append({"xT": core.turns(2), "qkv": core.turns(8)})
        for b in range(B):
            self.t[b]["qkT"] = core.turns(8)
        self.before_units = list(core.uses)
        self.o_turns = core.turns(T)
        for b in range(B):
            self.t[b].update(attT=core.turns(2), wo=core.turns(2))
        for b in range(B):
            self.t[b].update(x2T=core.turns(2), up=core.turns(8), down=core.turns(2))

    RING = 34

    @staticmethod
    def ring_use(a):
        half, k = divmod(a, 17)
        return ("turn", half, 0) if k == 16 else ("max", 4 * half + k // 4, k % 4)

    def ring_fill(self, pe, a, g, b, m, second=False):
        core, nc = self.core, self.core.nc
        slot = a % 2
        kind, qt, j = self.ring_use(a)
        if not second:
            first_of_all = isinstance(m, int) and m == 0 and b == 0 and a < 2
            if not first_of_all:
                pe.wait_ge(self.ring_out, m * (2 * self.RING) + (b * self.RING + a - 1))
        if kind == "turn":
            pe.wait_ge(self.max_in, m * 4 + (2 * b + qt + 1))
            out = core.psum[:, 2 * slot, 0:256].bitcast(F16)
            for i in range(4):
                last = nc.tensor.transpose(out[:, i * P:(i + 1) * P], self.m4[:, 4 * qt + i, :], self.w.ident16[:, :])
            last.then_inc(self.ring_in, 1)
            return
        half = int(second)
        at = g * N + (b * S + 512 * half)
        keys = self.kT.rearrange("p g n -> p (g n)")
        keys = keys[:, at:at + 512] if isinstance(g, int) else keys[:, bass.ds(at, 512)]
        last = nc.tensor.matmul(core.psum[:, 2 * slot + half, :], self.qM[:, b, j, qt * P:(qt + 1) * P], keys,
                                start=True, stop=True)
        if second:
            last.then_inc(self.ring_in, 1)

    def ring_read(self, dve, a, g, b, m):
        core, v = self.core, self.core.nc.vector
        slot = a % 2
        kind, qt, j = self.ring_use(a)
        dve.wait_ge(self.ring_in, m * (2 * self.RING) + (b * self.RING + a + 1))
        if kind == "max":
            v.reduce_max(self.mx[:, qt, j:j + 1], core.psum[:, 2 * slot:2 * slot + 2, :].rearrange("p a n -> p (a n)"),
                         AX.X).then_inc(self.ring_out, 1)
            if a % 17 == 15:
                half = a // 17
                dve.wait_ge(self.ring_out, m * (2 * self.RING) + (b * self.RING + a + 1))
                rows = self.m4[:, 4 * half:4 * half + 4, :].rearrange("p t (j r) -> p t j r", r=32)[:, :, :, 24]
                v.tensor_scalar(rows, self.mx[:, 4 * half:4 * half + 4, :], -1.0 / self.SHIFT, None,
                                ALU.mult).then_inc(self.max_in, 1)
        else:
            at = g * N + (b * S + 512 * qt)
            queries = self.qT.rearrange("p g n -> p (g n)")
            queries = queries[:, at:at + 512] if isinstance(g, int) else queries[:, bass.ds(at, 512)]
            v.tensor_tensor(self.qT2[:, b, 512 * qt:512 * (qt + 1)], queries,
                            core.psum[:, 2 * slot, 0:256].bitcast(F16), ALU.add).then_inc(self.ring_out, 1)

    def move_sum(self, dve, half, g, b, m):
        dve.wait_ge(self.wave_in, m * 32 + (16 * b + 8 * half + 8))
        at = g * N + (b * S + 512 * half)
        out = self.oT.rearrange("p g n -> p (g n)")
        out = out[:, at:at + 512] if isinstance(g, int) else out[:, bass.ds(at, 512)]
        self.core.nc.vector.tensor_copy(out, self.core.psum[:, 6 + half, :]).then_inc(self.sum_out, 1)

    def wave(self, pe, k, g, b, m):
        core, nc = self.core, self.core.nc
        half, kt = divmod(k, 8)
        pe.wait_ge(self.prob_in, m * 128 + (64 * b + 4 * k + 4))
        if kt == 0 and not (isinstance(m, int) and m == 0 and b == 0):
            pe.wait_ge(self.sum_out, m * 4 + (2 * b + half - 1))
        for j in range(HG):
            last = nc.tensor.matmul(core.psum[32 * j:32 * j + 32, 6 + half, :], self.vs[:, b, kt, j, :],
                                    self.prob[:, k % 2, j, :], start=(kt == 0), stop=(kt == TB - 1))
        last.then_inc(self.wave_in, 1)

    def unit_tensor(self, pe, b, m, following=True):
        core, nc = self.core, self.core.nc
        nb, nm = 1 - b, m + b
        plan = list(range(self.RING)) if following else []
        pe.wait_ge(self.masked_k[b], 64 * m + 64)
        pe.wait_ge(self.value_in, m * 2 + (b + 1))
        if following:
            pe.wait_ge(self.masked_q[nb], 64 * nm + 64)
        for k in range(16):
            half, kt = divmod(k, 8)
            if kt == 0:
                pe.wait_ge(self.ring_out, m * (2 * self.RING) + (b * self.RING + 17 * (half + 1)))
            parts = []
            for _ in range(3 if k in (4, 12) else 2):
                if plan:
                    a = plan.pop(0)
                    parts.append((a, False))
                    if self.ring_use(a)[0] == "max":
                        parts.append((a, True))
            for j in range(HG):
                tile = 64 * b + 4 * k + j
                if not (isinstance(m, int) and m == 0 and tile < 2):
                    pe.wait_ge(self.prob_in, m * 128 + (tile - 1))
                nc.tensor.matmul(core.psum[:, 4 + j % 2, :], self.kM[:, b, j, kt * P:(kt + 1) * P],
                                 self.qT2[:, b, 512 * half:512 * (half + 1)], start=True,
                                 stop=True).then_inc(self.score_in, 1)
                take = (len(parts) + HG - 1 - j) // (HG - j)
                for _ in range(take):
                    a, second = parts.pop(0)
                    self.ring_fill(pe, a, nm, nb, nm, second)
            if k > 0:
                self.wave(pe, k - 1, m, b, m)
        self.wave(pe, 15, m, b, m)

    def unit_vector(self, dve, b, m, following=True):
        nb, nm = 1 - b, m + b
        for a in range(self.RING if following else 0):
            self.ring_read(dve, a, nm, nb, nm)
            if a == 3 and not (isinstance(m, int) and m == 0 and b == 0):
                self.move_sum(dve, 1, m - (1 - b), nb, m - (1 - b))
            if a == 20:
                self.move_sum(dve, 0, m, b, m)
        if not following:
            self.move_sum(dve, 1, m - (1 - b), nb, m - (1 - b))
            self.move_sum(dve, 0, m, b, m)
            self.move_sum(dve, 1, m, b, m)

    def unit_scalar(self, act, b, m):
        core, nc = self.core, self.core.nc
        for k in range(16):
            if not (isinstance(m, int) and m == 0 and b == 0 and k < 2):
                act.wait_ge(self.wave_in, m * 32 + (16 * b + k - 1))
            for j in range(HG):
                act.wait_ge(self.score_in, m * 128 + (64 * b + 4 * k + j + 1))
                nc.scalar.activation(self.prob[:, k % 2, j, :], core.psum[:, 4 + j % 2, :],
                                     ACT.Exp).then_inc(self.prob_in, 1)

    def tensor(self, pe):
        core, w, nc = self.core, self.w, self.core.nc
        ps = core.psum
        pe.wait_ge(w.sa_in, w.sa_all)
        for b in range(B):
            pe.wait_ge(self.normed, b + 1)
            for g, turn in enumerate(self.t[b]["xT"]):
                transpose_tiles(core, pe, turn, [self.n1[:, b * TB + 4 * g + i, :] for i in range(4)], w.ident[:, :])
            for i, turn in enumerate(self.t[b]["qkv"]):
                core.claim(pe, turn)
                core.moved(pe, self.t[b]["xT"][i // 4])
                nc.tensor.matmul(ps[:, turn.bank, 0:384], core.xnT[:, b, 1 + i * P:1 + (i + 1) * P],
                                 w.sa_wqkv[:, :], start=True, stop=True).then_inc(core.filled[turn.bank], 1)
        pe.wait_ge(self.pads, 2)
        pe.wait_ge(w.ident16_in, 1)
        for b in range(B):
            pe.wait_ge(self.split_in, 2 * b + 2)
            for i, turn in enumerate(self.t[b]["qkT"]):
                parts, g = (self.qs, self.ks)[i // NG], i % NG
                core.claim(pe, turn)
                out = ps[:, turn.bank, :].bitcast(F16)
                for t in range(TB):
                    last = nc.tensor.transpose(
                        out[:, t * P:(t + 1) * P],
                        parts[:, b * TB + t, HG * g:HG * g + HG, :].rearrange("p j r -> p (j r)"), w.ident16[:, :])
                last.then_inc(core.filled[turn.bank], 1)
        for i in range(8):
            pe.wait_ge(core.emptied[i], self.before_units[i])
        pe.wait_ge(self.masked_q[0], 64)
        for a in range(self.RING):
            self.ring_fill(pe, a, 0, 0, 0)
            if self.ring_use(a)[0] == "max":
                self.ring_fill(pe, a, 0, 0, 0, second=True)
        for b in range(B):
            self.unit_tensor(pe, b, 0)
        with pe.Fori(1, NG - 1) as g:
            for b in range(B):
                self.unit_tensor(pe, b, g)
        self.unit_tensor(pe, 0, NG - 1)
        self.unit_tensor(pe, 1, NG - 1, following=False)
        pe.wait_ge(self.sum_out, 2 * B * NG)
        for t, turn in enumerate(self.o_turns):
            transpose_tiles(core, pe, turn, [self.oT[:, g, t * P:(t + 1) * P] for g in range(NG)], w.ident[:, :])
        for b in range(B):
            tb = self.t[b]
            for g, turn in enumerate(tb["attT"]):
                t = b * TB + 4 * g
                for i in range(4):
                    core.moved(pe, self.o_turns[t + i])
                transpose_tiles(core, pe, turn, [self.att[:, t + i, :] for i in range(4)], w.ident[:, :])
            for g, turn in enumerate(tb["wo"]):
                core.claim(pe, turn)
                core.moved(pe, tb["attT"][g])
                for i in range(4):
                    t = b * TB + 4 * g + i
                    last = nc.tensor.matmul(ps[:, turn.bank, i * D:(i + 1) * D], self.attT[:, t * P:(t + 1) * P],
                                            w.sa_wo[:, :], start=True, stop=True)
                last.then_inc(core.filled[turn.bank], 1)
        for b in range(B):
            tb = self.t[b]
            pe.wait_ge(self.ln2, b + 1)
            for g, turn in enumerate(tb["x2T"]):
                transpose_tiles(core, pe, turn, [self.n2[:, b * TB + 4 * g + i, :] for i in range(4)], w.ident[:, :])
            for i, turn in enumerate(tb["up"]):
                c, half = i % FC, i // FC
                core.claim(pe, turn)
                core.moved(pe, tb["x2T"][half])
                nc.tensor.matmul(ps[:, turn.bank, :], w.sa_w1[:, c * P:(c + 1) * P],
                                 core.xnT[:, b, 1 + 512 * half:1 + 512 * (half + 1)],
                                 start=True, stop=True).then_inc(core.filled[turn.bank], 1)
            for g, turn in enumerate(tb["down"]):
                core.claim(pe, turn)
                for c in range(FC):
                    core.moved(pe, tb["up"][FC * g + c])
                for i in range(4):
                    t = b * TB + 4 * g + i
                    for c in range(FC):
                        last = nc.tensor.matmul(ps[:, turn.bank, i * D:(i + 1) * D], self.hid[:, c, t * P:(t + 1) * P],
                                                w.sa_w2[:, c, :], start=(c == 0), stop=(c == FC - 1))
                last.then_inc(core.filled[turn.bank], 1)

    def scalar(self, act):
        core, w, nc = self.core, self.w, self.core.nc
        ps = core.psum
        for b in range(B):
            deviation(core, b)
            deviation(core, b)
        act.wait_ge(w.sa_in, w.sa_all)
        for b in range(B):
            for g, turn in enumerate(self.t[b]["xT"]):
                core.result(act, turn)
                nc.scalar.activation(core.xnT[:, b, 1 + 512 * g:1 + 512 * (g + 1)], ps[:, turn.bank, :], ACT.Identity,
                                     scale=w.sa_affine[:, 0:1], bias=w.sa_affine[:, 1:2]
                                     ).then_inc(core.emptied[turn.bank], 1)
        for b in range(B):
            for i, turn in enumerate(self.t[b]["qkT"]):
                parts, g = (self.qT, self.kT)[i // NG], i % NG
                core.result(act, turn)
                nc.scalar.copy(parts[:, g, b * S:(b + 1) * S],
                               ps[:, turn.bank, :].bitcast(F16)).then_inc(core.emptied[turn.bank], 1)
        for b in range(B):
            self.unit_scalar(act, b, 0)
        with act.Fori(1, NG) as g:
            for b in range(B):
                self.unit_scalar(act, b, g)
        for b in range(B):
            for g, turn in enumerate(self.t[b]["attT"]):
                at = b * S + 512 * g
                core.result(act, turn)
                nc.scalar.copy(self.attT[:, at:at + 512], ps[:, turn.bank, :]).then_inc(core.emptied[turn.bank], 1)
        for b in range(B):
            deviation(core, b)
        for b in range(B):
            for g, turn in enumerate(self.t[b]["x2T"]):
                core.result(act, turn)
                nc.scalar.activation(core.xnT[:, b, 1 + 512 * g:1 + 512 * (g + 1)], ps[:, turn.bank, :], ACT.Identity,
                                     scale=w.sa_affine[:, 2:3], bias=w.sa_affine[:, 3:4]
                                     ).then_inc(core.emptied[turn.bank], 1)
            for i, turn in enumerate(self.t[b]["up"]):
                c, half = i % FC, i // FC
                at = b * S + 512 * half
                core.result(act, turn)
                nc.scalar.activation(self.hid[:, c, at:at + 512], ps[:, turn.bank, :], ACT.Relu,
                                     bias=w.sa_b1[:, c:c + 1]).then_inc(core.emptied[turn.bank], 1)

    def vector(self, dve):
        core, w, nc = self.core, self.w, self.core.nc
        ps, v = core.psum, self.core.nc.vector
        for b in range(B):
            layer_norm(core, core.x, core.xn, b).then_inc(self.outer_normed, 1)
            dve.wait_ge(self.outer_normed, b + 1)
            layer_norm(core, core.xn, self.n1, b).then_inc(self.normed, 1)
        dve.wait_ge(w.sa_in, w.sa_all)
        for b in range(B):
            tiles = slice(b * TB, (b + 1) * TB)
            for i, turn in enumerate(self.t[b]["qkv"]):
                core.result(dve, turn)
                core.vmark(v.tensor_tensor(self.qk[:, b * TB + i, :], ps[:, turn.bank, 0:256], w.sa_bqkv[:, 0:256],
                                           ALU.add))
                v.tensor_tensor(self.v[:, b * TB + i, :], ps[:, turn.bank, 256:384], w.sa_bqkv[:, 256:384],
                                ALU.add).then_inc(core.emptied[turn.bank], 1)
            core.vsync()
            qk = self.qk[:, tiles, :].rearrange("p t (h j e) -> p t h j e", h=2 * H, e=2)
            rot = self.rot[:, tiles, :].rearrange("p t (h j e) -> p t h j e", h=2 * H, e=2)
            cos, sin = (w.rope[:, i, :, :].unsqueeze(2).to_broadcast([P, TB, 2 * H, HD // 2]) for i in range(2))
            ta, tb_ = (self.rtmp[:, i, :].rearrange("p (t h j) -> p t h j", t=TB, h=2 * H) for i in range(2))
            core.vmark(v.tensor_tensor(ta, qk[:, :, :, :, 0], cos, ALU.mult))
            core.vstep(v.tensor_tensor(tb_, qk[:, :, :, :, 1], sin, ALU.mult))
            core.vstep(v.tensor_tensor(rot[:, :, :, :, 0], ta, tb_, ALU.subtract))
            core.vmark(v.tensor_tensor(ta, qk[:, :, :, :, 0], sin, ALU.mult))
            core.vstep(v.tensor_tensor(tb_, qk[:, :, :, :, 1], cos, ALU.mult))
            core.vstep(v.tensor_tensor(rot[:, :, :, :, 1], ta, tb_, ALU.add))
            if b == 0:
                dve.wait_ge(self.pads, 2)
            q = self.rot[:, tiles, 0:D].rearrange("p t (h d) -> p t h d", d=HD)
            k = self.rot[:, tiles, D:2 * D].rearrange("p t (h d) -> p t h d", d=HD)
            qs, ks = self.qs[:, tiles, :, :], self.ks[:, tiles, :, :]
            scale = float(HD) ** -0.5
            core.vmark(v.tensor_scalar(qs[:, :, :, 0:8], q, scale, None, ALU.mult))
            core.vstep(v.tensor_copy(ks[:, :, :, 0:8], k))
            core.vmark(v.tensor_copy(qs[:, :, :, 8:16], qs[:, :, :, 0:8]))
            core.vmark(v.tensor_copy(ks[:, :, :, 16:24], ks[:, :, :, 0:8]))
            for t in range(b * TB, (b + 1) * TB):
                qt = self.rot[:, t, 0:D].rearrange("p (h d) -> p h d", d=HD)
                core.vmark(v.scalar_tensor_tensor(out=self.qs[:, t, :, 16:24], in0=qt, scalar=scale,
                                                  in1=self.qs[:, t, :, 0:8], op0=ALU.mult, op1=ALU.subtract))
            core.vsync()
            v.tensor_tensor(ks[:, :, :, 8:16], k, ks[:, :, :, 0:8], ALU.subtract).then_inc(self.split_in, 1)
            dve.wait_ge(self.split_in, 2 * b + 1)
            dve.engine_nop().then_inc(self.split_in, 1)
        for a in range(self.RING):
            self.ring_read(dve, a, 0, 0, 0)
        for b in range(B):
            self.unit_vector(dve, b, 0)
        with dve.Fori(1, NG - 1) as g:
            for b in range(B):
                self.unit_vector(dve, b, g)
        self.unit_vector(dve, 0, NG - 1)
        self.unit_vector(dve, 1, NG - 1, following=False)
        for t, turn in enumerate(self.o_turns):
            core.result(dve, turn)
            view = ps[:, turn.bank, :].rearrange("p (h r) -> p h r", r=32)
            den = self.den[:, t % 2, :]
            core.vstep(v.reciprocal(den, view[:, :, 8]))
            v.tensor_tensor(self.att[:, t, :].rearrange("p (h d) -> p h d", d=HD), view[:, :, 0:HD],
                            den.unsqueeze(2).to_broadcast([P, H, HD]), ALU.mult).then_inc(core.emptied[turn.bank], 1)
        u = core.xn
        for b in range(B):
            dve.wait_ge(self.bias_in, b + 1)
            for g, turn in enumerate(self.t[b]["wo"]):
                ts = slice(b * TB + 4 * g, b * TB + 4 * g + 4)
                core.result(dve, turn)
                v.tensor_tensor(u[:, ts, :], u[:, ts, :], ps[:, turn.bank, :].rearrange("p (t d) -> p t d", d=D),
                                ALU.add).then_inc(core.emptied[turn.bank], 1)
            for turn in self.t[b]["wo"]:
                core.moved(dve, turn)
            layer_norm(core, u, self.n2, b).then_inc(self.ln2, 1)
        for b in range(B):
            dve.wait_ge(self.x_in, b + 1)
            for g, turn in enumerate(self.t[b]["down"]):
                xs = core.x[:, b * TB + 4 * g:b * TB + 4 * g + 4, :]
                core.result(dve, turn)
                v.tensor_tensor(xs, xs, ps[:, turn.bank, :].rearrange("p (t d) -> p t d", d=D),
                                ALU.add).then_inc(core.emptied[turn.bank], 1)
        for b in range(B):
            for turn in self.t[b]["down"]:
                core.moved(dve, turn)

    def gpsimd(self, pool):
        core, w, g_ = self.core, self.w, self.core.nc.gpsimd
        pool.wait_ge(self.outer_normed, 1)
        g_.memset(self.qM, 0.0).then_inc(self.cleared, 1)
        g_.memset(self.m4, 0.0).then_inc(self.cleared, 1)
        g_.memset(self.qs[:, :, :, 24:32], 0.0).then_inc(self.pads, 1)
        g_.memset(self.ks[:, :, :, 25:32], 0.0).then_inc(self.cleared, 1)
        g_.memset(self.ks[:, :, :, 24:25], self.SHIFT).then_inc(self.pads, 1)
        g_.memset(self.vs[:, :, :, :, 9:32], 0.0).then_inc(self.cleared, 1)
        g_.memset(self.vs[:, :, :, :, 8:9], 1.0).then_inc(self.cleared, 1)
        for turn in self.t[1]["qkT"]:
            core.moved(pool, turn)
        g_.memset(self.kM, 0.0).then_inc(self.cleared, 1)

        def values(g, b, m):
            if not isinstance(m, int) or m > 0:
                pool.wait_ge(self.wave_in, m * 32 + 16 * (b - 1))
            src = self.v[:, b * TB:(b + 1) * TB, :]
            at = g * (HG * HD)
            src = src[:, :, at:at + HG * HD] if isinstance(g, int) else src[:, :, bass.ds(at, HG * HD)]
            g_.tensor_copy(self.vs[:, b, :, :, 0:HD], src.rearrange("p t (j d) -> p t j d", d=HD)
                           ).then_inc(self.value_in, 1)

        for b in range(B):
            values(0, b, 0)
        with pool.Fori(1, NG) as g:
            for b in range(B):
                values(g, b, g)
        for b in range(B):
            us = core.xn[:, b * TB:(b + 1) * TB, :]
            g_.tensor_tensor(us, us, w.sa_bo[:, :].unsqueeze(1).to_broadcast([P, TB, D]),
                             ALU.add).then_inc(self.bias_in, 1)
        for b in range(B):
            pool.wait_ge(self.ln2, b + 1)
            xs, us = core.x[:, b * TB:(b + 1) * TB, :], core.xn[:, b * TB:(b + 1) * TB, :]
            core.pstep(g_.tensor_tensor(xs, xs, us, ALU.add))
            g_.tensor_tensor(xs, xs, w.sa_b2[:, :].unsqueeze(1).to_broadcast([P, TB, D]),
                             ALU.add).then_inc(self.x_in, 1)

    def sync(self, sp):
        core = self.core

        def masked(src_all, dst, sem, g, b):
            at = g * N + b * S
            src = src_all.rearrange("p g n -> p (g n)")
            for j in range(HG):
                rows = slice(32 * j, 32 * j + 32)
                s = src[rows, at:at + S] if isinstance(g, int) else src[rows, bass.ds(at, S)]
                sp.dma_start(dst[rows, b, j, :], s).then_inc(sem[b], 16)

        def unit(g, b, m):
            if not isinstance(m, int) or m > 0:
                sp.wait_ge(self.ring_in, m * (2 * self.RING) + ((b - 2) * self.RING + 33))
            masked(self.qT, self.qM, self.masked_q, g, b)
            if not isinstance(m, int) or m > 0:
                sp.wait_ge(self.score_in, m * 128 + 64 * (b - 1))
            masked(self.kT, self.kM, self.masked_k, g, b)

        for b in range(B):
            for turn in self.t[b]["qkT"]:
                core.moved(sp, turn)
        sp.wait_ge(self.cleared, 6)
        for b in range(B):
            unit(0, b, 0)
        with sp.Fori(1, NG) as g:
            for b in range(B):
                unit(g, b, g)
        for turn in self.o_turns[-8:]:
            core.result(sp, turn)
        self.w.e1.bias_to_rows(sp)
        self.w.e1.load_big(sp)


class MemoryWeights:

    def __init__(self, core, w):
        self.core, self.w = core, w
        s, sb = core.sem, core.sb
        self.basisT, self.coeffT = sb("basisT", [64, P]), sb("coeffT", [64, 4, P])
        self.soft = sb("mw_soft", [P, 3, P])
        self.wqkv, self.owT = self.soft, sb("mw_owT", [P, P])
        self.small = sb("mw_small", [P, 2, 3])
        self.powers = sb("mw_powers", [P, 3, P])
        self.within, self.rise = self.powers[:, 0, :], self.powers[:, 1, :]
        self.scal = sb("mw_scal", [P, 8])
        self.loaded = s("mw_loaded")
        self.shifted, self.exps = s("mw_shifted"), s("mw_exps")
        self.normal = s("mw_normal")
        self.abs_in, self.ln_in = s("mw_abs"), s("mw_ln")
        self.lnd_in = s("mw_lnd")
        self.powers_in = s("mw_powers_in")
        self.within_in = s("mw_within_in")
        self.logits, self.back = core.turns(2)

    def load(self, sp):
        a = self.w.a
        for out, src in [(self.basisT[:, :], a["L1_attn_b_basisT"]), (self.coeffT[:, :, :], a["L1_attn_b_coeffT"]),
                         (self.powers[:, :, :], a["c_powers"]), (self.scal[:, 5:6], a["c_to_end"]),
                         (self.scal[:, 0:1], a["L1_attn_b_decay"].partition_broadcast(P)),
                         (self.scal[:, 1:2], a["L1_attn_b_out_scale"].partition_broadcast(P))]:
            sp.dma_start(out, src).then_inc(self.loaded, 16)

    def tensor(self, pe):
        core, nc, ps = self.core, self.core.nc, self.core.psum
        pe.wait_ge(self.loaded, 128)
        core.claim(pe, self.logits)
        for i in range(4):
            last = nc.tensor.matmul(ps[:, self.logits.bank, i * P:(i + 1) * P], self.coeffT[:, i, :], self.basisT[:, :],
                                    start=True, stop=True)
        last.then_inc(core.filled[self.logits.bank], 1)
        pe.wait_ge(self.normal, 1)
        transpose_tiles(core, pe, self.back, [self.soft[:, i, :] for i in range(3)], self.w.ident[:, :])

    def scalar(self, act):
        core, nc = self.core, self.core.nc
        c = self.scal
        act.wait_ge(self.abs_in, 1)
        nc.scalar.activation(c[:, 3:4], c[:, 2:3], ACT.Exp, scale=-1.0).then_inc(self.ln_in, 1)
        act.wait_ge(self.ln_in, 1)
        nc.scalar.activation(c[:, 3:4], c[:, 3:4], ACT.Ln, bias=self.w.ones[:, 0:1]).then_inc(self.ln_in, 1)
        act.wait_ge(self.shifted, 1)
        nc.scalar.activation(self.soft[:, :, :], self.soft[:, :, :], ACT.Exp).then_inc(self.exps, 1)
        act.wait_ge(self.lnd_in, 1)
        lnd = c[:, 4:5]
        nc.scalar.activation(self.within, self.powers[:, 0, :], ACT.Exp, scale=lnd).then_inc(self.powers_in, 1)
        nc.scalar.activation(self.rise, self.powers[:, 1, :], ACT.Exp, scale=lnd).then_inc(self.powers_in, 1)
        nc.scalar.activation(c[:, 6:7], c[:, 5:6], ACT.Exp, scale=lnd).then_inc(self.powers_in, 1)
        nc.scalar.activation(c[:, 7:8], lnd, ACT.Exp, scale=float(P)).then_inc(self.powers_in, 1)
        core.result(act, self.back)
        nc.scalar.copy(self.wqkv[:, :, :], core.psum[:, self.back.bank, 0:3 * P].rearrange("p (i c) -> p i c", i=3)
                       ).then_inc(core.emptied[self.back.bank], 1)

    def vector(self, dve):
        core, v = self.core, self.core.nc.vector
        c = self.scal
        dve.wait_ge(self.loaded, 128)
        core.vstep(v.tensor_scalar(c[:, 2:3], c[:, 0:1], -1.0, None, ALU.mult))
        v.tensor_tensor(c[:, 2:3], c[:, 2:3], c[:, 0:1], ALU.max).then_inc(self.abs_in, 1)
        dve.wait_ge(self.ln_in, 2)
        v.scalar_tensor_tensor(out=c[:, 4:5], in0=c[:, 0:1], scalar=0.0, in1=c[:, 3:4], op0=ALU.min,
                               op1=ALU.subtract).then_inc(self.lnd_in, 1)
        core.result(dve, self.logits)
        view = core.psum[:, self.logits.bank, :].rearrange("p (i c) -> p i c", i=4)
        top, total = self.small[:, 0, :], self.small[:, 1, :]
        core.vstep(v.tensor_reduce(top, view[:, 0:3, :], AX.X, ALU.max))
        core.vmark(v.tensor_copy(self.owT[:, :], view[:, 3, :]))
        v.tensor_tensor(self.soft[:, :, :], view[:, 0:3, :], top.unsqueeze(2).to_broadcast([P, 3, P]),
                        ALU.subtract).then_inc(core.emptied[self.logits.bank], 1)
        core.moved(dve, self.logits)
        dve.engine_nop().then_inc(self.shifted, 1)
        dve.wait_ge(self.exps, 1)
        core.vstep(v.tensor_reduce(total, self.soft[:, :, :], AX.X, ALU.add))
        core.vstep(v.reciprocal(total, total))
        v.tensor_tensor(self.soft[:, :, :], self.soft[:, :, :], total.unsqueeze(2).to_broadcast([P, 3, P]),
                        ALU.mult).then_inc(self.normal, 1)
        dve.wait_ge(self.powers_in, 4)
        v.tensor_tensor(self.within, self.within, self.powers[:, 2, :], ALU.mult).then_inc(self.within_in, 1)


class LinearMemory:

    def __init__(self, core, w, mw):
        self.core, self.w, self.mw = core, w, mw
        s = core.sem
        self.normed = s("lm_normed")
        self.qd_in = s("lm_qd")
        self.state_in = s("lm_state")
        c, at = carve, 0
        self.qT, at = c(core, at, [B, S])
        self.kT, at = c(core, at, [B, S])
        self.qd, at = c(core, at, [B, S])
        self.rT, at = c(core, at, [B, S])
        self.kd, at = c(core, at, [T, P])
        self.v, at = c(core, at, [T, P])
        self.att, at = c(core, at, [T, P])
        self.state, at = c(core, at, [B, TB, P])
        self.t = []
        for b in range(B):
            self.t.append({"xT": core.turns(2), "qT": core.turns(2), "kT": core.turns(2), "kv": core.turns(4)})
        for b in range(B):
            self.t[b].update(grow=core.turns(2), att=core.turns(2))
        for b in range(B):
            self.t[b].update(rT=core.turns(2), out=core.turns(2))

    def tensor(self, pe):
        core, nc, ps, mw = self.core, self.core.nc, self.core.psum, self.mw
        core.moved(pe, mw.back)
        for b in range(B):
            tb = self.t[b]
            pe.wait_ge(self.normed, b + 1)
            for g, turn in enumerate(tb["xT"]):
                transpose_tiles(core, pe, turn, [core.xn[:, b * TB + 4 * g + i, :] for i in range(4)], self.w.ident[:, :])
            for i, name in enumerate(("qT", "kT")):
                for g, turn in enumerate(tb[name]):
                    core.claim(pe, turn)
                    core.moved(pe, tb["xT"][g])
                    nc.tensor.matmul(ps[:, turn.bank, :], mw.wqkv[:, i, :],
                                     core.xnT[:, b, 1 + 512 * g:1 + 512 * (g + 1)],
                                     start=True, stop=True).then_inc(core.filled[turn.bank], 1)
            for r, turn in enumerate(tb["kv"]):
                core.claim(pe, turn)
                for j in range(2):
                    i = 2 * r + j
                    last = nc.tensor.matmul(ps[:, turn.bank, j * 256:(j + 1) * 256],
                                            core.xnT[:, b, 1 + i * P:1 + (i + 1) * P], mw.wqkv[:, 1:3, :],
                                            start=True, stop=True)
                last.then_inc(core.filled[turn.bank], 1)
        for b in range(B):
            tb = self.t[b]
            for g, turn in enumerate(tb["grow"]):
                core.claim(pe, turn)
                for i in range(4 - g):
                    core.moved(pe, tb["kv"][(4 * g + i) // 2])
                    t = b * TB + 4 * g + i
                    last = nc.tensor.matmul(ps[:, turn.bank, i * P:(i + 1) * P], self.kd[:, t, :], self.v[:, t, :],
                                            start=True, stop=True)
                last.then_inc(core.filled[turn.bank], 1)
            for g, turn in enumerate(tb["att"]):
                core.claim(pe, turn)
                core.moved(pe, tb["qT"][g])
                core.moved(pe, tb["kT"][g])
                for i in range(4):
                    at = (4 * g + i) * P
                    last = nc.tensor.matmul(ps[:, turn.bank, i * P:(i + 1) * P], self.kT[:, b, at:at + P],
                                            self.qT[:, b, at:at + P], start=True, stop=True)
                last.then_inc(core.filled[turn.bank], 1)
        for b in range(B):
            tb = self.t[b]
            for g, turn in enumerate(tb["rT"]):
                core.claim(pe, turn)
                core.moved(pe, tb["att"][g])
                for i in range(4):
                    n, t = 4 * g + i, b * TB + 4 * g + i
                    out = ps[:, turn.bank, i * P:(i + 1) * P]
                    last = nc.tensor.matmul(out, self.v[:, t, :], self.att[:, t, :], start=True, stop=(n == 0))
                    if n:
                        pe.wait_ge(self.state_in, (TB - 1) * b + n)
                        pe.wait_ge(self.qd_in, 2 * b + g + 1)
                        last = nc.tensor.matmul(out, self.state[:, b, n, :], self.qd[:, b, n * P:(n + 1) * P],
                                                start=False, stop=True)
                last.then_inc(core.filled[turn.bank], 1)
            for g, turn in enumerate(tb["out"]):
                core.claim(pe, turn)
                core.moved(pe, tb["rT"][g])
                for i in range(4):
                    at = (4 * g + i) * P
                    last = nc.tensor.matmul(ps[:, turn.bank, i * P:(i + 1) * P], self.rT[:, b, at:at + P],
                                            mw.owT[:, :], start=True, stop=True)
                last.then_inc(core.filled[turn.bank], 1)

    def scalar(self, act):
        core, nc, ps = self.core, self.core.nc, self.core.psum
        for b in range(B):
            deviation(core, b)
        for b in range(B):
            for name, to in (("xT", None), ("qT", self.qT), ("kT", self.kT)):
                for g, turn in enumerate(self.t[b][name]):
                    out = (core.xnT[:, b, 1 + 512 * g:1 + 512 * (g + 1)] if to is None
                           else to[:, b, 512 * g:512 * (g + 1)])
                    core.result(act, turn)
                    nc.scalar.copy(out, ps[:, turn.bank, :]).then_inc(core.emptied[turn.bank], 1)
        for b in range(B):
            for g, turn in enumerate(self.t[b]["rT"]):
                core.result(act, turn)
                nc.scalar.copy(self.rT[:, b, 512 * g:512 * (g + 1)],
                               ps[:, turn.bank, :]).then_inc(core.emptied[turn.bank], 1)

    def gpsimd(self, pool):
        core, mw = self.core, self.mw
        pool.wait_ge(mw.powers_in, 4)
        rise = mw.rise.unsqueeze(1).to_broadcast([P, 4, P])
        for b in range(B):
            for g, turn in enumerate(self.t[b]["qT"]):
                core.moved(pool, turn)
                view = "p (i t) -> p i t"
                core.nc.gpsimd.tensor_tensor(self.qd[:, b, 512 * g:512 * (g + 1)].rearrange(view, i=4),
                                             self.qT[:, b, 512 * g:512 * (g + 1)].rearrange(view, i=4), rise,
                                             ALU.mult).then_inc(self.qd_in, 1)

    def vector(self, dve):
        core, mw, ps, v = self.core, self.mw, self.core.psum, self.core.nc.vector
        for b in range(B):
            layer_norm(core, core.x, core.xn, b).then_inc(self.normed, 1)
        to_end, whole = mw.scal[:, 6:7], mw.scal[:, 7:8]
        for b in range(B):
            for r, turn in enumerate(self.t[b]["kv"]):
                ts = slice(b * TB + 2 * r, b * TB + 2 * r + 2)
                core.result(dve, turn)
                view = ps[:, turn.bank, :].rearrange("p (j c) -> p j c", j=2)
                core.vmark(v.tensor_scalar(self.kd[:, ts, :], view[:, :, 0:P], to_end, None, ALU.mult))
                v.tensor_copy(self.v[:, ts, :], view[:, :, P:2 * P]).then_inc(core.emptied[turn.bank], 1)
        within = mw.within.unsqueeze(1).to_broadcast([P, 4, P])
        core.vsync()
        for b in range(B):
            for g, turn in enumerate(self.t[b]["grow"]):
                core.result(dve, turn)
                for i in range(4 - g):
                    n = 4 * g + i
                    grow = ps[:, turn.bank, i * P:(i + 1) * P]
                    if n == 0:
                        v.tensor_copy(self.state[:, b, 1, :], grow).then_inc(self.state_in, 1)
                    else:
                        dve.wait_ge(self.state_in, (TB - 1) * b + n)
                        v.scalar_tensor_tensor(out=self.state[:, b, n + 1, :], in0=self.state[:, b, n, :],
                                               scalar=whole, in1=grow, op0=ALU.mult,
                                               op1=ALU.add).then_inc(self.state_in, 1)
                dve.wait_ge(self.state_in, (TB - 1) * b + 4 * g + 4 - g)
                dve.engine_nop().then_inc(core.emptied[turn.bank], 1)
            for g, turn in enumerate(self.t[b]["att"]):
                ts = slice(b * TB + 4 * g, b * TB + 4 * g + 4)
                core.result(dve, turn)
                v.tensor_tensor(self.att[:, ts, :], ps[:, turn.bank, :].rearrange("p (i t) -> p i t", i=4), within,
                                ALU.mult).then_inc(core.emptied[turn.bank], 1)
        for b in range(B):
            for g, turn in enumerate(self.t[b]["out"]):
                xs = core.x[:, b * TB + 4 * g:b * TB + 4 * g + 4, :]
                core.result(dve, turn)
                v.scalar_tensor_tensor(out=xs, in0=ps[:, turn.bank, :].rearrange("p (t d) -> p t d", d=D),
                                       scalar=mw.scal[:, 1:2], in1=xs, op0=ALU.mult,
                                       op1=ALU.add).then_inc(core.emptied[turn.bank], 1)
        for b in range(B):
            for turn in self.t[b]["out"]:
                core.moved(dve, turn)


def program(nc, a, out):
    with ExitStack() as ctx:
        core = Core(nc, ctx)
        w = Weights(core, a)
        mw = MemoryWeights(core, w)
        blocks = [mw, LinearAttention(core, w), ChannelMix(core, w, "cm1"),
                  Experts(core, w, w.e0, "top2", 2, ACT.Gelu_apprx_tanh), ChannelMix(core, w, "cm2"),
                  SoftmaxAttention(core, w), Experts(core, w, w.e1, "top1a", 1, ACT.Silu),
                  LinearMemory(core, w, mw), Experts(core, w, w.e1, "top1b", 1, ACT.Silu)]
        stored = core.sem("stored")
        final = core.sem("final")
        block = ctx.enter_context(nc.Block())

        @block.sync
        def _(sp):
            w.sync(sp, mw)
            for k in blocks:
                if isinstance(k, (Experts, SoftmaxAttention)):
                    k.sync(sp)
            sp.wait_ge(final, 1)
            sp.dma_start(out.rearrange("b (t p) d -> p b t d", p=P),
                         core.x[:, :, :].rearrange("p (b t) d -> p b t d", b=B)).then_inc(stored, 16)
            sp.wait_ge(stored, 16)

        @block.gpsimd
        def _(pool):
            w.gpsimd(pool)
            for k in blocks:
                if isinstance(k, (LinearAttention, Experts, SoftmaxAttention, LinearMemory)):
                    k.gpsimd(pool)

        @block.scalar
        def _(act):
            for k in blocks:
                k.scalar(act)

        @block.tensor
        def _(pe):
            for k in blocks:
                k.tensor(pe)

        @block.vector
        def _(dve):
            for k in blocks:
                k.vector(dve)
            dve.engine_nop().then_inc(final, 1)


def _constants():
    p = np.arange(P)
    freq = (1.0 / np.float32(10000.0) ** (np.arange(0, HD, 2, dtype=np.float32) / HD)).astype(np.float32)
    angle = (np.arange(S, dtype=np.float32)[:, None] * freq[None, :]).astype(np.float32)
    angle = angle.reshape(TB, P, HD // 2).transpose(1, 0, 2)
    head = 4 * np.arange(NG)[None, :] + (p // FEAT)[:, None]
    col_head = np.concatenate([np.arange(D) // HD, np.arange(H)])
    return {
        "c_before": (p[:, None] < p[None, :]).astype(np.float32),
        "c_ones": np.ones((P, P), np.float32),
        "c_expert_ids": np.arange(NE, dtype=np.float32) - NE,
        "c_not_first": (np.arange(NE * T) % T != 0).astype(np.float32),
        "c_tile_starts": np.arange(40, dtype=np.float32) * P,
        "c_rope": np.stack([np.cos(angle), np.sin(angle)], 1).astype(np.float32),
        "c_powers": np.stack([np.maximum(p[None, :] - 1 - p[:, None], 0), np.broadcast_to(p[None, :], (P, P)),
                              p[:, None] < p[None, :]], 1).astype(np.float32),
        "c_to_end": (P - 1 - p[:, None]).astype(np.float32),
        "c_ident": np.eye(P, dtype=np.float32),
        "c_head_mask": (p[:, None] // HD == np.arange(H)[None, :]).astype(np.float32),
        "c_kv_mask": (head[:, :, None] == col_head[None, None, :]).astype(np.float32),
    }


def _layouts(i):
    d = {k: v for k, v in i.items()}
    for n in "rkv":
        d[f"L0_ffn_W_{n}T"] = i[f"L0_ffn_W_{n}"].T
    d["L0_attn_a_bqkv"] = np.concatenate([i["L0_attn_a_b" + n] for n in "qkv"])
    d["L1_attn_a_bqkv"] = np.concatenate([i["L1_attn_a_b" + n] for n in "qkv"])
    d["L1_attn_a_b1_cols"] = i["L1_attn_a_b1"].reshape(FC, P).T
    d["L1_attn_b_basisT"] = i["L1_attn_b_basis"].T
    d["L1_attn_b_coeffT"] = np.stack([i[f"L1_attn_b_{n}_coeffs"].T for n in "qkvo"], 1)
    d["L0_attn_a_proj"] = i["L0_attn_a_projection"].transpose(0, 2, 1).reshape(P, FEAT)
    return d


_UNUSED = {"L0_ffn_W_r", "L0_ffn_W_k", "L0_ffn_W_v", "L0_attn_a_bq", "L0_attn_a_bk", "L0_attn_a_bv",
           "L0_attn_a_projection", "L1_attn_a_bq", "L1_attn_a_bk", "L1_attn_a_bv", "L1_attn_a_b1", "L1_attn_b_basis",
           "L1_attn_b_q_coeffs", "L1_attn_b_k_coeffs", "L1_attn_b_v_coeffs", "L1_attn_b_o_coeffs"}


def kernel(**inputs):
    import concourse.bacc as _bacc
    from concourse.bass_utils import run_bass_kernel_spmd as _run

    nc = _bacc.Bacc("TRN2", target_bir_lowering=False, num_devices=1)
    given = {k: np.asarray(v) for k, v in inputs.items()}
    data = {**_layouts(given), **_constants()}
    arrays, args = {}, {}
    for name in sorted(data):
        if name in _UNUSED:
            continue
        a = np.ascontiguousarray(data[name] if np.ndim(data[name]) else np.reshape(data[name], (1,)))
        arrays[f"in_{name}_dram"] = a
        args[name] = nc.dram_tensor(f"in_{name}_dram", a.shape, mybir.dt.from_np(a.dtype), kind="ExternalInput").ap()
    out = nc.dram_tensor("out_0_dram", (B, S, D), F32, kind="ExternalOutput").ap()
    program(nc, args, out)
    r = _run(nc, [arrays], core_ids=[0])
    return r.results[0]["out_0_dram"]
```

```python
from contextlib import ExitStack

import numpy as np

import concourse.bass as bass
from concourse import mybir

P = 128
F32 = mybir.dt.float32
F16 = mybir.dt.float16
BF16 = mybir.dt.bfloat16
I32 = mybir.dt.int32
ALU = mybir.AluOpType
ACT = mybir.ActivationFunctionType
AX = mybir.AxisListType

B, S, D = 2, 1024, 128
N = B * S
T = N // P
TB = T // B
H, HD = 16, 8
FEAT = 32
NE = 8
FF = 512
FC = FF // P
ROW = D + 2
PAIR = 4096
LANES = 8
ARENA = 28608
HG = 4
NG = H // HG




class Turn:

    def __init__(self, bank, before):
        self.bank, self.before = bank, before


class Core:

    def __init__(self, nc, ctx):
        self.nc, self.ctx = nc, ctx
        self.psum = ctx.enter_context(nc.psum_tensor("psum", [P, 8, 512], F32))
        self.filled = [self.sem(f"bank{i}_filled") for i in range(8)]
        self.emptied = [self.sem(f"bank{i}_emptied") for i in range(8)]
        self.uses = [0] * 8
        self.next_bank = 0
        self.vector_steps = self.sem("vector_steps")
        self.scalar_steps = self.sem("scalar_steps")
        self.pool_steps = self.sem("pool_steps")
        self.variance = self.sem("ln_variance")
        self.root = self.sem("ln_root")
        self.eps = self.sb("eps", [P, 1])
        self.eps_in = self.sem("eps_in")
        self.norms_v = self.norms_s = 0
        self.steps = {"v": 0, "s": 0, "p": 0}
        self.x = self.sb("x", [P, T, D])
        self.xn = self.sb("xn", [P, T, D])
        self.xnT = self.sb("xnT", [P, B, 1 + S])
        self.expert_w = self.sb("expert_w", [P, 2 * NE * FF])
        self.arena = self.sb("arena", [P, ARENA])
        self.stats = self.sb("stats", [P, T, 6])
        self.ln = self.sb("ln_small", [P, 8, T])

    def sem(self, name):
        return self.ctx.enter_context(self.nc.semaphore(name))

    def sb(self, name, shape, dt=F32):
        return self.ctx.enter_context(self.nc.sbuf_tensor(name, shape, dt))

    def turns(self, n):
        out = []
        for _ in range(n):
            b = self.next_bank
            out.append(Turn(b, self.uses[b]))
            self.uses[b] += 1
            self.next_bank = (b + 1) % 8
        return out

    def claim(self, pe, turn):
        if turn.before:
            pe.wait_ge(self.emptied[turn.bank], turn.before)

    def result(self, eng, turn):
        eng.wait_ge(self.filled[turn.bank], turn.before + 1)

    def moved(self, eng, turn):
        eng.wait_ge(self.emptied[turn.bank], turn.before + 1)

    def vstep(self, ins):
        self.steps["v"] += 1
        ins.then_inc(self.vector_steps, 1)
        self.nc.vector.wait_ge(self.vector_steps, self.steps["v"])

    def vmark(self, ins):
        self.steps["v"] += 1
        ins.then_inc(self.vector_steps, 1)

    def vsync(self):
        self.nc.vector.wait_ge(self.vector_steps, self.steps["v"])

    def pstep(self, ins):
        self.steps["p"] += 1
        ins.then_inc(self.pool_steps, 1)
        self.nc.gpsimd.wait_ge(self.pool_steps, self.steps["p"])

    def sstep(self, ins):
        self.steps["s"] += 1
        ins.then_inc(self.scalar_steps, 1)
        self.nc.scalar.wait_ge(self.scalar_steps, self.steps["s"])


def carve(core, at, shape, dt=F32):
    n = int(np.prod(shape))
    words = n * mybir.dt.size(dt) // 4 if False else (n // 2 if dt in (F16, BF16) else n)
    assert at + words <= ARENA, (at, words)
    v = core.arena[:, at:at + words]
    if dt is not F32:
        v = v.bitcast(dt)
    if len(shape) > 1:
        names = [f"d{i}" for i in range(len(shape))]
        v = v.rearrange(f"p ({' '.join(names)}) -> p {' '.join(names)}", **dict(zip(names[1:], shape[1:])))
    return v, at + words


def layer_norm(core, src, out, b):
    nc, ln = core.nc, core.ln
    t0, t1 = b * TB, (b + 1) * TB
    for t in range(t0, t1):
        core.vmark(nc.vector.bn_stats(core.stats[:, t, :], src[:, t, :]))
    core.vsync()
    st = core.stats
    me, mo = st[:, t0:t1, 1], st[:, t0:t1, 4]
    me2, mo2 = st[:, t0:t1, 2], st[:, t0:t1, 5]
    mean, diff, m2, var, rstd = (ln[:, i, t0:t1] for i in range(5))
    core.vmark(nc.vector.tensor_tensor(mean, me, mo, ALU.add))
    core.vmark(nc.vector.tensor_tensor(diff, me, mo, ALU.subtract))
    core.vstep(nc.vector.tensor_tensor(m2, me2, mo2, ALU.add))
    core.vmark(nc.vector.tensor_scalar(mean, mean, 0.5, None, ALU.mult))
    core.vstep(nc.vector.scalar_tensor_tensor(out=var, in0=diff, scalar=0.25, in1=diff, op0=ALU.mult, op1=ALU.mult))
    nc.vector.scalar_tensor_tensor(out=var, in0=m2, scalar=1.0 / D, in1=var, op0=ALU.mult,
                                   op1=ALU.add).then_inc(core.variance, 1)
    core.norms_v += 1
    nc.vector.wait_ge(core.root, core.norms_v)
    core.vstep(nc.vector.reciprocal(rstd, rstd))
    core.vstep(nc.vector.tensor_tensor(out[:, t0:t1, :], src[:, t0:t1, :],
                                       mean.unsqueeze(2).to_broadcast([P, TB, D]), ALU.subtract))
    return nc.vector.tensor_tensor(out[:, t0:t1, :], out[:, t0:t1, :],
                                   rstd.unsqueeze(2).to_broadcast([P, TB, D]), ALU.mult)


def deviation(core, b, eps=1e-5):
    ln, tiles = core.ln, slice(b * TB, (b + 1) * TB)
    core.norms_s += 1
    core.nc.scalar.wait_ge(core.variance, core.norms_s)
    core.nc.scalar.activation(ln[:, 4, tiles], ln[:, 3, tiles], ACT.Sqrt, bias=core.eps[:, 0:1]).then_inc(core.root, 1)


def transpose_tiles(core, pe, turn, pieces, identity):
    core.claim(pe, turn)
    for i, piece in enumerate(pieces):
        last = core.nc.tensor.transpose(core.psum[:, turn.bank, i * P:(i + 1) * P], piece, identity)
    last.then_inc(core.filled[turn.bank], 1)


class LinearAttention:

    def __init__(self, core, w):
        self.core, self.w = core, w
        s = core.sem
        self.normed = s("la_normed")
        self.ones = s("la_ones")
        self.squared = s("la_squared")
        self.sums = s("la_sums")
        self.norms = s("la_norms")
        self.unit = s("la_unit")
        self.qfeat_in = s("la_qfeat")
        self.att_in = s("la_att")
        self.bias_in = s("la_bias")
        at = 0
        self.qkv, at = carve(core, at, [T, 400])
        self.sq, _ = carve(core, at, [B, TB, 256])
        self.att, at = carve(core, at, [T, D])
        self.attT, at = carve(core, at, [N])
        self.qT, at = carve(core, at, [2, N])
        self.kfeat, at = carve(core, at, [TB, H * FEAT])
        self.qfeat, at = carve(core, at, [NG, N])
        self.kv, at = carve(core, at, [B, NG, D + H])
        self.rn, at = carve(core, at, [B, TB, 2 * H])
        self.den, at = carve(core, at, [2, 2, H])
        self.t = []
        for b in range(B):
            self.t.append({"xT": core.turns(2), "qkv": core.turns(8)})
        for b in range(B):
            self.t[b].update(qkT=core.turns(4), kfeat=core.turns(8), qfeat=core.turns(8))
            self.t[b].update(kv=core.turns(2), out=core.turns(4))
            self.t[b].update(attT=core.turns(2), wo=core.turns(2))

    def tensor(self, pe):
        core, w, nc = self.core, self.w, self.core.nc
        ps = core.psum
        for b in range(B):
            pe.wait_ge(self.normed, b + 1)
            if b == 0:
                pe.wait_ge(w.first_in, w.first_all)
            for g, turn in enumerate(self.t[b]["xT"]):
                t = b * TB + 4 * g
                transpose_tiles(core, pe, turn, [core.xn[:, t + i, :] for i in range(4)], w.ident[:, :])
            for i, turn in enumerate(self.t[b]["qkv"]):
                core.claim(pe, turn)
                core.moved(pe, self.t[b]["xT"][i // 4])
                nc.tensor.matmul(ps[:, turn.bank, 0:384], core.xnT[:, b, 1 + i * P:1 + (i + 1) * P],
                                 w.la_wqkv[:, :], start=True, stop=True).then_inc(core.filled[turn.bank], 1)
        for b in range(B):
            tb = self.t[b]
            pe.wait_ge(self.unit, b + 1)
            for g, turn in enumerate(tb["qkT"]):
                t, c = b * TB + 4 * (g % 2), D * (g // 2)
                transpose_tiles(core, pe, turn, [self.qkv[:, t + i, c:c + D] for i in range(4)], w.ident[:, :])
            if b == 0:
                pe.wait_ge(w.proj_in, 1)
            for i, turn in enumerate(tb["kfeat"]):
                core.claim(pe, turn)
                core.moved(pe, tb["qkT"][2 + i // 4])
                nc.tensor.matmul(ps[:, turn.bank, :], self.qT[:, 1, b * S + i * P:b * S + (i + 1) * P],
                                 w.proj[:, :, :], start=True, stop=True).then_inc(core.filled[turn.bank], 1)
            for i, turn in enumerate(tb["qfeat"]):
                c, half = i // 2, i % 2
                core.claim(pe, turn)
                nc.tensor.matmul(ps[:, turn.bank, :], w.proj[:, HG * c:HG * c + HG, :],
                                 self.qT[:, 0, b * S + 512 * half:b * S + 512 * (half + 1)],
                                 start=True, stop=True).then_inc(core.filled[turn.bank], 1)
            if b == 0:
                pe.wait_ge(self.ones, 1)
            for r, turn in enumerate(tb["kv"]):
                core.claim(pe, turn)
                for c in (2 * r, 2 * r + 1):
                    for i in range(TB):
                        if c == 0:
                            core.moved(pe, tb["kfeat"][i])
                        last = nc.tensor.matmul(ps[:, turn.bank, (c % 2) * 144:(c % 2 + 1) * 144],
                                                self.kfeat[:, i, c * P:(c + 1) * P],
                                                self.qkv[:, b * TB + i, 256:400],
                                                start=(i == 0), stop=(i == TB - 1))
                last.then_inc(core.filled[turn.bank], 1)
            core.moved(pe, tb["kv"][0])
            core.moved(pe, tb["kv"][1])
            pe.wait_ge(self.qfeat_in, 8 * b + 8)
            for r, turn in enumerate(tb["out"]):
                core.claim(pe, turn)
                for j in range(2):
                    t = b * TB + 2 * r + j
                    for c in range(NG):
                        last = nc.tensor.matmul(ps[:, turn.bank, j * 144:(j + 1) * 144],
                                                self.qfeat[:, c, t * P:(t + 1) * P], self.kv[:, b, c, :],
                                                start=(c == 0), stop=(c == NG - 1))
                last.then_inc(core.filled[turn.bank], 1)
            for g, turn in enumerate(tb["attT"]):
                t = b * TB + 4 * g
                core.moved(pe, tb["out"][2 * g])
                core.moved(pe, tb["out"][2 * g + 1])
                transpose_tiles(core, pe, turn, [self.att[:, t + i, :] for i in range(4)], w.ident[:, :])
            for g, turn in enumerate(tb["wo"]):
                core.claim(pe, turn)
                core.moved(pe, tb["attT"][g])
                for i in range(4):
                    t = b * TB + 4 * g + i
                    last = nc.tensor.matmul(ps[:, turn.bank, i * D:(i + 1) * D], self.attT[:, t * P:(t + 1) * P],
                                            w.la_wo[:, :], start=True, stop=True)
                last.then_inc(core.filled[turn.bank], 1)

    def scalar(self, act):
        core, nc = self.core, self.core.nc
        ps = core.psum
        act.wait_ge(core.eps_in, 1)
        for b in range(B):
            deviation(core, b)
        for b in range(B):
            for g, turn in enumerate(self.t[b]["xT"]):
                core.result(act, turn)
                nc.scalar.copy(core.xnT[:, b, 1 + 512 * g:1 + 512 * (g + 1)],
                               ps[:, turn.bank, :]).then_inc(core.emptied[turn.bank], 1)
        for b in range(B):
            for turn in self.t[b]["qkv"]:
                core.moved(act, turn)
            nc.scalar.activation(self.sq[:, b, :, :], self.qkv[:, b * TB:(b + 1) * TB, 0:256],
                                 ACT.Square).then_inc(self.squared, 1)
            act.wait_ge(self.sums, b + 1)
            nc.scalar.activation(self.rn[:, b, :, :], self.rn[:, b, :, :], ACT.Sqrt).then_inc(self.norms, 1)
        for b in range(B):
            for g, turn in enumerate(self.t[b]["qkT"]):
                at = b * S + 512 * (g % 2)
                core.result(act, turn)
                nc.scalar.copy(self.qT[:, g // 2, at:at + 512],
                               ps[:, turn.bank, :]).then_inc(core.emptied[turn.bank], 1)
            for i, turn in enumerate(self.t[b]["qfeat"]):
                at = b * S + 512 * (i % 2)
                core.result(act, turn)
                nc.scalar.activation(self.qfeat[:, i // 2, at:at + 512], ps[:, turn.bank, :],
                                     ACT.Relu).then_inc(core.emptied[turn.bank], 1)
            for g, turn in enumerate(self.t[b]["attT"]):
                at = b * S + 512 * g
                core.result(act, turn)
                nc.scalar.copy(self.attT[:, at:at + 512],
                               ps[:, turn.bank, :]).then_inc(core.emptied[turn.bank], 1)

    def vector(self, dve):
        core, w, nc = self.core, self.w, self.core.nc
        ps, v = core.psum, self.core.nc.vector
        dve.wait_ge(w.x_in, 16 * B)
        for b in range(B):
            layer_norm(core, core.x, core.xn, b).then_inc(self.normed, 1)
        dve.wait_ge(w.first_in, w.first_all)
        v.tensor_tensor(w.proj[:, :, :], w.proj_rows[:, :].unsqueeze(1).to_broadcast([P, H, FEAT]),
                        w.head_mask[:, :].unsqueeze(2).to_broadcast([P, H, FEAT]),
                        ALU.mult).then_inc(w.proj_in, 1)
        v.tensor_copy(w.ident16[:, :], w.ident[:, :]).then_inc(w.ident16_in, 1)
        w.e0.split_biases(dve)
        w.e1.split_biases(dve)
        for b in range(B):
            for i, turn in enumerate(self.t[b]["qkv"]):
                core.result(dve, turn)
                v.tensor_tensor(self.qkv[:, b * TB + i, 0:384], ps[:, turn.bank, 0:384], w.la_bqkv[:, :],
                                ALU.add).then_inc(core.emptied[turn.bank], 1)
            dve.wait_ge(self.squared, b + 1)
            rn = self.rn[:, b, :, :]
            v.tensor_reduce(rn, self.sq[:, b, :, :].rearrange("p t (h d) -> p t h d", d=HD), AX.X,
                            ALU.add).then_inc(self.sums, 1)
            dve.wait_ge(self.norms, b + 1)
            core.vstep(v.tensor_scalar(rn, rn, 1e-8, None, ALU.add))
            core.vstep(v.reciprocal(rn, rn))
            qk = self.qkv[:, b * TB:(b + 1) * TB, 0:256].rearrange("p t (h d) -> p t h d", d=HD)
            v.tensor_tensor(qk, qk, rn.unsqueeze(3).to_broadcast([P, TB, 2 * H, HD]),
                            ALU.mult).then_inc(self.unit, 1)
        for b in range(B):
            tb = self.t[b]
            for i, turn in enumerate(tb["kfeat"]):
                core.result(dve, turn)
                v.tensor_scalar(self.kfeat[:, i, :], ps[:, turn.bank, :], 0.0, 0.1, ALU.max,
                                ALU.add).then_inc(core.emptied[turn.bank], 1)
            for r, turn in enumerate(tb["kv"]):
                core.result(dve, turn)
                v.tensor_tensor(self.kv[:, b, 2 * r:2 * r + 2, :],
                                ps[:, turn.bank, 0:288].rearrange("p (c n) -> p c n", c=2),
                                w.kv_mask[:, 2 * r:2 * r + 2, :], ALU.mult).then_inc(core.emptied[turn.bank], 1)
            for r, turn in enumerate(tb["out"]):
                t = b * TB + 2 * r
                core.result(dve, turn)
                view = ps[:, turn.bank, 0:288].rearrange("p (j n) -> p j n", j=2)
                den = self.den[:, r % 2, :, :]
                core.vstep(v.tensor_scalar(den, view[:, :, D:], 1e-6, None, ALU.max))
                core.vstep(v.reciprocal(den, den))
                v.tensor_tensor(self.att[:, t:t + 2, :].rearrange("p j (h d) -> p j h d", d=HD),
                                view[:, :, 0:D].rearrange("p j (h d) -> p j h d", d=HD),
                                den.unsqueeze(3).to_broadcast([P, 2, H, HD]),
                                ALU.mult).then_inc(core.emptied[turn.bank], 1)
            dve.wait_ge(self.bias_in, b + 1)
            for g, turn in enumerate(tb["wo"]):
                t = b * TB + 4 * g
                core.result(dve, turn)
                xs = core.x[:, t:t + 4, :]
                v.tensor_tensor(xs, xs, ps[:, turn.bank, :].rearrange("p (t d) -> p t d", d=D),
                                ALU.add).then_inc(core.emptied[turn.bank], 1)
        for b in range(B):
            for turn in self.t[b]["wo"]:
                core.moved(dve, turn)

    def gpsimd(self, pool):
        core, w, nc = self.core, self.w, self.core.nc
        nc.gpsimd.memset(self.qkv[:, :, 384:400], 1.0).then_inc(self.ones, 1)
        pool.wait_ge(w.first_in, w.first_all)
        for b in range(B):
            pool.wait_ge(self.normed, b + 1)
            xs = core.x[:, b * TB:(b + 1) * TB, :]
            nc.gpsimd.tensor_tensor(xs, xs, w.la_bo[:, :].unsqueeze(1).to_broadcast([P, TB, D]),
                                    ALU.add).then_inc(self.bias_in, 1)
        for b in range(B):
            for i, turn in enumerate(self.t[b]["qfeat"]):
                at = b * S + 512 * (i % 2)
                core.moved(pool, turn)
                q = self.qfeat[:, i // 2, at:at + 512]
                nc.gpsimd.tensor_scalar(q, q, 0.1, None, ALU.add).then_inc(self.qfeat_in, 1)


class ChannelMix:

    def __init__(self, core, w, name):
        self.core, self.w = core, w
        s = core.sem
        self.normed = s(name + "_normed")
        self.xk_in = s(name + "_xk")
        self.xr_in = s(name + "_xr")
        self.act_in = s(name + "_act")
        at = 0
        self.dx, at = carve(core, at, [B, S])
        self.xk, at = carve(core, at, [B, S])
        self.xr, at = carve(core, at, [B, S])
        self.kact, at = carve(core, at, [N])
        self.gate, at = carve(core, at, [T, D])
        self.prod, at = carve(core, at, [T, D])
        self.t = [{"xT": core.turns(2)} for b in range(B)]
        for b in range(B):
            self.t[b].update(k=core.turns(2), r=core.turns(2))
        for b in range(B):
            self.t[b].update(v=core.turns(2))

    def tensor(self, pe):
        core, w, nc = self.core, self.w, self.core.nc
        ps = core.psum
        for b in range(B):
            pe.wait_ge(self.normed, b + 1)
            for g, turn in enumerate(self.t[b]["xT"]):
                t = b * TB + 4 * g
                transpose_tiles(core, pe, turn, [core.xn[:, t + i, :] for i in range(4)], w.ident[:, :])
        pe.wait_ge(w.cm_in, w.cm_all)
        for b in range(B):
            pe.wait_ge(self.xk_in, b + 1)
            for g, turn in enumerate(self.t[b]["k"]):
                core.claim(pe, turn)
                nc.tensor.matmul(ps[:, turn.bank, :], w.cm_wkT[:, :], self.xk[:, b, 512 * g:512 * (g + 1)],
                                 start=True, stop=True).then_inc(core.filled[turn.bank], 1)
            pe.wait_ge(self.xr_in, b + 1)
            for g, turn in enumerate(self.t[b]["r"]):
                core.claim(pe, turn)
                for i in range(4):
                    at = (4 * g + i) * P
                    last = nc.tensor.matmul(ps[:, turn.bank, i * D:(i + 1) * D], self.xr[:, b, at:at + P],
                                            w.cm_wrT[:, :], start=True, stop=True)
                last.then_inc(core.filled[turn.bank], 1)
        for b in range(B):
            for g, turn in enumerate(self.t[b]["v"]):
                core.claim(pe, turn)
                pe.wait_ge(self.act_in, 2 * b + g + 1)
                for i in range(4):
                    at = b * S + (4 * g + i) * P
                    last = nc.tensor.matmul(ps[:, turn.bank, i * D:(i + 1) * D], self.kact[:, at:at + P],
                                            w.cm_wvT[:, :], start=True, stop=True)
                last.then_inc(core.filled[turn.bank], 1)

    def scalar(self, act):
        core, nc = self.core, self.core.nc
        ps = core.psum
        for b in range(B):
            deviation(core, b)
        for b in range(B):
            for g, turn in enumerate(self.t[b]["xT"]):
                core.result(act, turn)
                nc.scalar.copy(core.xnT[:, b, 1 + 512 * g:1 + 512 * (g + 1)],
                               ps[:, turn.bank, :]).then_inc(core.emptied[turn.bank], 1)
        for b in range(B):
            for g, turn in enumerate(self.t[b]["k"]):
                k = self.kact[:, b * S + 512 * g:b * S + 512 * (g + 1)]
                core.result(act, turn)
                nc.scalar.activation(k, ps[:, turn.bank, :], ACT.Relu).then_inc(core.emptied[turn.bank], 1)
                core.moved(act, turn)
                nc.scalar.activation(k, k, ACT.Square).then_inc(self.act_in, 1)
            for g, turn in enumerate(self.t[b]["r"]):
                t = b * TB + 4 * g
                core.result(act, turn)
                nc.scalar.activation(self.gate[:, t:t + 4, :],
                                     ps[:, turn.bank, :].rearrange("p (t d) -> p t d", d=D),
                                     ACT.Sigmoid).then_inc(core.emptied[turn.bank], 1)

    def vector(self, dve):
        core, w, nc = self.core, self.w, self.core.nc
        ps, v = core.psum, self.core.nc.vector
        for b in range(B):
            layer_norm(core, core.x, core.xn, b).then_inc(self.normed, 1)
        dve.wait_ge(w.cm_in, w.cm_all)
        dve.wait_ge(w.zero_column, 1)
        for b in range(B):
            for turn in self.t[b]["xT"]:
                core.moved(dve, turn)
            now, before = core.xnT[:, b, 1:1 + S], core.xnT[:, b, 0:S]
            core.vstep(v.tensor_tensor(self.dx[:, b, :], now, before, ALU.subtract))
            v.scalar_tensor_tensor(out=self.xk[:, b, :], in0=self.dx[:, b, :], scalar=w.cm_mu[:, 0:1], in1=before,
                                   op0=ALU.mult, op1=ALU.add).then_inc(self.xk_in, 1)
            v.scalar_tensor_tensor(out=self.xr[:, b, :], in0=self.dx[:, b, :], scalar=w.cm_mu[:, 1:2], in1=before,
                                   op0=ALU.mult, op1=ALU.add).then_inc(self.xr_in, 1)
        for b in range(B):
            for g, turn in enumerate(self.t[b]["v"]):
                t = b * TB + 4 * g
                core.moved(dve, self.t[b]["r"][g])
                core.result(dve, turn)
                prod, xs = self.prod[:, t:t + 4, :], core.x[:, t:t + 4, :]
                v.tensor_tensor(prod, ps[:, turn.bank, :].rearrange("p (t d) -> p t d", d=D),
                                self.gate[:, t:t + 4, :], ALU.mult).then_inc(core.emptied[turn.bank], 1)
                core.moved(dve, turn)
                core.vmark(v.tensor_tensor(xs, xs, prod, ALU.add))
        core.vsync()


class Weights:

    def __init__(self, core, a):
        self.core, self.a = core, a
        s, sb = core.sem, core.sb
        self.x_in, self.first_in, self.cm_in = s("x_in"), s("first_in"), s("cm_in")
        self.proj_in, self.zero_column = s("proj_in"), s("zero_column")
        self.ident = sb("ident", [P, P])
        self.la_wqkv = sb("la_wqkv", [P, 3, D])
        self.la_bqkv = sb("la_bqkv", [P, 3 * D])
        self.la_wo, self.la_bo = sb("la_wo", [P, D]), sb("la_bo", [P, D])
        self.proj_rows, self.proj = sb("proj_rows", [P, FEAT]), sb("proj", [P, H, FEAT])
        self.head_mask, self.kv_mask = sb("head_mask", [P, H]), sb("kv_mask", [P, NG, D + H])
        self.cm_wkT, self.cm_wrT, self.cm_wvT = (sb(f"cm_w{n}T", [P, D]) for n in "krv")
        self.cm_mu = sb("cm_mu", [P, 2])
        self.before, self.ones = sb("before", [P, P]), sb("ones", [P, P])
        self.expert_ids, self.not_first = sb("expert_ids", [P, NE]), sb("not_first", [P, NE * T])
        self.tile_starts = sb("tile_starts", [1, 40])
        self.ones_rows = sb("ones_rows", [3, P], BF16)
        self.ones_rows_in = s("ones_rows_in")
        self.sorted_clear = s("sorted_clear")
        self.token_rows = sb("token_rows", [P, 2, T], I32)
        self.sorted_rows = {n: core.nc.dram_tensor(n + "_sorted", ((N * top // P + LANES) * P, ROW), I32).ap()
                            for n, top in (("top2", 2), ("top1a", 1), ("top1b", 1))}
        self.results = core.nc.dram_tensor("results", (2 * N + LANES * P, D), F32).ap()
        self.sorted_clear_all = 16 * sum(r.shape[0] // (LANES * P) for r in self.sorted_rows.values())
        self.result_out = [s(f"result_out{i}") for i in range(LANES)]
        self.results_before = [0] * LANES
        self.sa_in, self.ident16_in = s("sa_in"), s("ident16_in")
        self.ident16 = sb("ident16", [P, P], F16)
        self.sa_wqkv, self.sa_bqkv = sb("sa_wqkv", [P, 3, D]), sb("sa_bqkv", [P, 3 * D])
        self.sa_wo, self.sa_bo, self.sa_b2 = sb("sa_wo", [P, D]), sb("sa_bo", [P, D]), sb("sa_b2", [P, D])
        self.sa_w1, self.sa_b1, self.sa_w2 = sb("sa_w1", [P, FF]), sb("sa_b1", [P, FC]), sb("sa_w2", [P, FC, D])
        self.sa_affine = sb("sa_affine", [P, 4])
        self.rope = sb("rope", [P, 2, TB, HD // 2])
        self.sa_all = 16 * 15
        self.bias_rows = sb("bias_rows", [3, NE * FF], BF16)
        self.e0 = ExpertWeights(core, self, "e0")
        self.e1 = ExpertWeights(core, self, "e1")
        self.first_all, self.cm_all = 16 * 10, 16 * 11

    def sync(self, sp, mw):
        core, a = self.core, self.a
        xv = a["L0_attn_a_x"].rearrange("b (t p) d -> b p t d", p=P)
        for b in range(B):
            sp.dma_start(core.x[:, b * TB:(b + 1) * TB, :], xv[b]).then_inc(self.x_in, 16)
        loads = [(self.ident[:, :], a["c_ident"])] + [(self.la_wqkv[:, i, :], a["L0_attn_a_W" + n]) for i, n in enumerate("qkv")]
        loads += [(self.la_bqkv[:, :], a["L0_attn_a_bqkv"].partition_broadcast(P))]
        loads += [(self.proj_rows[:, :], a["L0_attn_a_proj"]), (self.head_mask[:, :], a["c_head_mask"]),
                  (self.kv_mask[:, :, :], a["c_kv_mask"]), (self.la_wo[:, :], a["L0_attn_a_Wo"]),
                  (self.la_bo[:, :], a["L0_attn_a_bo"].partition_broadcast(P))]
        self.first_all = 16 * len(loads)
        for out, src in loads:
            sp.dma_start(out, src).then_inc(self.first_in, 16)
        for out, src in [(self.before[:, :], a["c_before"]), (self.ones[:, :], a["c_ones"]),
                         (self.expert_ids[:, :], a["c_expert_ids"].partition_broadcast(P)),
                         (self.not_first[:, :], a["c_not_first"].partition_broadcast(P)),
                         (self.token_rows[:, :, :], a["c_token_rows"]),
                         (self.tile_starts[:, :], a["c_tile_starts"].partition_broadcast(1))]:
            sp.dma_start(out, src).then_inc(self.cm_in, 16)
        for n in "krv":
            sp.dma_start({"k": self.cm_wkT, "r": self.cm_wrT, "v": self.cm_wvT}[n][:, :],
                         a[f"L0_ffn_W_{n}T"]).then_inc(self.cm_in, 16)
        for i, n in enumerate("kr"):
            sp.dma_start(self.cm_mu[:, i:i + 1], a["L0_ffn_mu_" + n].rearrange("(p a) -> p a", a=1)).then_inc(self.cm_in, 16)
        for rows in self.sorted_rows.values():
            for at in range(0, rows.shape[0], LANES * P):
                sp.dma_start(rows[at:at + LANES * P, :].rearrange("(i p) d -> p i d", p=P), a["c_padding"]
                             ).then_inc(self.sorted_clear, 16)
        mw.load(sp)
        self.e0.load_small(sp)
        self.e1.load_small(sp)
        self.e0.load_w2(sp)
        col = "(p a) -> p a"
        loads = [(self.sa_wqkv[:, i, :], a["L1_attn_a_W" + n]) for i, n in enumerate("qkv")]
        loads += [(self.sa_bqkv[:, :], a["L1_attn_a_bqkv"].partition_broadcast(P)),
                  (self.sa_wo[:, :], a["L1_attn_a_Wo"]), (self.sa_bo[:, :], a["L1_attn_a_bo"].partition_broadcast(P)),
                  (self.sa_b2[:, :], a["L1_attn_a_b2"].partition_broadcast(P)), (self.sa_w1[:, :], a["L1_attn_a_W1"]),
                  (self.sa_b1[:, :], a["L1_attn_a_b1_cols"]),
                  (self.sa_w2[:, :, :], a["L1_attn_a_W2"].rearrange("(c p) d -> p c d", p=P)),
                  (self.rope[:, :, :, :], a["c_rope"])]
        loads += [(self.sa_affine[:, i:i + 1], a["L1_attn_a_" + n].rearrange(col, a=1))
                  for i, n in enumerate(("g1", "beta1", "g2", "beta2"))]
        for out, src in loads:
            sp.dma_start(out, src).then_inc(self.sa_in, 16)
        for e in (self.e0, self.e1):
            e.bias_to_rows(sp)
        for e in (self.e0, self.e1):
            sp.wait_ge(e.rows_in, e.rows_all)
        sp.wait_ge(self.arena_free, 1)
        self.e0.load_w1(sp)

    def gpsimd(self, pool):
        g = self.core.nc.gpsimd
        g.memset(self.core.eps[:, :], 1e-5).then_inc(self.core.eps_in, 1)
        g.memset(self.ones_rows[:, :], 1.0).then_inc(self.ones_rows_in, 1)
        g.memset(self.core.xnT[:, :, 0:1], 0.0).then_inc(self.zero_column, 1)


class ExpertWeights:

    def __init__(self, core, w, name):
        self.core, self.w, self.name = core, w, name
        s, sb = core.sem, core.sb
        self.gate, self.gate_b = sb(name + "_gate", [P, NE]), sb(name + "_gate_b", [P, NE])
        self.b1 = sb(name + "_b1", [P, NE * FC])
        which = 0 if name == "e0" else 1
        room = core.expert_w[0:NE, which * 4 * D:(which + 1) * 4 * D]
        self.bias_wide, self.bias_rest = room[:, 0:D], room[:, D:2 * D]
        self.bias_parts = room[:, 2 * D:4 * D].bitcast(BF16).rearrange("e (k d) -> e k d", d=D)
        self.bias_rows = w.bias_rows[:, which * D:]
        self.bias_dst = w.bias_rows[:, :].rearrange("k (e f) -> k e f", e=NE)[:, :, which * D:(which + 1) * D]
        self.w1_parts = core.expert_w[:, 0:NE * FF].bitcast(F16).rearrange("p (k n) -> p k n", k=2)
        self.w2 = core.expert_w[:, NE * FF:]
        self.w1_wide = core.arena[:, ARENA - NE * FF:]
        self.small_in = s(name + "_small_in")
        self.w1_in, self.w2_in = s(name + "_w1_in"), s(name + "_w2_in")
        self.w1_rounded = s(name + "_w1_rounded")
        self.w1_split = s(name + "_w1_split")
        self.parts_in = s(name + "_bias_parts_in")
        self.rows_in = s(name + "_bias_rows_in")
        self.small_all, self.rows_all = 16 * 4, 16 * 3
        prefix, (gate, gate_b, w1, b1, w2, b2) = (
            ("L0_attn_b_", ("gate_w", "gate_b", "w1", "b1_cols", "w2", "b2")) if name == "e0" else
            ("L1_ffn_", ("Wg", "bg", "W1", "b1_cols", "W2", "b2")))
        a = w.a
        self.from_dram = {"gate": a[prefix + gate], "gate_b": a[prefix + gate_b], "w1": a[prefix + w1],
                          "b1": a[prefix + b1], "w2": a[prefix + w2], "b2": a[prefix + b2]}

    def load_small(self, sp):
        d = self.from_dram
        loads = [(self.gate[:, :], d["gate"]), (self.gate_b[:, :], d["gate_b"].partition_broadcast(P)),
                 (self.b1[:, :], d["b1"]), (self.bias_wide[:, :], d["b2"])]
        for out, src in loads:
            sp.dma_start(out, src).then_inc(self.small_in, 16)

    def load_w1(self, sp):
        sp.dma_start(self.w1_wide.rearrange("p (e f) -> p e f", e=NE),
                     self.from_dram["w1"].rearrange("e p f -> p e f")).then_inc(self.w1_in, 16)

    def load_w2(self, sp):
        sp.dma_start(self.w2.rearrange("p (e c d) -> p e c d", e=NE, c=FC),
                     self.from_dram["w2"].rearrange("e (c p) d -> p e c d", p=P)).then_inc(self.w2_in, 16)

    def round_w1(self, act):
        act.wait_ge(self.w1_in, 16)
        for k in range(2):
            half = slice(k * NE * FF // 2, (k + 1) * NE * FF // 2)
            self.core.nc.scalar.copy(self.w1_parts[:, 0, half], self.w1_wide[:, half]).then_inc(self.w1_rounded, 1)

    def split_w1(self, dve):
        for k in range(2):
            half = slice(k * NE * FF // 2, (k + 1) * NE * FF // 2)
            dve.wait_ge(self.w1_rounded, k + 1)
            self.core.nc.vector.tensor_tensor(self.w1_parts[:, 1, half], self.w1_wide[:, half],
                                              self.w1_parts[:, 0, half], ALU.subtract).then_inc(self.w1_split, 1)

    def bias_to_rows(self, sp):
        sp.wait_ge(self.parts_in, 3)
        for k in range(3):
            sp.dma_start(self.bias_dst[k:k + 1, :, :], self.bias_parts[:, k, :]).then_inc(self.rows_in, 16)

    def split_biases(self, dve):
        core, v = self.core, self.core.nc.vector
        dve.wait_ge(self.small_in, self.small_all)
        parts, rest = self.bias_parts, self.bias_rest
        v.tensor_copy(parts[:, 0, :], self.bias_wide[:, :]).then_inc(self.parts_in, 1)
        dve.wait_ge(self.parts_in, 1)
        core.vstep(v.tensor_tensor(rest[:, :], self.bias_wide[:, :], parts[:, 0, :], ALU.subtract))
        v.tensor_copy(parts[:, 1, :], rest[:, :]).then_inc(self.parts_in, 1)
        dve.wait_ge(self.parts_in, 2)
        v.tensor_tensor(parts[:, 2, :], rest[:, :], parts[:, 1, :], ALU.subtract).then_inc(self.parts_in, 1)


class Experts:

    def __init__(self, core, w, ew, name, top, func, fresh=True, meanwhile=None):
        self.meanwhile = meanwhile
        self.core, self.w, self.ew, self.top, self.func, self.fresh = core, w, ew, top, func, fresh
        self.tiles = tiles = N * top // P + NE - 1
        assert tiles % 2 == 1
        s, sb = core.sem, core.sb
        self.normed = s(name + "_normed")
        self.shifted = s(name + "_shifted")
        self.exps = s(name + "_exps")
        self.chosen = s(name + "_chosen")
        self.slots_in = s(name + "_slots")
        self.rounded = s(name + "_rounded")
        self.rows_in = s(name + "_rows_in")
        self.scattered = s(name + "_scattered")
        self.tile_in = [s(f"{name}_tile_in{i}") for i in range(2)]
        self.back = [s(f"{name}_back{i}") for i in range(4)]
        at = 0
        c = carve
        self.probs, at = c(core, at, [T, NE])
        self.top_p, at = c(core, at, [2, T])
        self.tmp, at = c(core, at, [T, NE])
        self.hot, at = c(core, at, [2, T, NE])
        self.both, at = c(core, at, [T, NE])
        self.r1, at = c(core, at, [T])
        self.tot, at = c(core, at, [NE, T])
        self.incl, at = c(core, at, [NE, T])
        self.cnt, at = c(core, at, [4, NE])
        self.cnt_i, at = c(core, at, [NE], I32)
        self.pos, at = c(core, at, [T, NE])
        self.slot, at = c(core, at, [2, T], I32)
        self.over, at = c(core, at, [40, NE])
        self.tile_w, at = c(core, at, [40])
        self.tile_at, at = c(core, at, [2, 44], I32)
        self.pair, at = c(core, at, [44])
        self.y, at = c(core, at, [tiles, D])
        self.xgT, at = c(core, at, [2, 2, P], F16)
        self.hT, at = c(core, at, [2, FC, P])
        self.rows, _ = c(core, at, [top, T, ROW])
        self.rows_int, _ = c(core, at, [top, T, ROW], I32)
        self.rows16, at = c(core, at, [top, T, 2 * ROW], F16)
        self.sorted, _ = c(core, at, [tiles, ROW])
        self.sorted_int, _ = c(core, at, [tiles, ROW], I32)
        self.sorted16, at = c(core, at, [tiles, 2 * ROW], F16)
        self.yg, at = c(core, at, [top, T, D])
        assert at <= ARENA - NE * FF
        self.xT = core.turns(4)
        (self.logits,) = core.turns(1)
        (self.ranks,) = core.turns(1)
        if meanwhile:
            meanwhile.take_banks()
        self.base = list(core.uses)
        assert min(self.base) > 0
        for i in range(6):
            core.uses[i] += (tiles + 1 - i % 2) // 2
        self.xs, self.results = w.sorted_rows[name], w.results
        self.results_before = list(w.results_before)
        for i in range(tiles):
            w.results_before[i % LANES] += 1

    def claim(self, eng, k, p, m):
        eng.wait_ge(self.core.emptied[2 * k + p], m + self.base[2 * k + p])

    def result(self, eng, k, p, m):
        eng.wait_ge(self.core.filled[2 * k + p], m + (self.base[2 * k + p] + 1))

    def moved(self, eng, k, p, m):
        eng.wait_ge(self.core.emptied[2 * k + p], m + (self.base[2 * k + p] + 1))

    def used_before(self, eng, k, p, m):
        eng.wait_ge(self.core.filled[2 * k + p], m + self.base[2 * k + p])

    def over_tiles(self, eng, step, lag):
        first = 2 * ((lag + 3) // 2)
        last = first + 2 * ((self.tiles - first) // 2)
        for s in range(first):
            step(s, s % 2, s // 2)
        with eng.Fori(first // 2, last // 2) as m:
            for p in range(2):
                step(None, p, m)
        for s in range(last, self.tiles + lag):
            step(s, s % 2, s // 2)

    def sync(self, sp):
        if self.fresh and self.ew is self.w.e1:
            sp.wait_ge(self.normed, 1)
            self.ew.load_w1(sp)
        sp.wait_ge(self.scattered, 16 * self.top * T)

        def load(s, p, m):
            if s is None or s >= 2:
                sp.wait_ge(self.tile_in[p], 16 * m)
            if s is not None:
                sp.dma_start(self.sorted_int[:, s, :], self.xs[s * P:(s + 1) * P, :]).then_inc(self.tile_in[p], 16)
            else:
                sp.dma_start(self.sorted_int[:, bass.ds(2 * m + p, 1), :],
                             self.xs[bass.ds(m * (2 * P) + p * P, P), :].unsqueeze(1)).then_inc(self.tile_in[p], 16)

        self.over_tiles(sp, load, 0)
        for s in range(self.tiles - LANES, self.tiles):
            sp.wait_ge(self.w.result_out[s % LANES], self.result_count(s))
        rows = self.results[0:self.top * N, :].rearrange("(k t p) d -> p k t d", p=P, t=T)
        for g in range(4):
            for k in range(self.top):
                sp.dma_start(self.yg[:, k, 4 * g:4 * g + 4, :], rows[:, k, 4 * g:4 * g + 4, :]
                             ).then_inc(self.back[g], 16)

    def gpsimd(self, pool):
        core, w, g_ = self.core, self.w, self.core.nc.gpsimd
        pool.wait_ge(self.normed, 1)
        for k in range(self.top):
            last = g_.tensor_copy(self.rows_int[:, k, :, D], w.token_rows[:, k, :])
        last.then_inc(self.rows_in, 1)
        for b in range(B):
            ts = slice(b * TB, (b + 1) * TB)
            pool.wait_ge(self.rounded, b + 1)
            core.pstep(g_.tensor_tensor(self.rows16[:, 0, ts, D:2 * D], core.xn[:, ts, :],
                                        self.rows16[:, 0, ts, 0:D], ALU.subtract))
            for k in range(1, self.top):
                g_.tensor_copy(self.rows[:, k, ts, 0:D], self.rows[:, 0, ts, 0:D]).then_inc(self.rows_in, 1)
        pool.wait_ge(self.rows_in, 1 + B * (self.top - 1))
        pool.wait_ge(self.slots_in, 1)
        pool.wait_ge(w.sorted_clear, w.sorted_clear_all)
        for k in range(self.top):
            for t in range(T):
                pool.indirect_dma_start(out=self.xs[:, :],
                                        out_offset=bass.IndirectOffsetOnAxis(ap=self.slot[:, k, t:t + 1], axis=0),
                                        in_=self.rows_int[:, k, t, :], in_offset=None).then_inc(self.scattered, 16)

        for s in range(self.tiles):
            i = s % LANES
            self.moved(pool, 2, s % 2, s // 2)
            if s >= LANES:
                pool.wait_ge(w.result_out[i], self.result_count(s - LANES))
            pool.indirect_dma_start(out=self.results[:, :],
                                    out_offset=bass.IndirectOffsetOnAxis(ap=self.sorted_int[:, s, D:D + 1], axis=0),
                                    in_=self.y[:, s, :], in_offset=None).then_inc(w.result_out[i], 16)

    def result_count(self, s):
        return 16 * (self.results_before[s % LANES] + s // LANES + 1)

    def tensor(self, pe):
        core, w, nc = self.core, self.w, self.core.nc
        ps = core.psum
        for g, turn in enumerate(self.xT):
            pe.wait_ge(self.normed, g // 2 + 1)
            transpose_tiles(core, pe, turn, [core.xn[:, 4 * g + i, :] for i in range(4)], w.ident[:, :])
        pe.wait_ge(self.ew.small_in, self.ew.small_all)
        core.claim(pe, self.logits)
        for t in range(T):
            if t % 4 == 0:
                core.moved(pe, self.xT[t // 4])
            b, i = t // TB, t % TB
            last = nc.tensor.matmul(ps[:, self.logits.bank, t * NE:(t + 1) * NE],
                                    core.xnT[:, b, 1 + i * P:1 + (i + 1) * P], self.ew.gate[:, :],
                                    start=True, stop=True)
        last.then_inc(core.filled[self.logits.bank], 1)
        pe.wait_ge(self.chosen, 1)
        core.claim(pe, self.ranks)
        both = self.both.rearrange("p t e -> p (t e)")
        nc.tensor.matmul(ps[:, self.ranks.bank, 0:P], w.before[:, :], both, start=True, stop=True)
        nc.tensor.matmul(ps[:, self.ranks.bank, P:2 * P], w.ones[:, :], both, start=True,
                         stop=True).then_inc(core.filled[self.ranks.bank], 1)
        if self.meanwhile:
            self.meanwhile.tensor(pe)
        pe.wait_ge(self.ew.w1_split, 2)
        pe.wait_ge(self.ew.w2_in, 16)
        pe.wait_ge(self.ew.rows_in, self.ew.rows_all)
        pe.wait_ge(self.slots_in, 3)
        pe.wait_ge(w.ones_rows_in, 1)
        pe.wait_ge(w.ident16_in, 1)
        w1, w2, brows = self.ew.w1_parts, self.ew.w2, self.ew.bias_rows

        def step(s, p, m):
            def live(lag):
                return s is None or 0 <= s - lag < self.tiles
            q = 1 - p
            mq = m - q if s is not None or q else m
            if live(1) or live(3):
                both = self.tile_value(pe, 0, s, 2 * m + p, (PAIR + 1) * (NE - 1) * FF)
                first = (both & (PAIR - 1)).with_bounds(max_val=(NE - 1) * FF)
                second = (both >> (PAIR.bit_length() - 1)).with_bounds(max_val=(NE - 1) * FF)
            if live(0):
                pe.wait_ge(self.tile_in[p], 16 * m + 16)
                if s is not None and s < 2:
                    self.claim(pe, 0, p, m)
                for k in range(2):
                    part = (self.sorted16[:, s, k * D:(k + 1) * D] if s is not None else
                            self.sorted16[:, bass.ds(2 * m + p, 1), k * D:(k + 1) * D])
                    last = nc.tensor.transpose(ps[:, p, k * 64:(k + 1) * 64].bitcast(F16), part, w.ident16[:, :])
                last.then_inc(core.filled[p], 1)
            if live(1):
                self.moved(pe, 0, q, mq)
                self.claim(pe, 1, q, mq)
                for c in range(FC):
                    for i, (of_w, of_x) in enumerate(((0, 0), (0, 1), (1, 0))):
                        last = nc.tensor.matmul(ps[:, 2 + q, c * P:(c + 1) * P],
                                                w1[:, of_w, c * P:][:, bass.ds(first, P)], self.xgT[:, q, of_x, :],
                                                start=(i == 0), stop=(i == 2))
                last.then_inc(core.filled[2 + q], 1)
            if live(3):
                if not live(1):
                    self.moved(pe, 1, q, mq - 1)
                self.claim(pe, 2, q, mq - 1)
                for c in range(FC):
                    nc.tensor.matmul(ps[:, 4 + q, 0:D], self.hT[:, q, c, :], w2[:, c * D:][:, bass.ds(second, D)],
                                     start=(c == 0), stop=False)
                nc.tensor.matmul(ps[:, 4 + q, 0:D], w.ones_rows[:, :], brows[:, bass.ds(second, D)],
                                 start=False, stop=True).then_inc(core.filled[4 + q], 1)

        self.over_tiles(pe, step, 3)

    def tile_value(self, eng, which, s, tile, largest):
        return eng.value_load(self.tile_at[0:1, which, slice(tile, tile + 1) if s is not None else bass.ds(tile, 1)],
                              min_val=0, max_val=largest)

    def scalar(self, act):
        core, nc = self.core, self.core.nc
        ps = core.psum
        for b in range(B):
            deviation(core, b)
        for g, turn in enumerate(self.xT):
            core.result(act, turn)
            nc.scalar.copy(core.xnT[:, g // 2, 1 + 512 * (g % 2):1 + 512 * (g % 2 + 1)],
                           ps[:, turn.bank, :]).then_inc(core.emptied[turn.bank], 1)
        for b in range(B):
            ts = slice(b * TB, (b + 1) * TB)
            act.wait_ge(self.normed, b + 1)
            nc.scalar.copy(self.rows16[:, 0, ts, 0:D], core.xn[:, ts, :]).then_inc(self.rounded, 1)
        act.wait_ge(self.shifted, 1)
        nc.scalar.activation(self.probs, self.probs, ACT.Exp).then_inc(self.exps, 1)
        if self.fresh:
            self.ew.round_w1(act)
        if self.meanwhile:
            self.meanwhile.scalar(act)
        act.wait_ge(self.slots_in, 3)

        def step(s, p, m):
            at = self.tile_value(act, 1, s, 2 * m + p, (NE - 1) * FC)
            if s is None or s >= 2:
                self.used_before(act, 2, p, m)
            self.result(act, 1, p, m)
            for c in range(FC):
                last = nc.scalar.activation(self.hT[:, p, c, :], ps[:, 2 + p, c * P:(c + 1) * P], self.func,
                                            bias=self.ew.b1[:, c:][:, bass.ds(at, 1)])
            last.then_inc(core.emptied[2 + p], 1)

        self.over_tiles(act, step, 0)

    def vector(self, dve):
        core, w, nc = self.core, self.w, self.core.nc
        ps, v = core.psum, self.core.nc.vector
        for b in range(B):
            layer_norm(core, core.x, core.xn, b).then_inc(self.normed, 1)
        pr, tmp, r1 = self.probs, self.tmp, self.r1

        def per_tile(a):
            return a.unsqueeze(2).to_broadcast([P, T, NE])

        gate_b = self.ew.gate_b[:, :].unsqueeze(1).to_broadcast([P, T, NE])
        ids = w.expert_ids[:, :].unsqueeze(1).to_broadcast([P, T, NE])
        dve.wait_ge(self.ew.small_in, self.ew.small_all)
        core.result(dve, self.logits)
        v.tensor_tensor(pr, ps[:, self.logits.bank, 0:T * NE].rearrange("p (t e) -> p t e", e=NE), gate_b,
                        ALU.add).then_inc(core.emptied[self.logits.bank], 1)
        core.moved(dve, self.logits)
        core.vstep(v.tensor_reduce(r1, pr, AX.X, ALU.max))
        v.tensor_tensor(pr, pr, per_tile(r1), ALU.subtract).then_inc(self.shifted, 1)
        dve.wait_ge(self.exps, 1)
        core.vstep(v.tensor_reduce(r1, pr, AX.X, ALU.add))
        core.vstep(v.reciprocal(r1, r1))
        core.vstep(v.tensor_tensor(pr, pr, per_tile(r1), ALU.mult))
        for k in range(self.top):
            best, hot = self.top_p[:, k, :], self.hot[:, k, :, :]
            core.vstep(v.tensor_reduce(best, pr, AX.X, ALU.max))
            core.vstep(v.tensor_tensor(tmp, pr, per_tile(best), ALU.is_equal))
            core.vstep(v.tensor_tensor(tmp, tmp, ids, ALU.mult))
            core.vstep(v.tensor_reduce(r1, tmp, AX.X, ALU.min))
            core.vstep(v.tensor_tensor(hot, per_tile(r1), ids, ALU.is_equal))
            if k + 1 < self.top:
                core.vstep(v.scalar_tensor_tensor(out=pr, in0=hot, scalar=-2.0, in1=pr, op0=ALU.mult, op1=ALU.add))
        if self.top == 2:
            v.tensor_tensor(self.both, self.hot[:, 0, :, :], self.hot[:, 1, :, :], ALU.add).then_inc(self.chosen, 1)
            core.vstep(v.tensor_tensor(r1, self.top_p[:, 0, :], self.top_p[:, 1, :], ALU.add))
            core.vstep(v.reciprocal(r1, r1))
            core.vstep(v.tensor_tensor(self.top_p, self.top_p, r1.unsqueeze(1).to_broadcast([P, 2, T]), ALU.mult))
        else:
            v.tensor_copy(self.both, self.hot[:, 0, :, :]).then_inc(self.chosen, 1)
        for k in range(self.top):
            core.vmark(v.tensor_copy(self.rows[:, k, :, D + 1], self.top_p[:, k, :]))
        totals = ps[:, self.ranks.bank, P:2 * P].rearrange("p (t e) -> p e t", e=NE)
        ranks = ps[:, self.ranks.bank, 0:P].rearrange("p (t e) -> p t e", e=NE)
        cnt = self.cnt
        core.result(dve, self.ranks)
        core.vstep(v.tensor_copy(self.tot, totals))
        flat = "p e t -> p (e t)"
        core.vstep(v.tensor_tensor_scan(self.incl.rearrange(flat), w.not_first[:, :], self.tot.rearrange(flat), 0.0,
                                        ALU.mult, ALU.add))
        core.vstep(v.tensor_scalar(self.cnt_i, self.incl[:, :, T - 1], float(P - 1), None, ALU.add))
        core.vstep(v.tensor_scalar(self.cnt_i, self.cnt_i, 7, 7, ALU.logical_shift_right, ALU.logical_shift_left))
        core.vstep(v.tensor_copy(cnt[:, 0, :], self.cnt_i))
        core.vstep(v.tensor_tensor_scan(cnt[:, 1, :], w.ones[:, 0:NE], cnt[:, 0, :], 0.0, ALU.mult, ALU.add))
        core.vstep(v.tensor_tensor(cnt[:, 2, :], cnt[:, 1, :], cnt[:, 0, :], ALU.subtract))
        core.vstep(v.tensor_tensor(self.incl, self.incl, self.tot, ALU.subtract))
        core.vstep(v.tensor_tensor(self.incl, self.incl, cnt[:, 2, :].unsqueeze(2).to_broadcast([P, NE, T]), ALU.add))
        v.tensor_tensor(self.pos, ranks, self.incl.rearrange("p e t -> p t e"),
                        ALU.add).then_inc(core.emptied[self.ranks.bank], 1)
        core.moved(dve, self.ranks)
        for k in range(self.top):
            core.vstep(v.tensor_tensor(tmp, self.hot[:, k, :, :], self.pos, ALU.mult))
            core.vstep(v.tensor_reduce(r1, tmp, AX.X, ALU.add))
            if k + 1 < self.top:
                core.vstep(v.tensor_copy(self.slot[:, k, :], r1))
        v.tensor_copy(self.slot[:, self.top - 1, :], r1).then_inc(self.slots_in, 1)
        n = self.tiles
        over, off = self.over[0:1, 0:n, :], self.tile_w[0:1, 0:n]
        core.vstep(v.tensor_tensor(over, w.tile_starts[0:1, 0:n].unsqueeze(2).to_broadcast([1, n, NE]),
                                   cnt[0:1, 1, :].unsqueeze(1).to_broadcast([1, n, NE]), ALU.is_ge))
        core.vstep(v.tensor_reduce(off, over, AX.X, ALU.add))
        core.vstep(v.tensor_scalar(off, off, float(NE - 1), None, ALU.min))
        v.tensor_scalar(self.tile_at[0:1, 1, 0:n], off, float(FC), None, ALU.mult).then_inc(self.slots_in, 1)
        pair = self.pair[0:1, :]
        core.vstep(v.memset(pair, 0.0))
        core.vstep(v.tensor_scalar(pair[:, 3:n + 3], off, float(PAIR * FF), None, ALU.mult))
        core.vstep(v.scalar_tensor_tensor(out=pair[:, 1:n + 1], in0=off, scalar=float(FF), in1=pair[:, 1:n + 1],
                                          op0=ALU.mult, op1=ALU.add))
        v.tensor_copy(self.tile_at[0:1, 0, 0:n + 3], pair[:, 0:n + 3]).then_inc(self.slots_in, 1)
        if self.fresh:
            self.ew.split_w1(dve)
        if self.meanwhile:
            self.meanwhile.vector(dve)

        def step(s, p, m):
            def live(lag):
                return s is None or 0 <= s - lag < self.tiles
            q = 1 - p
            mq = m - q
            if live(0):
                if s is None or s >= 2:
                    self.used_before(dve, 1, p, m)
                self.result(dve, 0, p, m)
                v.tensor_copy(self.xgT[:, p, :, :].rearrange("p k t -> p (k t)"),
                              ps[:, p, 0:P].bitcast(F16)).then_inc(core.emptied[p], 1)
            if live(3):
                tile = 2 * (mq - 1) + q
                which = slice(tile, tile + 1) if s is not None else bass.ds(tile, 1)
                self.result(dve, 2, q, mq - 1)
                v.tensor_tensor(self.y[:, which, :], ps[:, 4 + q:5 + q, 0:D],
                                self.sorted[:, which, D + 1:D + 2].to_broadcast([P, 1, D]), ALU.mult
                                ).then_inc(core.emptied[4 + q], 1)

        self.over_tiles(dve, step, 3)
        for g in range(4):
            ts = slice(4 * g, 4 * g + 4)
            dve.wait_ge(self.back[g], 16 * self.top)
            for k in range(self.top):
                core.vstep(v.tensor_tensor(core.x[:, ts, :], core.x[:, ts, :], self.yg[:, k, ts, :], ALU.add))


class SoftmaxAttention:

    SHIFT = 256.0

    def __init__(self, core, w):
        self.core, self.w = core, w
        s = core.sem
        self.outer_normed = s("sa_outer_normed")
        self.normed = s("sa_normed")
        self.rotated = s("sa_rotated")
        self.split_in = s("sa_split")
        self.pads = s("sa_pads")
        self.cleared = s("sa_cleared")
        self.masked_q = [s(f"sa_masked_q{i}") for i in range(2)]
        self.masked_k = [s(f"sa_masked_k{i}") for i in range(2)]
        self.ring_in = s("sa_ring_in")
        self.ring_out = s("sa_ring_out")
        self.max_in = s("sa_max_in")
        self.score_in = s("sa_score_in")
        self.prob_in = s("sa_prob_in")
        self.wave_in = s("sa_wave_in")
        self.sum_out = s("sa_sum_out")
        self.value_in = s("sa_value_in")
        self.att_in = s("sa_att")
        self.u2_in = s("sa_u2")
        self.bias_in = s("sa_bias")
        self.x_in = s("sa_x")
        self.ln2 = s("sa_ln2")
        c, at = carve, 0
        self.qT, at = c(core, at, [NG, N], F16)
        self.kT, at = c(core, at, [NG, N], F16)
        self.qM, at = c(core, at, [2, HG, S], F16)
        self.kM, mid = c(core, at, [2, HG, S], F16)
        self.qs, _ = c(core, at, [T, H, 32], F16)
        self.prob, _ = c(core, mid, [2, HG, 512])
        self.ks, at = c(core, mid, [T, H, 32], F16)
        self.v, at = c(core, at, [T, D])
        self.vs, at = c(core, at, [2, TB, HG, 32])
        self.qT2, at = c(core, at, [2, S], F16)
        self.m4, at = c(core, at, [TB, P], F16)
        self.mx, at = c(core, at, [TB, HG])
        self.n1, _ = c(core, 0, [T, D])
        ew = core.expert_w
        self.qk = ew[:, 0:T * 256].rearrange("p (t c) -> p t c", t=T)
        self.rot = ew[:, T * 256:2 * T * 256].rearrange("p (t c) -> p t c", t=T)
        self.rtmp, _ = c(core, at, [2, TB * 2 * H * HD // 2])
        self.oT = ew[:, :].rearrange("p (g n) -> p g n", g=NG)
        at = 0
        self.att, at = c(core, at, [T, D])
        self.attT, at = c(core, at, [N])
        self.n2, at = c(core, at, [T, D])
        self.hid, at = c(core, at, [FC, N])
        self.den, at = c(core, at, [2, H])
        self.t = []
        for b in range(B):
            self.t.append({"xT": core.turns(2), "qkv": core.turns(8)})
        for b in range(B):
            self.t[b]["qkT"] = core.turns(8)
        self.before_units = list(core.uses)
        self.o_turns = core.turns(T)
        for b in range(B):
            self.t[b].update(attT=core.turns(2), wo=core.turns(2))
        for b in range(B):
            self.t[b].update(x2T=core.turns(2), up=core.turns(8), down=core.turns(2))

    RING = 34

    @staticmethod
    def ring_use(a):
        half, k = divmod(a, 17)
        return ("turn", half, 0) if k == 16 else ("max", 4 * half + k // 4, k % 4)

    def ring_fill(self, pe, a, g, b, m, second=False):
        core, nc = self.core, self.core.nc
        slot = a % 2
        kind, qt, j = self.ring_use(a)
        if not second:
            first_of_all = isinstance(m, int) and m == 0 and b == 0 and a < 2
            if not first_of_all:
                pe.wait_ge(self.ring_out, m * (2 * self.RING) + (b * self.RING + a - 1))
        if kind == "turn":
            pe.wait_ge(self.max_in, m * 4 + (2 * b + qt + 1))
            out = core.psum[:, 2 * slot, 0:256].bitcast(F16)
            for i in range(4):
                last = nc.tensor.transpose(out[:, i * P:(i + 1) * P], self.m4[:, 4 * qt + i, :], self.w.ident16[:, :])
            last.then_inc(self.ring_in, 1)
            return
        half = int(second)
        at = g * N + (b * S + 512 * half)
        keys = self.kT.rearrange("p g n -> p (g n)")
        keys = keys[:, at:at + 512] if isinstance(g, int) else keys[:, bass.ds(at, 512)]
        last = nc.tensor.matmul(core.psum[:, 2 * slot + half, :], self.qM[:, b, j, qt * P:(qt + 1) * P], keys,
                                start=True, stop=True)
        if second:
            last.then_inc(self.ring_in, 1)

    def ring_read(self, dve, a, g, b, m):
        core, v = self.core, self.core.nc.vector
        slot = a % 2
        kind, qt, j = self.ring_use(a)
        dve.wait_ge(self.ring_in, m * (2 * self.RING) + (b * self.RING + a + 1))
        if kind == "max":
            v.reduce_max(self.mx[:, qt, j:j + 1], core.psum[:, 2 * slot:2 * slot + 2, :].rearrange("p a n -> p (a n)"),
                         AX.X).then_inc(self.ring_out, 1)
            if a % 17 == 15:
                half = a // 17
                dve.wait_ge(self.ring_out, m * (2 * self.RING) + (b * self.RING + a + 1))
                rows = self.m4[:, 4 * half:4 * half + 4, :].rearrange("p t (j r) -> p t j r", r=32)[:, :, :, 24]
                v.tensor_scalar(rows, self.mx[:, 4 * half:4 * half + 4, :], -1.0 / self.SHIFT, None,
                                ALU.mult).then_inc(self.max_in, 1)
        else:
            at = g * N + (b * S + 512 * qt)
            queries = self.qT.rearrange("p g n -> p (g n)")
            queries = queries[:, at:at + 512] if isinstance(g, int) else queries[:, bass.ds(at, 512)]
            v.tensor_tensor(self.qT2[:, b, 512 * qt:512 * (qt + 1)], queries,
                            core.psum[:, 2 * slot, 0:256].bitcast(F16), ALU.add).then_inc(self.ring_out, 1)

    def move_sum(self, dve, half, g, b, m):
        dve.wait_ge(self.wave_in, m * 32 + (16 * b + 8 * half + 8))
        at = g * N + (b * S + 512 * half)
        out = self.oT.rearrange("p g n -> p (g n)")
        out = out[:, at:at + 512] if isinstance(g, int) else out[:, bass.ds(at, 512)]
        self.core.nc.vector.tensor_copy(out, self.core.psum[:, 6 + half, :]).then_inc(self.sum_out, 1)

    def wave(self, pe, k, g, b, m):
        core, nc = self.core, self.core.nc
        half, kt = divmod(k, 8)
        pe.wait_ge(self.prob_in, m * 128 + (64 * b + 4 * k + 4))
        if kt == 0 and not (isinstance(m, int) and m == 0 and b == 0):
            pe.wait_ge(self.sum_out, m * 4 + (2 * b + half - 1))
        for j in range(HG):
            last = nc.tensor.matmul(core.psum[32 * j:32 * j + 32, 6 + half, :], self.vs[:, b, kt, j, :],
                                    self.prob[:, k % 2, j, :], start=(kt == 0), stop=(kt == TB - 1))
        last.then_inc(self.wave_in, 1)

    def unit_tensor(self, pe, b, m, following=True):
        core, nc = self.core, self.core.nc
        nb, nm = 1 - b, m + b
        plan = list(range(self.RING)) if following else []
        pe.wait_ge(self.masked_k[b], 64 * m + 64)
        pe.wait_ge(self.value_in, m * 2 + (b + 1))
        if following:
            pe.wait_ge(self.masked_q[nb], 64 * nm + 64)
        for k in range(16):
            half, kt = divmod(k, 8)
            if kt == 0:
                pe.wait_ge(self.ring_out, m * (2 * self.RING) + (b * self.RING + 17 * (half + 1)))
            parts = []
            for _ in range(3 if k in (4, 12) else 2):
                if plan:
                    a = plan.pop(0)
                    parts.append((a, False))
                    if self.ring_use(a)[0] == "max":
                        parts.append((a, True))
            for j in range(HG):
                tile = 64 * b + 4 * k + j
                if not (isinstance(m, int) and m == 0 and tile < 2):
                    pe.wait_ge(self.prob_in, m * 128 + (tile - 1))
                nc.tensor.matmul(core.psum[:, 4 + j % 2, :], self.kM[:, b, j, kt * P:(kt + 1) * P],
                                 self.qT2[:, b, 512 * half:512 * (half + 1)], start=True,
                                 stop=True).then_inc(self.score_in, 1)
                take = (len(parts) + HG - 1 - j) // (HG - j)
                for _ in range(take):
                    a, second = parts.pop(0)
                    self.ring_fill(pe, a, nm, nb, nm, second)
            if k > 0:
                self.wave(pe, k - 1, m, b, m)
        self.wave(pe, 15, m, b, m)

    def unit_vector(self, dve, b, m, following=True):
        nb, nm = 1 - b, m + b
        for a in range(self.RING if following else 0):
            self.ring_read(dve, a, nm, nb, nm)
            if a == 3 and not (isinstance(m, int) and m == 0 and b == 0):
                self.move_sum(dve, 1, m - (1 - b), nb, m - (1 - b))
            if a == 20:
                self.move_sum(dve, 0, m, b, m)
        if not following:
            self.move_sum(dve, 1, m - (1 - b), nb, m - (1 - b))
            self.move_sum(dve, 0, m, b, m)
            self.move_sum(dve, 1, m, b, m)

    def unit_scalar(self, act, b, m):
        core, nc = self.core, self.core.nc
        for k in range(16):
            if not (isinstance(m, int) and m == 0 and b == 0 and k < 2):
                act.wait_ge(self.wave_in, m * 32 + (16 * b + k - 1))
            for j in range(HG):
                act.wait_ge(self.score_in, m * 128 + (64 * b + 4 * k + j + 1))
                nc.scalar.activation(self.prob[:, k % 2, j, :], core.psum[:, 4 + j % 2, :],
                                     ACT.Exp).then_inc(self.prob_in, 1)

    def tensor(self, pe):
        core, w, nc = self.core, self.w, self.core.nc
        ps = core.psum
        pe.wait_ge(w.sa_in, w.sa_all)
        for b in range(B):
            pe.wait_ge(self.normed, b + 1)
            for g, turn in enumerate(self.t[b]["xT"]):
                transpose_tiles(core, pe, turn, [self.n1[:, b * TB + 4 * g + i, :] for i in range(4)], w.ident[:, :])
            for i, turn in enumerate(self.t[b]["qkv"]):
                core.claim(pe, turn)
                core.moved(pe, self.t[b]["xT"][i // 4])
                nc.tensor.matmul(ps[:, turn.bank, 0:384], core.xnT[:, b, 1 + i * P:1 + (i + 1) * P],
                                 w.sa_wqkv[:, :], start=True, stop=True).then_inc(core.filled[turn.bank], 1)
        pe.wait_ge(self.pads, 2)
        pe.wait_ge(w.ident16_in, 1)
        for b in range(B):
            pe.wait_ge(self.split_in, 2 * b + 2)
            for i, turn in enumerate(self.t[b]["qkT"]):
                parts, g = (self.qs, self.ks)[i // NG], i % NG
                core.claim(pe, turn)
                out = ps[:, turn.bank, :].bitcast(F16)
                for t in range(TB):
                    last = nc.tensor.transpose(
                        out[:, t * P:(t + 1) * P],
                        parts[:, b * TB + t, HG * g:HG * g + HG, :].rearrange("p j r -> p (j r)"), w.ident16[:, :])
                last.then_inc(core.filled[turn.bank], 1)
        for i in range(8):
            pe.wait_ge(core.emptied[i], self.before_units[i])
        pe.wait_ge(self.masked_q[0], 64)
        for a in range(self.RING):
            self.ring_fill(pe, a, 0, 0, 0)
            if self.ring_use(a)[0] == "max":
                self.ring_fill(pe, a, 0, 0, 0, second=True)
        for b in range(B):
            self.unit_tensor(pe, b, 0)
        with pe.Fori(1, NG - 1) as g:
            for b in range(B):
                self.unit_tensor(pe, b, g)
        self.unit_tensor(pe, 0, NG - 1)
        self.unit_tensor(pe, 1, NG - 1, following=False)
        pe.wait_ge(self.sum_out, 2 * B * NG)
        for t, turn in enumerate(self.o_turns):
            transpose_tiles(core, pe, turn, [self.oT[:, g, t * P:(t + 1) * P] for g in range(NG)], w.ident[:, :])
        for b in range(B):
            tb = self.t[b]
            for g, turn in enumerate(tb["attT"]):
                t = b * TB + 4 * g
                for i in range(4):
                    core.moved(pe, self.o_turns[t + i])
                transpose_tiles(core, pe, turn, [self.att[:, t + i, :] for i in range(4)], w.ident[:, :])
            for g, turn in enumerate(tb["wo"]):
                core.claim(pe, turn)
                core.moved(pe, tb["attT"][g])
                for i in range(4):
                    t = b * TB + 4 * g + i
                    last = nc.tensor.matmul(ps[:, turn.bank, i * D:(i + 1) * D], self.attT[:, t * P:(t + 1) * P],
                                            w.sa_wo[:, :], start=True, stop=True)
                last.then_inc(core.filled[turn.bank], 1)
        for b in range(B):
            tb = self.t[b]
            pe.wait_ge(self.ln2, b + 1)
            for g, turn in enumerate(tb["x2T"]):
                transpose_tiles(core, pe, turn, [self.n2[:, b * TB + 4 * g + i, :] for i in range(4)], w.ident[:, :])
            for i, turn in enumerate(tb["up"]):
                c, half = i % FC, i // FC
                core.claim(pe, turn)
                core.moved(pe, tb["x2T"][half])
                nc.tensor.matmul(ps[:, turn.bank, :], w.sa_w1[:, c * P:(c + 1) * P],
                                 core.xnT[:, b, 1 + 512 * half:1 + 512 * (half + 1)],
                                 start=True, stop=True).then_inc(core.filled[turn.bank], 1)
            for g, turn in enumerate(tb["down"]):
                core.claim(pe, turn)
                for c in range(FC):
                    core.moved(pe, tb["up"][FC * g + c])
                for i in range(4):
                    t = b * TB + 4 * g + i
                    for c in range(FC):
                        last = nc.tensor.matmul(ps[:, turn.bank, i * D:(i + 1) * D], self.hid[:, c, t * P:(t + 1) * P],
                                                w.sa_w2[:, c, :], start=(c == 0), stop=(c == FC - 1))
                last.then_inc(core.filled[turn.bank], 1)

    def scalar(self, act):
        core, w, nc = self.core, self.w, self.core.nc
        ps = core.psum
        for b in range(B):
            deviation(core, b)
            deviation(core, b)
        act.wait_ge(w.sa_in, w.sa_all)
        for b in range(B):
            for g, turn in enumerate(self.t[b]["xT"]):
                core.result(act, turn)
                nc.scalar.activation(core.xnT[:, b, 1 + 512 * g:1 + 512 * (g + 1)], ps[:, turn.bank, :], ACT.Identity,
                                     scale=w.sa_affine[:, 0:1], bias=w.sa_affine[:, 1:2]
                                     ).then_inc(core.emptied[turn.bank], 1)
        for b in range(B):
            for i, turn in enumerate(self.t[b]["qkT"]):
                parts, g = (self.qT, self.kT)[i // NG], i % NG
                core.result(act, turn)
                nc.scalar.copy(parts[:, g, b * S:(b + 1) * S],
                               ps[:, turn.bank, :].bitcast(F16)).then_inc(core.emptied[turn.bank], 1)
        for b in range(B):
            self.unit_scalar(act, b, 0)
        with act.Fori(1, NG) as g:
            for b in range(B):
                self.unit_scalar(act, b, g)
        for b in range(B):
            for g, turn in enumerate(self.t[b]["attT"]):
                at = b * S + 512 * g
                core.result(act, turn)
                nc.scalar.copy(self.attT[:, at:at + 512], ps[:, turn.bank, :]).then_inc(core.emptied[turn.bank], 1)
        for b in range(B):
            deviation(core, b)
        for b in range(B):
            for g, turn in enumerate(self.t[b]["x2T"]):
                core.result(act, turn)
                nc.scalar.activation(core.xnT[:, b, 1 + 512 * g:1 + 512 * (g + 1)], ps[:, turn.bank, :], ACT.Identity,
                                     scale=w.sa_affine[:, 2:3], bias=w.sa_affine[:, 3:4]
                                     ).then_inc(core.emptied[turn.bank], 1)
            for i, turn in enumerate(self.t[b]["up"]):
                c, half = i % FC, i // FC
                at = b * S + 512 * half
                core.result(act, turn)
                nc.scalar.activation(self.hid[:, c, at:at + 512], ps[:, turn.bank, :], ACT.Relu,
                                     bias=w.sa_b1[:, c:c + 1]).then_inc(core.emptied[turn.bank], 1)

    def vector(self, dve):
        core, w, nc = self.core, self.w, self.core.nc
        ps, v = core.psum, self.core.nc.vector
        for b in range(B):
            layer_norm(core, core.x, core.xn, b).then_inc(self.outer_normed, 1)
            dve.wait_ge(self.outer_normed, b + 1)
            layer_norm(core, core.xn, self.n1, b).then_inc(self.normed, 1)
        dve.wait_ge(w.sa_in, w.sa_all)
        for b in range(B):
            tiles = slice(b * TB, (b + 1) * TB)
            for i, turn in enumerate(self.t[b]["qkv"]):
                core.result(dve, turn)
                core.vmark(v.tensor_tensor(self.qk[:, b * TB + i, :], ps[:, turn.bank, 0:256], w.sa_bqkv[:, 0:256],
                                           ALU.add))
                v.tensor_tensor(self.v[:, b * TB + i, :], ps[:, turn.bank, 256:384], w.sa_bqkv[:, 256:384],
                                ALU.add).then_inc(core.emptied[turn.bank], 1)
            core.vsync()
            qk = self.qk[:, tiles, :].rearrange("p t (h j e) -> p t h j e", h=2 * H, e=2)
            rot = self.rot[:, tiles, :].rearrange("p t (h j e) -> p t h j e", h=2 * H, e=2)
            cos, sin = (w.rope[:, i, :, :].unsqueeze(2).to_broadcast([P, TB, 2 * H, HD // 2]) for i in range(2))
            ta, tb_ = (self.rtmp[:, i, :].rearrange("p (t h j) -> p t h j", t=TB, h=2 * H) for i in range(2))
            core.vmark(v.tensor_tensor(ta, qk[:, :, :, :, 0], cos, ALU.mult))
            core.vstep(v.tensor_tensor(tb_, qk[:, :, :, :, 1], sin, ALU.mult))
            core.vstep(v.tensor_tensor(rot[:, :, :, :, 0], ta, tb_, ALU.subtract))
            core.vmark(v.tensor_tensor(ta, qk[:, :, :, :, 0], sin, ALU.mult))
            core.vstep(v.tensor_tensor(tb_, qk[:, :, :, :, 1], cos, ALU.mult))
            core.vstep(v.tensor_tensor(rot[:, :, :, :, 1], ta, tb_, ALU.add))
            if b == 0:
                dve.wait_ge(self.pads, 2)
            q = self.rot[:, tiles, 0:D].rearrange("p t (h d) -> p t h d", d=HD)
            k = self.rot[:, tiles, D:2 * D].rearrange("p t (h d) -> p t h d", d=HD)
            qs, ks = self.qs[:, tiles, :, :], self.ks[:, tiles, :, :]
            scale = float(HD) ** -0.5
            core.vmark(v.tensor_scalar(qs[:, :, :, 0:8], q, scale, None, ALU.mult))
            core.vstep(v.tensor_copy(ks[:, :, :, 0:8], k))
            core.vmark(v.tensor_copy(qs[:, :, :, 8:16], qs[:, :, :, 0:8]))
            core.vmark(v.tensor_copy(ks[:, :, :, 16:24], ks[:, :, :, 0:8]))
            for t in range(b * TB, (b + 1) * TB):
                qt = self.rot[:, t, 0:D].rearrange("p (h d) -> p h d", d=HD)
                core.vmark(v.scalar_tensor_tensor(out=self.qs[:, t, :, 16:24], in0=qt, scalar=scale,
                                                  in1=self.qs[:, t, :, 0:8], op0=ALU.mult, op1=ALU.subtract))
            core.vsync()
            v.tensor_tensor(ks[:, :, :, 8:16], k, ks[:, :, :, 0:8], ALU.subtract).then_inc(self.split_in, 1)
            dve.wait_ge(self.split_in, 2 * b + 1)
            dve.engine_nop().then_inc(self.split_in, 1)
        for a in range(self.RING):
            self.ring_read(dve, a, 0, 0, 0)
        for b in range(B):
            self.unit_vector(dve, b, 0)
        with dve.Fori(1, NG - 1) as g:
            for b in range(B):
                self.unit_vector(dve, b, g)
        self.unit_vector(dve, 0, NG - 1)
        self.unit_vector(dve, 1, NG - 1, following=False)
        for t, turn in enumerate(self.o_turns):
            core.result(dve, turn)
            view = ps[:, turn.bank, :].rearrange("p (h r) -> p h r", r=32)
            den = self.den[:, t % 2, :]
            core.vstep(v.reciprocal(den, view[:, :, 8]))
            v.tensor_tensor(self.att[:, t, :].rearrange("p (h d) -> p h d", d=HD), view[:, :, 0:HD],
                            den.unsqueeze(2).to_broadcast([P, H, HD]), ALU.mult).then_inc(core.emptied[turn.bank], 1)
        u = core.xn
        for b in range(B):
            dve.wait_ge(self.bias_in, b + 1)
            for g, turn in enumerate(self.t[b]["wo"]):
                ts = slice(b * TB + 4 * g, b * TB + 4 * g + 4)
                core.result(dve, turn)
                v.tensor_tensor(u[:, ts, :], u[:, ts, :], ps[:, turn.bank, :].rearrange("p (t d) -> p t d", d=D),
                                ALU.add).then_inc(core.emptied[turn.bank], 1)
            for turn in self.t[b]["wo"]:
                core.moved(dve, turn)
            layer_norm(core, u, self.n2, b).then_inc(self.ln2, 1)
        for b in range(B):
            dve.wait_ge(self.x_in, b + 1)
            for g, turn in enumerate(self.t[b]["down"]):
                xs = core.x[:, b * TB + 4 * g:b * TB + 4 * g + 4, :]
                core.result(dve, turn)
                v.tensor_tensor(xs, xs, ps[:, turn.bank, :].rearrange("p (t d) -> p t d", d=D),
                                ALU.add).then_inc(core.emptied[turn.bank], 1)
        for b in range(B):
            for turn in self.t[b]["down"]:
                core.moved(dve, turn)

    def gpsimd(self, pool):
        core, w, g_ = self.core, self.w, self.core.nc.gpsimd
        pool.wait_ge(self.outer_normed, 1)
        g_.memset(self.qM, 0.0).then_inc(self.cleared, 1)
        g_.memset(self.m4, 0.0).then_inc(self.cleared, 1)
        g_.memset(self.qs[:, :, :, 24:32], 0.0).then_inc(self.pads, 1)
        g_.memset(self.ks[:, :, :, 25:32], 0.0).then_inc(self.cleared, 1)
        g_.memset(self.ks[:, :, :, 24:25], self.SHIFT).then_inc(self.pads, 1)
        g_.memset(self.vs[:, :, :, :, 9:32], 0.0).then_inc(self.cleared, 1)
        g_.memset(self.vs[:, :, :, :, 8:9], 1.0).then_inc(self.cleared, 1)
        for turn in self.t[1]["qkT"]:
            core.moved(pool, turn)
        g_.memset(self.kM, 0.0).then_inc(self.cleared, 1)

        def values(g, b, m):
            if not isinstance(m, int) or m > 0:
                pool.wait_ge(self.wave_in, m * 32 + 16 * (b - 1))
            src = self.v[:, b * TB:(b + 1) * TB, :]
            at = g * (HG * HD)
            src = src[:, :, at:at + HG * HD] if isinstance(g, int) else src[:, :, bass.ds(at, HG * HD)]
            g_.tensor_copy(self.vs[:, b, :, :, 0:HD], src.rearrange("p t (j d) -> p t j d", d=HD)
                           ).then_inc(self.value_in, 1)

        for b in range(B):
            values(0, b, 0)
        with pool.Fori(1, NG) as g:
            for b in range(B):
                values(g, b, g)
        for b in range(B):
            us = core.xn[:, b * TB:(b + 1) * TB, :]
            g_.tensor_tensor(us, us, w.sa_bo[:, :].unsqueeze(1).to_broadcast([P, TB, D]),
                             ALU.add).then_inc(self.bias_in, 1)
        for b in range(B):
            pool.wait_ge(self.ln2, b + 1)
            xs, us = core.x[:, b * TB:(b + 1) * TB, :], core.xn[:, b * TB:(b + 1) * TB, :]
            core.pstep(g_.tensor_tensor(xs, xs, us, ALU.add))
            g_.tensor_tensor(xs, xs, w.sa_b2[:, :].unsqueeze(1).to_broadcast([P, TB, D]),
                             ALU.add).then_inc(self.x_in, 1)

    def sync(self, sp):
        core = self.core

        def masked(src_all, dst, sem, g, b):
            at = g * N + b * S
            src = src_all.rearrange("p g n -> p (g n)")
            for j in range(HG):
                rows = slice(32 * j, 32 * j + 32)
                s = src[rows, at:at + S] if isinstance(g, int) else src[rows, bass.ds(at, S)]
                sp.dma_start(dst[rows, b, j, :], s).then_inc(sem[b], 16)

        def unit(g, b, m):
            if not isinstance(m, int) or m > 0:
                sp.wait_ge(self.ring_in, m * (2 * self.RING) + ((b - 2) * self.RING + 33))
            masked(self.qT, self.qM, self.masked_q, g, b)
            if not isinstance(m, int) or m > 0:
                sp.wait_ge(self.score_in, m * 128 + 64 * (b - 1))
            masked(self.kT, self.kM, self.masked_k, g, b)

        for b in range(B):
            for turn in self.t[b]["qkT"]:
                core.moved(sp, turn)
        sp.wait_ge(self.cleared, 6)
        for b in range(B):
            unit(0, b, 0)
        with sp.Fori(1, NG) as g:
            for b in range(B):
                unit(g, b, g)
        for turn in self.o_turns[-8:]:
            core.result(sp, turn)
        self.w.e1.load_w2(sp)


class MemoryWeights:

    def __init__(self, core, w):
        self.core, self.w = core, w
        s, sb = core.sem, core.sb
        self.basisT, self.coeffT = sb("basisT", [64, P]), sb("coeffT", [64, 4, P])
        self.soft = sb("mw_soft", [P, 3, P])
        self.wqkv, self.owT = self.soft, sb("mw_owT", [P, P])
        self.small = sb("mw_small", [P, 2, 3])
        self.powers = sb("mw_powers", [P, 3, P])
        self.within, self.rise = self.powers[:, 0, :], self.powers[:, 1, :]
        self.scal = sb("mw_scal", [P, 8])
        self.loaded = s("mw_loaded")
        self.shifted, self.exps = s("mw_shifted"), s("mw_exps")
        self.normal = s("mw_normal")
        self.abs_in, self.ln_in = s("mw_abs"), s("mw_ln")
        self.lnd_in = s("mw_lnd")
        self.powers_in = s("mw_powers_in")
        self.within_in = s("mw_within_in")

    def take_banks(self):
        self.logits, self.back = self.core.turns(2)

    def load(self, sp):
        a = self.w.a
        for out, src in [(self.basisT[:, :], a["L1_attn_b_basisT"]), (self.coeffT[:, :, :], a["L1_attn_b_coeffT"]),
                         (self.powers[:, :, :], a["c_powers"]), (self.scal[:, 5:6], a["c_to_end"]),
                         (self.scal[:, 0:1], a["L1_attn_b_decay"].partition_broadcast(P)),
                         (self.scal[:, 1:2], a["L1_attn_b_out_scale"].partition_broadcast(P))]:
            sp.dma_start(out, src).then_inc(self.loaded, 16)

    def tensor(self, pe):
        core, nc, ps = self.core, self.core.nc, self.core.psum
        pe.wait_ge(self.loaded, 96)
        core.claim(pe, self.logits)
        for i in range(4):
            last = nc.tensor.matmul(ps[:, self.logits.bank, i * P:(i + 1) * P], self.coeffT[:, i, :], self.basisT[:, :],
                                    start=True, stop=True)
        last.then_inc(core.filled[self.logits.bank], 1)
        pe.wait_ge(self.normal, 1)
        transpose_tiles(core, pe, self.back, [self.soft[:, i, :] for i in range(3)], self.w.ident[:, :])

    def scalar(self, act):
        core, nc = self.core, self.core.nc
        c = self.scal
        act.wait_ge(self.abs_in, 1)
        nc.scalar.activation(c[:, 3:4], c[:, 2:3], ACT.Exp, scale=-1.0).then_inc(self.ln_in, 1)
        act.wait_ge(self.ln_in, 1)
        nc.scalar.activation(c[:, 3:4], c[:, 3:4], ACT.Ln, bias=self.w.ones[:, 0:1]).then_inc(self.ln_in, 1)
        act.wait_ge(self.shifted, 1)
        nc.scalar.activation(self.soft[:, :, :], self.soft[:, :, :], ACT.Exp).then_inc(self.exps, 1)
        act.wait_ge(self.lnd_in, 1)
        lnd = c[:, 4:5]
        nc.scalar.activation(self.within, self.powers[:, 0, :], ACT.Exp, scale=lnd).then_inc(self.powers_in, 1)
        nc.scalar.activation(self.rise, self.powers[:, 1, :], ACT.Exp, scale=lnd).then_inc(self.powers_in, 1)
        nc.scalar.activation(c[:, 6:7], c[:, 5:6], ACT.Exp, scale=lnd).then_inc(self.powers_in, 1)
        nc.scalar.activation(c[:, 7:8], lnd, ACT.Exp, scale=float(P)).then_inc(self.powers_in, 1)
        core.result(act, self.back)
        nc.scalar.copy(self.wqkv[:, :, :], core.psum[:, self.back.bank, 0:3 * P].rearrange("p (i c) -> p i c", i=3)
                       ).then_inc(core.emptied[self.back.bank], 1)

    def vector(self, dve):
        core, v = self.core, self.core.nc.vector
        c = self.scal
        dve.wait_ge(self.loaded, 96)
        core.vstep(v.tensor_scalar(c[:, 2:3], c[:, 0:1], -1.0, None, ALU.mult))
        v.tensor_tensor(c[:, 2:3], c[:, 2:3], c[:, 0:1], ALU.max).then_inc(self.abs_in, 1)
        dve.wait_ge(self.ln_in, 2)
        v.scalar_tensor_tensor(out=c[:, 4:5], in0=c[:, 0:1], scalar=0.0, in1=c[:, 3:4], op0=ALU.min,
                               op1=ALU.subtract).then_inc(self.lnd_in, 1)
        core.result(dve, self.logits)
        view = core.psum[:, self.logits.bank, :].rearrange("p (i c) -> p i c", i=4)
        top, total = self.small[:, 0, :], self.small[:, 1, :]
        core.vstep(v.tensor_reduce(top, view[:, 0:3, :], AX.X, ALU.max))
        core.vmark(v.tensor_copy(self.owT[:, :], view[:, 3, :]))
        v.tensor_tensor(self.soft[:, :, :], view[:, 0:3, :], top.unsqueeze(2).to_broadcast([P, 3, P]),
                        ALU.subtract).then_inc(core.emptied[self.logits.bank], 1)
        core.moved(dve, self.logits)
        dve.engine_nop().then_inc(self.shifted, 1)
        dve.wait_ge(self.exps, 1)
        core.vstep(v.tensor_reduce(total, self.soft[:, :, :], AX.X, ALU.add))
        core.vstep(v.reciprocal(total, total))
        v.tensor_tensor(self.soft[:, :, :], self.soft[:, :, :], total.unsqueeze(2).to_broadcast([P, 3, P]),
                        ALU.mult).then_inc(self.normal, 1)
        dve.wait_ge(self.powers_in, 4)
        v.tensor_tensor(self.within, self.within, self.powers[:, 2, :], ALU.mult).then_inc(self.within_in, 1)


class LinearMemory:

    def __init__(self, core, w, mw):
        self.core, self.w, self.mw = core, w, mw
        s = core.sem
        self.normed = s("lm_normed")
        self.qd_in = s("lm_qd")
        self.state_in = s("lm_state")
        c, at = carve, 0
        self.qT, at = c(core, at, [B, S])
        self.kT, at = c(core, at, [B, S])
        self.qd, at = c(core, at, [B, S])
        self.rT, at = c(core, at, [B, S])
        self.kd, at = c(core, at, [T, P])
        self.v, at = c(core, at, [T, P])
        self.att, at = c(core, at, [T, P])
        self.state, at = c(core, at, [B, TB, P])
        self.t = []
        for b in range(B):
            self.t.append({"xT": core.turns(2), "qT": core.turns(2), "kT": core.turns(2), "kv": core.turns(4)})
        for b in range(B):
            self.t[b].update(grow=core.turns(2), att=core.turns(2))
        for b in range(B):
            self.t[b].update(rT=core.turns(2), out=core.turns(2))

    def tensor(self, pe):
        core, nc, ps, mw = self.core, self.core.nc, self.core.psum, self.mw
        core.moved(pe, mw.back)
        for b in range(B):
            tb = self.t[b]
            pe.wait_ge(self.normed, b + 1)
            for g, turn in enumerate(tb["xT"]):
                transpose_tiles(core, pe, turn, [core.xn[:, b * TB + 4 * g + i, :] for i in range(4)], self.w.ident[:, :])
            for i, name in enumerate(("qT", "kT")):
                for g, turn in enumerate(tb[name]):
                    core.claim(pe, turn)
                    core.moved(pe, tb["xT"][g])
                    nc.tensor.matmul(ps[:, turn.bank, :], mw.wqkv[:, i, :],
                                     core.xnT[:, b, 1 + 512 * g:1 + 512 * (g + 1)],
                                     start=True, stop=True).then_inc(core.filled[turn.bank], 1)
            for r, turn in enumerate(tb["kv"]):
                core.claim(pe, turn)
                for j in range(2):
                    i = 2 * r + j
                    last = nc.tensor.matmul(ps[:, turn.bank, j * 256:(j + 1) * 256],
                                            core.xnT[:, b, 1 + i * P:1 + (i + 1) * P], mw.wqkv[:, 1:3, :],
                                            start=True, stop=True)
                last.then_inc(core.filled[turn.bank], 1)
        for b in range(B):
            tb = self.t[b]
            for g, turn in enumerate(tb["grow"]):
                core.claim(pe, turn)
                for i in range(4 - g):
                    core.moved(pe, tb["kv"][(4 * g + i) // 2])
                    t = b * TB + 4 * g + i
                    last = nc.tensor.matmul(ps[:, turn.bank, i * P:(i + 1) * P], self.kd[:, t, :], self.v[:, t, :],
                                            start=True, stop=True)
                last.then_inc(core.filled[turn.bank], 1)
            for g, turn in enumerate(tb["att"]):
                core.claim(pe, turn)
                core.moved(pe, tb["qT"][g])
                core.moved(pe, tb["kT"][g])
                for i in range(4):
                    at = (4 * g + i) * P
                    last = nc.tensor.matmul(ps[:, turn.bank, i * P:(i + 1) * P], self.kT[:, b, at:at + P],
                                            self.qT[:, b, at:at + P], start=True, stop=True)
                last.then_inc(core.filled[turn.bank], 1)
        for b in range(B):
            tb = self.t[b]
            for g, turn in enumerate(tb["rT"]):
                core.claim(pe, turn)
                core.moved(pe, tb["att"][g])
                for i in range(4):
                    n, t = 4 * g + i, b * TB + 4 * g + i
                    out = ps[:, turn.bank, i * P:(i + 1) * P]
                    last = nc.tensor.matmul(out, self.v[:, t, :], self.att[:, t, :], start=True, stop=(n == 0))
                    if n:
                        pe.wait_ge(self.state_in, (TB - 1) * b + n)
                        pe.wait_ge(self.qd_in, 2 * b + g + 1)
                        last = nc.tensor.matmul(out, self.state[:, b, n, :], self.qd[:, b, n * P:(n + 1) * P],
                                                start=False, stop=True)
                last.then_inc(core.filled[turn.bank], 1)
            for g, turn in enumerate(tb["out"]):
                core.claim(pe, turn)
                core.moved(pe, tb["rT"][g])
                for i in range(4):
                    at = (4 * g + i) * P
                    last = nc.tensor.matmul(ps[:, turn.bank, i * P:(i + 1) * P], self.rT[:, b, at:at + P],
                                            mw.owT[:, :], start=True, stop=True)
                last.then_inc(core.filled[turn.bank], 1)

    def scalar(self, act):
        core, nc, ps = self.core, self.core.nc, self.core.psum
        for b in range(B):
            deviation(core, b)
        for b in range(B):
            for name, to in (("xT", None), ("qT", self.qT), ("kT", self.kT)):
                for g, turn in enumerate(self.t[b][name]):
                    out = (core.xnT[:, b, 1 + 512 * g:1 + 512 * (g + 1)] if to is None
                           else to[:, b, 512 * g:512 * (g + 1)])
                    core.result(act, turn)
                    nc.scalar.copy(out, ps[:, turn.bank, :]).then_inc(core.emptied[turn.bank], 1)
        for b in range(B):
            for g, turn in enumerate(self.t[b]["rT"]):
                core.result(act, turn)
                nc.scalar.copy(self.rT[:, b, 512 * g:512 * (g + 1)],
                               ps[:, turn.bank, :]).then_inc(core.emptied[turn.bank], 1)

    def gpsimd(self, pool):
        core, mw = self.core, self.mw
        pool.wait_ge(mw.powers_in, 4)
        rise = mw.rise.unsqueeze(1).to_broadcast([P, 4, P])
        for b in range(B):
            for g, turn in enumerate(self.t[b]["qT"]):
                core.moved(pool, turn)
                view = "p (i t) -> p i t"
                core.nc.gpsimd.tensor_tensor(self.qd[:, b, 512 * g:512 * (g + 1)].rearrange(view, i=4),
                                             self.qT[:, b, 512 * g:512 * (g + 1)].rearrange(view, i=4), rise,
                                             ALU.mult).then_inc(self.qd_in, 1)

    def vector(self, dve):
        core, mw, ps, v = self.core, self.mw, self.core.psum, self.core.nc.vector
        for b in range(B):
            layer_norm(core, core.x, core.xn, b).then_inc(self.normed, 1)
        to_end, whole = mw.scal[:, 6:7], mw.scal[:, 7:8]
        for b in range(B):
            for r, turn in enumerate(self.t[b]["kv"]):
                ts = slice(b * TB + 2 * r, b * TB + 2 * r + 2)
                core.result(dve, turn)
                view = ps[:, turn.bank, :].rearrange("p (j c) -> p j c", j=2)
                core.vmark(v.tensor_scalar(self.kd[:, ts, :], view[:, :, 0:P], to_end, None, ALU.mult))
                v.tensor_copy(self.v[:, ts, :], view[:, :, P:2 * P]).then_inc(core.emptied[turn.bank], 1)
        within = mw.within.unsqueeze(1).to_broadcast([P, 4, P])
        core.vsync()
        for b in range(B):
            for g, turn in enumerate(self.t[b]["grow"]):
                core.result(dve, turn)
                for i in range(4 - g):
                    n = 4 * g + i
                    grow = ps[:, turn.bank, i * P:(i + 1) * P]
                    if n == 0:
                        v.tensor_copy(self.state[:, b, 1, :], grow).then_inc(self.state_in, 1)
                    else:
                        dve.wait_ge(self.state_in, (TB - 1) * b + n)
                        v.scalar_tensor_tensor(out=self.state[:, b, n + 1, :], in0=self.state[:, b, n, :],
                                               scalar=whole, in1=grow, op0=ALU.mult,
                                               op1=ALU.add).then_inc(self.state_in, 1)
                dve.wait_ge(self.state_in, (TB - 1) * b + 4 * g + 4 - g)
                dve.engine_nop().then_inc(core.emptied[turn.bank], 1)
            for g, turn in enumerate(self.t[b]["att"]):
                ts = slice(b * TB + 4 * g, b * TB + 4 * g + 4)
                core.result(dve, turn)
                v.tensor_tensor(self.att[:, ts, :], ps[:, turn.bank, :].rearrange("p (i t) -> p i t", i=4), within,
                                ALU.mult).then_inc(core.emptied[turn.bank], 1)
        for b in range(B):
            for g, turn in enumerate(self.t[b]["out"]):
                xs = core.x[:, b * TB + 4 * g:b * TB + 4 * g + 4, :]
                core.result(dve, turn)
                v.scalar_tensor_tensor(out=xs, in0=ps[:, turn.bank, :].rearrange("p (t d) -> p t d", d=D),
                                       scalar=mw.scal[:, 1:2], in1=xs, op0=ALU.mult,
                                       op1=ALU.add).then_inc(core.emptied[turn.bank], 1)
        for b in range(B):
            for turn in self.t[b]["out"]:
                core.moved(dve, turn)


def program(nc, a, out):
    with ExitStack() as ctx:
        core = Core(nc, ctx)
        w = Weights(core, a)
        mw = MemoryWeights(core, w)
        blocks = [LinearAttention(core, w), ChannelMix(core, w, "cm1"),
                  Experts(core, w, w.e0, "top2", 2, ACT.Gelu_apprx_tanh, meanwhile=mw), ChannelMix(core, w, "cm2"),
                  SoftmaxAttention(core, w), Experts(core, w, w.e1, "top1a", 1, ACT.Silu),
                  LinearMemory(core, w, mw), Experts(core, w, w.e1, "top1b", 1, ACT.Silu, fresh=False)]
        w.arena_free = blocks[1].normed if len(blocks) > 1 else mw.loaded
        stored = core.sem("stored")
        final = core.sem("final")
        block = ctx.enter_context(nc.Block())

        @block.sync
        def _(sp):
            w.sync(sp, mw)
            for k in blocks:
                if isinstance(k, (Experts, SoftmaxAttention)):
                    k.sync(sp)
            sp.wait_ge(final, 1)
            sp.dma_start(out.rearrange("b (t p) d -> p b t d", p=P),
                         core.x[:, :, :].rearrange("p (b t) d -> p b t d", b=B)).then_inc(stored, 16)
            sp.wait_ge(stored, 16)

        @block.gpsimd
        def _(pool):
            w.gpsimd(pool)
            for k in blocks:
                if isinstance(k, (LinearAttention, Experts, SoftmaxAttention, LinearMemory)):
                    k.gpsimd(pool)

        @block.scalar
        def _(act):
            for k in blocks:
                k.scalar(act)

        @block.tensor
        def _(pe):
            for k in blocks:
                k.tensor(pe)

        @block.vector
        def _(dve):
            for k in blocks:
                k.vector(dve)
            dve.engine_nop().then_inc(final, 1)


def _constants():
    p = np.arange(P)
    freq = (1.0 / np.float32(10000.0) ** (np.arange(0, HD, 2, dtype=np.float32) / HD)).astype(np.float32)
    angle = (np.arange(S, dtype=np.float32)[:, None] * freq[None, :]).astype(np.float32)
    angle = angle.reshape(TB, P, HD // 2).transpose(1, 0, 2)
    head = 4 * np.arange(NG)[None, :] + (p // FEAT)[:, None]
    col_head = np.concatenate([np.arange(D) // HD, np.arange(H)])
    return {
        "c_before": (p[:, None] < p[None, :]).astype(np.float32),
        "c_token_rows": np.arange(2 * N, dtype=np.int32).reshape(2, T, P).transpose(2, 0, 1),
        "c_padding": np.stack([np.where(np.arange(ROW)[None, :] == D, 2 * N + P * i + p[:, None], 0)
                               for i in range(LANES)], 1).astype(np.int32),
        "c_ones": np.ones((P, P), np.float32),
        "c_expert_ids": np.arange(NE, dtype=np.float32) - NE,
        "c_not_first": (np.arange(NE * T) % T != 0).astype(np.float32),
        "c_tile_starts": np.arange(40, dtype=np.float32) * P,
        "c_rope": np.stack([np.cos(angle), np.sin(angle)], 1).astype(np.float32),
        "c_powers": np.stack([np.maximum(p[None, :] - 1 - p[:, None], 0), np.broadcast_to(p[None, :], (P, P)),
                              p[:, None] < p[None, :]], 1).astype(np.float32),
        "c_to_end": (P - 1 - p[:, None]).astype(np.float32),
        "c_ident": np.eye(P, dtype=np.float32),
        "c_head_mask": (p[:, None] // HD == np.arange(H)[None, :]).astype(np.float32),
        "c_kv_mask": (head[:, :, None] == col_head[None, None, :]).astype(np.float32),
    }


def _layouts(i):
    d = {k: v for k, v in i.items()}
    for n in "rkv":
        d[f"L0_ffn_W_{n}T"] = i[f"L0_ffn_W_{n}"].T
    d["L0_attn_a_bqkv"] = np.concatenate([i["L0_attn_a_b" + n] for n in "qkv"])
    d["L1_attn_a_bqkv"] = np.concatenate([i["L1_attn_a_b" + n] for n in "qkv"])
    d["L1_attn_a_b1_cols"] = i["L1_attn_a_b1"].reshape(FC, P).T
    d["L0_attn_b_b1_cols"] = i["L0_attn_b_b1"].reshape(NE * FC, P).T
    d["L1_ffn_b1_cols"] = i["L1_ffn_b1"].reshape(NE * FC, P).T
    d["L1_attn_b_basisT"] = i["L1_attn_b_basis"].T
    d["L1_attn_b_coeffT"] = np.stack([i[f"L1_attn_b_{n}_coeffs"].T for n in "qkvo"], 1)
    d["L0_attn_a_proj"] = i["L0_attn_a_projection"].transpose(0, 2, 1).reshape(P, FEAT)
    return d


_UNUSED = {"L0_ffn_W_r", "L0_ffn_W_k", "L0_ffn_W_v", "L0_attn_a_bq", "L0_attn_a_bk", "L0_attn_a_bv",
           "L0_attn_a_projection", "L1_attn_a_bq", "L1_attn_a_bk", "L1_attn_a_bv", "L1_attn_a_b1", "L0_attn_b_b1", "L1_ffn_b1", "L1_attn_b_basis",
           "L1_attn_b_q_coeffs", "L1_attn_b_k_coeffs", "L1_attn_b_v_coeffs", "L1_attn_b_o_coeffs"}


def kernel(**inputs):
    import concourse.bacc as _bacc
    from concourse.bass_utils import run_bass_kernel_spmd as _run

    nc = _bacc.Bacc("TRN2", target_bir_lowering=False, num_devices=1)
    given = {k: np.asarray(v) for k, v in inputs.items()}
    data = {**_layouts(given), **_constants()}
    arrays, args = {}, {}
    for name in sorted(data):
        if name in _UNUSED:
            continue
        a = np.ascontiguousarray(data[name] if np.ndim(data[name]) else np.reshape(data[name], (1,)))
        arrays[f"in_{name}_dram"] = a
        args[name] = nc.dram_tensor(f"in_{name}_dram", a.shape, mybir.dt.from_np(a.dtype), kind="ExternalInput").ap()
    out = nc.dram_tensor("out_0_dram", (B, S, D), F32, kind="ExternalOutput").ap()
    program(nc, args, out)
    r = _run(nc, [arrays], core_ids=[0])
    return r.results[0]["out_0_dram"]
```

```python
from contextlib import ExitStack

import numpy as np

import concourse.bass as bass
from concourse import mybir

P = 128
F32 = mybir.dt.float32
F16 = mybir.dt.float16
BF16 = mybir.dt.bfloat16
I32 = mybir.dt.int32
ALU = mybir.AluOpType
ACT = mybir.ActivationFunctionType
AX = mybir.AxisListType

B, S, D = 2, 1024, 128
N = B * S
T = N // P
TB = T // B
H, HD = 16, 8
FEAT = 32
NE = 8
FF = 512
FC = FF // P
LANES = 8
ARENA = 28608
HG = 4
NG = H // HG




class Turn:

    def __init__(self, bank, before):
        self.bank, self.before = bank, before


class Core:

    def __init__(self, nc, ctx):
        self.nc, self.ctx = nc, ctx
        self.psum = ctx.enter_context(nc.psum_tensor("psum", [P, 8, 512], F32))
        self.filled = [self.sem(f"bank{i}_filled") for i in range(8)]
        self.emptied = [self.sem(f"bank{i}_emptied") for i in range(8)]
        self.uses = [0] * 8
        self.next_bank = 0
        self.vector_steps = self.sem("vector_steps")
        self.scalar_steps = self.sem("scalar_steps")
        self.pool_steps = self.sem("pool_steps")
        self.variance = self.sem("ln_variance")
        self.root = self.sem("ln_root")
        self.eps = self.sb("eps", [P, 1])
        self.eps_in = self.sem("eps_in")
        self.norms_v = self.norms_s = 0
        self.steps = {"v": 0, "s": 0, "p": 0}
        self.x = self.sb("x", [P, T, D])
        self.xn = self.sb("xn", [P, T, D])
        self.xnT = self.sb("xnT", [P, B, 1 + S])
        self.expert_w = self.sb("expert_w", [P, 2 * NE * FF])
        self.arena = self.sb("arena", [P, ARENA])
        self.stats = self.sb("stats", [P, T, 6])
        self.ln = self.sb("ln_small", [P, 8, T])

    def sem(self, name):
        return self.ctx.enter_context(self.nc.semaphore(name))

    def sb(self, name, shape, dt=F32):
        return self.ctx.enter_context(self.nc.sbuf_tensor(name, shape, dt))

    def turns(self, n):
        out = []
        for _ in range(n):
            b = self.next_bank
            out.append(Turn(b, self.uses[b]))
            self.uses[b] += 1
            self.next_bank = (b + 1) % 8
        return out

    def claim(self, pe, turn):
        if turn.before:
            pe.wait_ge(self.emptied[turn.bank], turn.before)

    def result(self, eng, turn):
        eng.wait_ge(self.filled[turn.bank], turn.before + 1)

    def moved(self, eng, turn):
        eng.wait_ge(self.emptied[turn.bank], turn.before + 1)

    def vstep(self, ins):
        self.steps["v"] += 1
        ins.then_inc(self.vector_steps, 1)
        self.nc.vector.wait_ge(self.vector_steps, self.steps["v"])

    def vmark(self, ins):
        self.steps["v"] += 1
        ins.then_inc(self.vector_steps, 1)

    def vsync(self):
        self.nc.vector.wait_ge(self.vector_steps, self.steps["v"])

    def pstep(self, ins):
        self.steps["p"] += 1
        ins.then_inc(self.pool_steps, 1)
        self.nc.gpsimd.wait_ge(self.pool_steps, self.steps["p"])

    def sstep(self, ins):
        self.steps["s"] += 1
        ins.then_inc(self.scalar_steps, 1)
        self.nc.scalar.wait_ge(self.scalar_steps, self.steps["s"])


def carve(core, at, shape, dt=F32):
    n = int(np.prod(shape))
    words = n // 2 if dt in (F16, BF16) else n
    assert at + words <= ARENA, (at, words)
    v = core.arena[:, at:at + words]
    if dt is not F32:
        v = v.bitcast(dt)
    if len(shape) > 1:
        names = [f"d{i}" for i in range(len(shape))]
        v = v.rearrange(f"p ({' '.join(names)}) -> p {' '.join(names)}", **dict(zip(names[1:], shape[1:])))
    return v, at + words


def spread(core, src, b, between=None):
    nc, ln = core.nc, core.ln
    t0, t1 = b * TB, (b + 1) * TB
    for t in range(t0, t1):
        if t == t0 + TB // 2 and between:
            between()
        core.vmark(nc.vector.bn_stats(core.stats[:, t, :], src[:, t, :]))
    core.vsync()
    st = core.stats
    me, mo = st[:, t0:t1, 1], st[:, t0:t1, 4]
    me2, mo2 = st[:, t0:t1, 2], st[:, t0:t1, 5]
    mean, diff, m2, var = (ln[:, i, t0:t1] for i in range(4))
    core.vmark(nc.vector.tensor_tensor(mean, me, mo, ALU.add))
    core.vmark(nc.vector.tensor_tensor(diff, me, mo, ALU.subtract))
    core.vstep(nc.vector.tensor_tensor(m2, me2, mo2, ALU.add))
    core.vmark(nc.vector.tensor_scalar(mean, mean, 0.5, None, ALU.mult))
    core.vstep(nc.vector.scalar_tensor_tensor(out=var, in0=diff, scalar=0.25, in1=diff, op0=ALU.mult, op1=ALU.mult))
    nc.vector.scalar_tensor_tensor(out=var, in0=m2, scalar=1.0 / D, in1=var, op0=ALU.mult,
                                   op1=ALU.add).then_inc(core.variance, 1)


def inverse_root(core, row, b):
    ln, tiles = core.ln, slice(b * TB, (b + 1) * TB)
    core.norms_v += 1
    core.nc.vector.wait_ge(core.root, core.norms_v)
    core.vstep(core.nc.vector.reciprocal(ln[:, row, tiles], ln[:, row, tiles]))


def center_and_scale(core, src, out, row, b, done):
    ln = core.ln
    for t in range(b * TB, (b + 1) * TB):
        last = core.nc.vector.tensor_scalar(out[:, t, :], src[:, t, :], ln[:, 0, t:t + 1], ln[:, row, t:t + 1],
                                            ALU.subtract, ALU.mult)
        if t < (b + 1) * TB - 1:
            core.vmark(last)
    last.then_inc(done, 1)


def layer_norms(core, src, out, done):
    def first():
        inverse_root(core, 4, 0)
        center_and_scale(core, src, out, 4, 0, done)
    spread(core, src, 0)
    spread(core, src, 1, between=first)
    inverse_root(core, 4, 1)
    center_and_scale(core, src, out, 4, 1, done)


def deviation(core, b, var=3, root=4):
    ln, tiles = core.ln, slice(b * TB, (b + 1) * TB)
    core.norms_s += 1
    core.nc.scalar.wait_ge(core.variance, core.norms_s)
    core.nc.scalar.activation(ln[:, root, tiles], ln[:, var, tiles], ACT.Sqrt,
                              bias=core.eps[:, 0:1]).then_inc(core.root, 1)


def transpose_tiles(core, pe, turn, pieces, identity):
    core.claim(pe, turn)
    for i, piece in enumerate(pieces):
        last = core.nc.tensor.transpose(core.psum[:, turn.bank, i * P:(i + 1) * P], piece, identity)
    last.then_inc(core.filled[turn.bank], 1)


class LinearAttention:

    def __init__(self, core, w):
        self.core, self.w = core, w
        s = core.sem
        self.normed = s("la_normed")
        self.ones = s("la_ones")
        self.squared = s("la_squared")
        self.sums = s("la_sums")
        self.norms = s("la_norms")
        self.unit = s("la_unit")
        self.att_in = s("la_att")
        self.bias_in = s("la_bias")
        at = 0
        self.qkv, at = carve(core, at, [T, 400])
        self.sq, _ = carve(core, at, [B, TB, 256])
        self.att, at = carve(core, at, [T, D])
        self.attT, at = carve(core, at, [N])
        self.qT, at = carve(core, at, [2, N])
        self.kfeat, at = carve(core, at, [TB, H * FEAT])
        self.qfeat, at = carve(core, at, [NG, N])
        self.kv, at = carve(core, at, [B, NG, D + H])
        self.rn, at = carve(core, at, [B, TB, 2 * H])
        self.den, at = carve(core, at, [2, 2, H])
        self.t = []
        for b in range(B):
            self.t.append({"xT": core.turns(2), "qkv": core.turns(8)})
        for b in range(B):
            self.t[b].update(qkT=core.turns(4), kfeat=core.turns(8), qfeat=core.turns(8))
            self.t[b].update(kv=core.turns(2), out=core.turns(4))
            self.t[b].update(attT=core.turns(2), wo=core.turns(2))

    def tensor(self, pe):
        core, w, nc = self.core, self.w, self.core.nc
        ps = core.psum
        for b in range(B):
            pe.wait_ge(self.normed, b + 1)
            if b == 0:
                pe.wait_ge(w.first_in, w.first_all)
            for g, turn in enumerate(self.t[b]["xT"]):
                t = b * TB + 4 * g
                transpose_tiles(core, pe, turn, [core.xn[:, t + i, :] for i in range(4)], w.ident[:, :])
            for i, turn in enumerate(self.t[b]["qkv"]):
                core.claim(pe, turn)
                core.moved(pe, self.t[b]["xT"][i // 4])
                nc.tensor.matmul(ps[:, turn.bank, 0:384], core.xnT[:, b, 1 + i * P:1 + (i + 1) * P],
                                 w.la_wqkv[:, :], start=True, stop=True).then_inc(core.filled[turn.bank], 1)
        for b in range(B):
            tb = self.t[b]
            pe.wait_ge(self.unit, b + 1)
            for g, turn in enumerate(tb["qkT"]):
                t, c = b * TB + 4 * (g % 2), D * (g // 2)
                transpose_tiles(core, pe, turn, [self.qkv[:, t + i, c:c + D] for i in range(4)], w.ident[:, :])
            if b == 0:
                pe.wait_ge(w.proj_in, 1)
            for i, turn in enumerate(tb["kfeat"]):
                core.claim(pe, turn)
                core.moved(pe, tb["qkT"][2 + i // 4])
                nc.tensor.matmul(ps[:, turn.bank, :], self.qT[:, 1, b * S + i * P:b * S + (i + 1) * P],
                                 w.proj[:, :, :], start=True, stop=True).then_inc(core.filled[turn.bank], 1)
            for i, turn in enumerate(tb["qfeat"]):
                c, half = i // 2, i % 2
                core.claim(pe, turn)
                nc.tensor.matmul(ps[:, turn.bank, :], w.proj[:, HG * c:HG * c + HG, :],
                                 self.qT[:, 0, b * S + 512 * half:b * S + 512 * (half + 1)],
                                 start=True, stop=True).then_inc(core.filled[turn.bank], 1)
            if b == 0:
                pe.wait_ge(self.ones, 1)
            for r, turn in enumerate(tb["kv"]):
                core.claim(pe, turn)
                for c in (2 * r, 2 * r + 1):
                    for i in range(TB):
                        if c == 0:
                            core.moved(pe, tb["kfeat"][i])
                        last = nc.tensor.matmul(ps[:, turn.bank, (c % 2) * 144:(c % 2 + 1) * 144],
                                                self.kfeat[:, i, c * P:(c + 1) * P],
                                                self.qkv[:, b * TB + i, 256:400],
                                                start=(i == 0), stop=(i == TB - 1))
                last.then_inc(core.filled[turn.bank], 1)
            core.moved(pe, tb["kv"][0])
            core.moved(pe, tb["kv"][1])
            for turn in tb["qfeat"]:
                core.moved(pe, turn)
            for r, turn in enumerate(tb["out"]):
                core.claim(pe, turn)
                for j in range(2):
                    t = b * TB + 2 * r + j
                    for c in range(NG):
                        last = nc.tensor.matmul(ps[:, turn.bank, j * 144:(j + 1) * 144],
                                                self.qfeat[:, c, t * P:(t + 1) * P], self.kv[:, b, c, :],
                                                start=(c == 0), stop=(c == NG - 1))
                last.then_inc(core.filled[turn.bank], 1)
            for g, turn in enumerate(tb["attT"]):
                t = b * TB + 4 * g
                core.moved(pe, tb["out"][2 * g])
                core.moved(pe, tb["out"][2 * g + 1])
                transpose_tiles(core, pe, turn, [self.att[:, t + i, :] for i in range(4)], w.ident[:, :])
            for g, turn in enumerate(tb["wo"]):
                core.claim(pe, turn)
                core.moved(pe, tb["attT"][g])
                for i in range(4):
                    t = b * TB + 4 * g + i
                    last = nc.tensor.matmul(ps[:, turn.bank, i * D:(i + 1) * D], self.attT[:, t * P:(t + 1) * P],
                                            w.la_wo[:, :], start=True, stop=True)
                last.then_inc(core.filled[turn.bank], 1)

    def scalar(self, act):
        core, nc = self.core, self.core.nc
        ps = core.psum
        act.wait_ge(core.eps_in, 1)
        for b in range(B):
            deviation(core, b)
        for b in range(B):
            for g, turn in enumerate(self.t[b]["xT"]):
                core.result(act, turn)
                nc.scalar.copy(core.xnT[:, b, 1 + 512 * g:1 + 512 * (g + 1)],
                               ps[:, turn.bank, :]).then_inc(core.emptied[turn.bank], 1)
        for b in range(B):
            for turn in self.t[b]["qkv"]:
                core.moved(act, turn)
            nc.scalar.activation(self.sq[:, b, :, :], self.qkv[:, b * TB:(b + 1) * TB, 0:256],
                                 ACT.Square).then_inc(self.squared, 1)
            act.wait_ge(self.sums, b + 1)
            nc.scalar.activation(self.rn[:, b, :, :], self.rn[:, b, :, :], ACT.Sqrt).then_inc(self.norms, 1)
        for b in range(B):
            for g, turn in enumerate(self.t[b]["qkT"]):
                at = b * S + 512 * (g % 2)
                core.result(act, turn)
                nc.scalar.copy(self.qT[:, g // 2, at:at + 512],
                               ps[:, turn.bank, :]).then_inc(core.emptied[turn.bank], 1)
            for g, turn in enumerate(self.t[b]["attT"]):
                at = b * S + 512 * g
                core.result(act, turn)
                nc.scalar.copy(self.attT[:, at:at + 512],
                               ps[:, turn.bank, :]).then_inc(core.emptied[turn.bank], 1)

    def vector(self, dve):
        core, w, nc = self.core, self.w, self.core.nc
        ps, v = core.psum, self.core.nc.vector
        dve.wait_ge(w.x_in, 16 * B)
        layer_norms(core, core.x, core.xn, self.normed)
        dve.wait_ge(w.first_in, w.first_all)
        v.tensor_tensor(w.proj[:, :, :], w.proj_rows[:, :].unsqueeze(1).to_broadcast([P, H, FEAT]),
                        w.head_mask[:, :].unsqueeze(2).to_broadcast([P, H, FEAT]),
                        ALU.mult).then_inc(w.proj_in, 1)
        v.tensor_copy(w.ident16[:, :], w.ident[:, :]).then_inc(w.ident16_in, 1)
        w.e0.split_biases(dve)
        w.e1.split_biases(dve)
        for b in range(B):
            for i, turn in enumerate(self.t[b]["qkv"]):
                core.result(dve, turn)
                v.tensor_tensor(self.qkv[:, b * TB + i, 0:384], ps[:, turn.bank, 0:384], w.la_bqkv[:, :],
                                ALU.add).then_inc(core.emptied[turn.bank], 1)
            dve.wait_ge(self.squared, b + 1)
            rn = self.rn[:, b, :, :]
            v.tensor_reduce(rn, self.sq[:, b, :, :].rearrange("p t (h d) -> p t h d", d=HD), AX.X,
                            ALU.add).then_inc(self.sums, 1)
            dve.wait_ge(self.norms, b + 1)
            core.vstep(v.tensor_scalar(rn, rn, 1e-8, None, ALU.add))
            core.vstep(v.reciprocal(rn, rn))
            qk = self.qkv[:, b * TB:(b + 1) * TB, 0:256].rearrange("p t (h d) -> p t h d", d=HD)
            v.tensor_tensor(qk, qk, rn.unsqueeze(3).to_broadcast([P, TB, 2 * H, HD]),
                            ALU.mult).then_inc(self.unit, 1)
        for b in range(B):
            tb = self.t[b]
            for i, turn in enumerate(tb["kfeat"]):
                core.result(dve, turn)
                v.tensor_scalar(self.kfeat[:, i, :], ps[:, turn.bank, :], 0.0, 0.1, ALU.max,
                                ALU.add).then_inc(core.emptied[turn.bank], 1)
            for i, turn in enumerate(tb["qfeat"]):
                at = b * S + 512 * (i % 2)
                core.result(dve, turn)
                v.tensor_scalar(self.qfeat[:, i // 2, at:at + 512], ps[:, turn.bank, :], 0.0, 0.1, ALU.max,
                                ALU.add).then_inc(core.emptied[turn.bank], 1)
            for r, turn in enumerate(tb["kv"]):
                core.result(dve, turn)
                v.tensor_tensor(self.kv[:, b, 2 * r:2 * r + 2, :],
                                ps[:, turn.bank, 0:288].rearrange("p (c n) -> p c n", c=2),
                                w.kv_mask[:, 2 * r:2 * r + 2, :], ALU.mult).then_inc(core.emptied[turn.bank], 1)
            for r, turn in enumerate(tb["out"]):
                t = b * TB + 2 * r
                core.result(dve, turn)
                view = ps[:, turn.bank, 0:288].rearrange("p (j n) -> p j n", j=2)
                den = self.den[:, r % 2, :, :]
                core.vstep(v.tensor_scalar(den, view[:, :, D:], 1e-6, None, ALU.max))
                core.vstep(v.reciprocal(den, den))
                v.tensor_tensor(self.att[:, t:t + 2, :].rearrange("p j (h d) -> p j h d", d=HD),
                                view[:, :, 0:D].rearrange("p j (h d) -> p j h d", d=HD),
                                den.unsqueeze(3).to_broadcast([P, 2, H, HD]),
                                ALU.mult).then_inc(core.emptied[turn.bank], 1)
            dve.wait_ge(self.bias_in, b + 1)
            for g, turn in enumerate(tb["wo"]):
                t = b * TB + 4 * g
                core.result(dve, turn)
                xs = core.x[:, t:t + 4, :]
                v.tensor_tensor(xs, xs, ps[:, turn.bank, :].rearrange("p (t d) -> p t d", d=D),
                                ALU.add).then_inc(core.emptied[turn.bank], 1)
        for b in range(B):
            for turn in self.t[b]["wo"]:
                core.moved(dve, turn)

    def gpsimd(self, pool):
        core, w, nc = self.core, self.w, self.core.nc
        nc.gpsimd.memset(self.qkv[:, :, 384:400], 1.0).then_inc(self.ones, 1)
        pool.wait_ge(w.first_in, w.first_all)
        for b in range(B):
            pool.wait_ge(self.normed, b + 1)
            xs = core.x[:, b * TB:(b + 1) * TB, :]
            nc.gpsimd.tensor_tensor(xs, xs, w.la_bo[:, :].unsqueeze(1).to_broadcast([P, TB, D]),
                                    ALU.add).then_inc(self.bias_in, 1)


class ChannelMix:

    def __init__(self, core, w, name):
        self.core, self.w = core, w
        s = core.sem
        self.normed = s(name + "_normed")
        self.xk_in = s(name + "_xk")
        self.xr_in = s(name + "_xr")
        self.act_in = s(name + "_act")
        at = 0
        self.dx, at = carve(core, at, [B, S])
        self.xk, at = carve(core, at, [B, S])
        self.xr, at = carve(core, at, [B, S])
        self.kact, at = carve(core, at, [N])
        self.gate, at = carve(core, at, [T, D])
        self.prod, at = carve(core, at, [T, D])
        self.t = [{"xT": core.turns(2)} for b in range(B)]
        for b in range(B):
            self.t[b].update(k=core.turns(2), r=core.turns(2))
        for b in range(B):
            self.t[b].update(v=core.turns(2))

    def tensor(self, pe):
        core, w, nc = self.core, self.w, self.core.nc
        ps = core.psum
        for b in range(B):
            pe.wait_ge(self.normed, b + 1)
            for g, turn in enumerate(self.t[b]["xT"]):
                t = b * TB + 4 * g
                transpose_tiles(core, pe, turn, [core.xn[:, t + i, :] for i in range(4)], w.ident[:, :])
        pe.wait_ge(w.cm_in, w.cm_all)
        for b in range(B):
            pe.wait_ge(self.xk_in, b + 1)
            for g, turn in enumerate(self.t[b]["k"]):
                core.claim(pe, turn)
                nc.tensor.matmul(ps[:, turn.bank, :], w.cm_wkT[:, :], self.xk[:, b, 512 * g:512 * (g + 1)],
                                 start=True, stop=True).then_inc(core.filled[turn.bank], 1)
            pe.wait_ge(self.xr_in, b + 1)
            for g, turn in enumerate(self.t[b]["r"]):
                core.claim(pe, turn)
                for i in range(4):
                    at = (4 * g + i) * P
                    last = nc.tensor.matmul(ps[:, turn.bank, i * D:(i + 1) * D], self.xr[:, b, at:at + P],
                                            w.cm_wrT[:, :], start=True, stop=True)
                last.then_inc(core.filled[turn.bank], 1)
        for b in range(B):
            for g, turn in enumerate(self.t[b]["v"]):
                core.claim(pe, turn)
                pe.wait_ge(self.act_in, 2 * b + g + 1)
                for i in range(4):
                    at = b * S + (4 * g + i) * P
                    last = nc.tensor.matmul(ps[:, turn.bank, i * D:(i + 1) * D], self.kact[:, at:at + P],
                                            w.cm_wvT[:, :], start=True, stop=True)
                last.then_inc(core.filled[turn.bank], 1)

    def scalar(self, act):
        core, nc = self.core, self.core.nc
        ps = core.psum
        for b in range(B):
            deviation(core, b)
        for b in range(B):
            for g, turn in enumerate(self.t[b]["xT"]):
                core.result(act, turn)
                nc.scalar.copy(core.xnT[:, b, 1 + 512 * g:1 + 512 * (g + 1)],
                               ps[:, turn.bank, :]).then_inc(core.emptied[turn.bank], 1)
        for b in range(B):
            for g, turn in enumerate(self.t[b]["k"]):
                k = self.kact[:, b * S + 512 * g:b * S + 512 * (g + 1)]
                core.result(act, turn)
                nc.scalar.activation(k, ps[:, turn.bank, :], ACT.Relu).then_inc(core.emptied[turn.bank], 1)
                core.moved(act, turn)
                nc.scalar.activation(k, k, ACT.Square).then_inc(self.act_in, 1)
            for g, turn in enumerate(self.t[b]["r"]):
                t = b * TB + 4 * g
                core.result(act, turn)
                nc.scalar.activation(self.gate[:, t:t + 4, :],
                                     ps[:, turn.bank, :].rearrange("p (t d) -> p t d", d=D),
                                     ACT.Sigmoid).then_inc(core.emptied[turn.bank], 1)

    def vector(self, dve):
        core, w, nc = self.core, self.w, self.core.nc
        ps, v = core.psum, self.core.nc.vector
        layer_norms(core, core.x, core.xn, self.normed)
        dve.wait_ge(w.cm_in, w.cm_all)
        dve.wait_ge(w.zero_column, 1)
        for b in range(B):
            for turn in self.t[b]["xT"]:
                core.moved(dve, turn)
            now, before = core.xnT[:, b, 1:1 + S], core.xnT[:, b, 0:S]
            core.vstep(v.tensor_tensor(self.dx[:, b, :], now, before, ALU.subtract))
            v.scalar_tensor_tensor(out=self.xk[:, b, :], in0=self.dx[:, b, :], scalar=w.cm_mu[:, 0:1], in1=before,
                                   op0=ALU.mult, op1=ALU.add).then_inc(self.xk_in, 1)
            v.scalar_tensor_tensor(out=self.xr[:, b, :], in0=self.dx[:, b, :], scalar=w.cm_mu[:, 1:2], in1=before,
                                   op0=ALU.mult, op1=ALU.add).then_inc(self.xr_in, 1)
        for b in range(B):
            for g, turn in enumerate(self.t[b]["v"]):
                t = b * TB + 4 * g
                core.moved(dve, self.t[b]["r"][g])
                core.result(dve, turn)
                prod, xs = self.prod[:, t:t + 4, :], core.x[:, t:t + 4, :]
                v.tensor_tensor(prod, ps[:, turn.bank, :].rearrange("p (t d) -> p t d", d=D),
                                self.gate[:, t:t + 4, :], ALU.mult).then_inc(core.emptied[turn.bank], 1)
                core.moved(dve, turn)
                core.vmark(v.tensor_tensor(xs, xs, prod, ALU.add))
        core.vsync()


class Weights:

    def __init__(self, core, a):
        self.core, self.a = core, a
        s, sb = core.sem, core.sb
        self.x_in, self.first_in, self.cm_in = s("x_in"), s("first_in"), s("cm_in")
        self.proj_in, self.zero_column = s("proj_in"), s("zero_column")
        self.ident = sb("ident", [P, P])
        self.la_wqkv = sb("la_wqkv", [P, 3, D])
        self.la_bqkv = sb("la_bqkv", [P, 3 * D])
        self.la_wo, self.la_bo = sb("la_wo", [P, D]), sb("la_bo", [P, D])
        self.proj_rows, self.proj = sb("proj_rows", [P, FEAT]), sb("proj", [P, H, FEAT])
        self.head_mask, self.kv_mask = sb("head_mask", [P, H]), sb("kv_mask", [P, NG, D + H])
        self.cm_wkT, self.cm_wrT, self.cm_wvT = (sb(f"cm_w{n}T", [P, D]) for n in "krv")
        self.cm_mu = sb("cm_mu", [P, 2])
        self.before, self.ones = sb("before", [P, P]), sb("ones", [P, P])
        self.expert_ids, self.not_first = sb("expert_ids", [P, NE]), sb("not_first", [P, NE * T])
        self.tile_starts = sb("tile_starts", [1, 40])
        self.ones_rows = sb("ones_rows", [3, P], BF16)
        self.ones_rows_in = s("ones_rows_in")
        self.counting = sb("counting", [P, P])
        self.choice_ids = sb("choice_ids", [P, 2, T])
        self.padding_rows = sb("padding_rows", [P, 40])
        self.tokens = core.nc.dram_tensor("tokens", (N, D), F32).ap()
        self.results = core.nc.dram_tensor("results", (2 * N + LANES * P, D), F32).ap()
        self.result_out = [s(f"result_out{i}") for i in range(LANES)]
        self.results_before = [0] * LANES
        self.back = [s(f"results_back{i}") for i in range(4)]
        self.back_before = 0
        self.sa_in, self.ident16_in = s("sa_in"), s("ident16_in")
        self.ident16 = sb("ident16", [P, P], F16)
        self.sa_wqkv, self.sa_bqkv = sb("sa_wqkv", [P, 3, D]), sb("sa_bqkv", [P, 3 * D])
        self.sa_wo, self.sa_bo, self.sa_b2 = sb("sa_wo", [P, D]), sb("sa_bo", [P, D]), sb("sa_b2", [P, D])
        self.sa_w1, self.sa_b1, self.sa_w2 = sb("sa_w1", [P, FF]), sb("sa_b1", [P, FC]), sb("sa_w2", [P, FC, D])
        self.sa_affine = sb("sa_affine", [P, 4])
        self.rope = sb("rope", [P, 2, TB, HD // 2])
        self.sa_all = 16 * 15
        self.bias_rows = sb("bias_rows", [3, NE * FF], BF16)
        self.e0 = ExpertWeights(core, self, "e0")
        self.e1 = ExpertWeights(core, self, "e1")
        self.first_all, self.cm_all = 16 * 10, 16 * 13

    def sync(self, sp, mw):
        core, a = self.core, self.a
        xv = a["L0_attn_a_x"].rearrange("b (t p) d -> b p t d", p=P)
        for b in range(B):
            sp.dma_start(core.x[:, b * TB:(b + 1) * TB, :], xv[b]).then_inc(self.x_in, 16)
        loads = [(self.ident[:, :], a["c_ident"])] + [(self.la_wqkv[:, i, :], a["L0_attn_a_W" + n]) for i, n in enumerate("qkv")]
        loads += [(self.la_bqkv[:, :], a["L0_attn_a_bqkv"].partition_broadcast(P))]
        loads += [(self.proj_rows[:, :], a["L0_attn_a_proj"]), (self.head_mask[:, :], a["c_head_mask"]),
                  (self.kv_mask[:, :, :], a["c_kv_mask"]), (self.la_wo[:, :], a["L0_attn_a_Wo"]),
                  (self.la_bo[:, :], a["L0_attn_a_bo"].partition_broadcast(P))]
        self.first_all = 16 * len(loads)
        for out, src in loads:
            sp.dma_start(out, src).then_inc(self.first_in, 16)
        for out, src in [(self.before[:, :], a["c_before"]), (self.ones[:, :], a["c_ones"]),
                         (self.expert_ids[:, :], a["c_expert_ids"].partition_broadcast(P)),
                         (self.not_first[:, :], a["c_not_first"].partition_broadcast(P)),
                         (self.choice_ids[:, :, :], a["c_choice_ids"]),
                         (self.counting[:, :], a["c_counting"].partition_broadcast(P)),
                         (self.padding_rows[:, :], a["c_padding_rows"]),
                         (self.tile_starts[:, :], a["c_tile_starts"].partition_broadcast(1))]:
            sp.dma_start(out, src).then_inc(self.cm_in, 16)
        for n in "krv":
            sp.dma_start({"k": self.cm_wkT, "r": self.cm_wrT, "v": self.cm_wvT}[n][:, :],
                         a[f"L0_ffn_W_{n}T"]).then_inc(self.cm_in, 16)
        for i, n in enumerate("kr"):
            sp.dma_start(self.cm_mu[:, i:i + 1], a["L0_ffn_mu_" + n].rearrange("(p a) -> p a", a=1)).then_inc(self.cm_in, 16)
        mw.load(sp)
        self.e0.load_small(sp)
        self.e1.load_small(sp)
        self.e0.load_w2(sp)
        col = "(p a) -> p a"
        loads = [(self.sa_wqkv[:, i, :], a["L1_attn_a_W" + n]) for i, n in enumerate("qkv")]
        loads += [(self.sa_bqkv[:, :], a["L1_attn_a_bqkv"].partition_broadcast(P)),
                  (self.sa_wo[:, :], a["L1_attn_a_Wo"]), (self.sa_bo[:, :], a["L1_attn_a_bo"].partition_broadcast(P)),
                  (self.sa_b2[:, :], a["L1_attn_a_b2"].partition_broadcast(P)), (self.sa_w1[:, :], a["L1_attn_a_W1"]),
                  (self.sa_b1[:, :], a["L1_attn_a_b1_cols"]),
                  (self.sa_w2[:, :, :], a["L1_attn_a_W2"].rearrange("(c p) d -> p c d", p=P)),
                  (self.rope[:, :, :, :], a["c_rope"])]
        loads += [(self.sa_affine[:, i:i + 1], a["L1_attn_a_" + n].rearrange(col, a=1))
                  for i, n in enumerate(("g1", "beta1", "g2", "beta2"))]
        for out, src in loads:
            sp.dma_start(out, src).then_inc(self.sa_in, 16)
        for e in (self.e0, self.e1):
            e.bias_to_rows(sp)
        for e in (self.e0, self.e1):
            sp.wait_ge(e.rows_in, e.rows_all)
        sp.wait_ge(self.arena_free, 1)
        self.e0.load_w1(sp)

    def gpsimd(self, pool):
        g = self.core.nc.gpsimd
        g.memset(self.core.eps[:, :], 1e-5).then_inc(self.core.eps_in, 1)
        g.memset(self.ones_rows[:, :], 1.0).then_inc(self.ones_rows_in, 1)
        g.memset(self.core.xnT[:, :, 0:1], 0.0).then_inc(self.zero_column, 1)


class ExpertWeights:

    def __init__(self, core, w, name):
        self.core, self.w, self.name = core, w, name
        s, sb = core.sem, core.sb
        self.gate, self.gate_b = sb(name + "_gate", [P, NE]), sb(name + "_gate_b", [P, NE])
        self.b1 = sb(name + "_b1", [P, NE * FC])
        which = 0 if name == "e0" else 1
        room = core.expert_w[0:NE, which * 4 * D:(which + 1) * 4 * D]
        self.bias_wide, self.bias_rest = room[:, 0:D], room[:, D:2 * D]
        self.bias_parts = room[:, 2 * D:4 * D].bitcast(BF16).rearrange("e (k d) -> e k d", d=D)
        self.bias_rows = w.bias_rows[:, which * D:]
        self.bias_dst = w.bias_rows[:, :].rearrange("k (e f) -> k e f", e=NE)[:, :, which * D:(which + 1) * D]
        self.w1_parts = core.expert_w[:, 0:NE * FF].bitcast(F16).rearrange("p (k n) -> p k n", k=2)
        self.w2 = core.expert_w[:, NE * FF:]
        self.w1_wide = core.arena[:, ARENA - NE * FF:]
        self.small_in = s(name + "_small_in")
        self.w1_in, self.w2_in = s(name + "_w1_in"), s(name + "_w2_in")
        self.w1_rounded = s(name + "_w1_rounded")
        self.w1_split = s(name + "_w1_split")
        self.parts_in = s(name + "_bias_parts_in")
        self.rows_in = s(name + "_bias_rows_in")
        self.small_all, self.rows_all = 16 * 4, 16 * 3
        prefix, (gate, gate_b, w1, b1, w2, b2) = (
            ("L0_attn_b_", ("gate_w", "gate_b", "w1", "b1_cols", "w2", "b2")) if name == "e0" else
            ("L1_ffn_", ("Wg", "bg", "W1", "b1_cols", "W2", "b2")))
        a = w.a
        self.from_dram = {"gate": a[prefix + gate], "gate_b": a[prefix + gate_b], "w1": a[prefix + w1],
                          "b1": a[prefix + b1], "w2": a[prefix + w2], "b2": a[prefix + b2]}

    def load_small(self, sp):
        d = self.from_dram
        loads = [(self.gate[:, :], d["gate"]), (self.gate_b[:, :], d["gate_b"].partition_broadcast(P)),
                 (self.b1[:, :], d["b1"]), (self.bias_wide[:, :], d["b2"])]
        for out, src in loads:
            sp.dma_start(out, src).then_inc(self.small_in, 16)

    def load_w1(self, sp):
        sp.dma_start(self.w1_wide.rearrange("p (e f) -> p e f", e=NE),
                     self.from_dram["w1"].rearrange("e p f -> p e f")).then_inc(self.w1_in, 16)

    def load_w2(self, sp):
        sp.dma_start(self.w2.rearrange("p (e c d) -> p e c d", e=NE, c=FC),
                     self.from_dram["w2"].rearrange("e (c p) d -> p e c d", p=P)).then_inc(self.w2_in, 16)

    def round_w1(self, act):
        act.wait_ge(self.w1_in, 16)
        for k in range(2):
            half = slice(k * NE * FF // 2, (k + 1) * NE * FF // 2)
            self.core.nc.scalar.copy(self.w1_parts[:, 0, half], self.w1_wide[:, half]).then_inc(self.w1_rounded, 1)

    def split_w1(self, eng, k):
        half = slice(k * NE * FF // 2, (k + 1) * NE * FF // 2)
        eng.wait_ge(self.w1_rounded, k + 1)
        eng.tensor_tensor(self.w1_parts[:, 1, half], self.w1_wide[:, half], self.w1_parts[:, 0, half],
                          ALU.subtract).then_inc(self.w1_split, 1)

    def bias_to_rows(self, sp):
        sp.wait_ge(self.parts_in, 3)
        for k in range(3):
            sp.dma_start(self.bias_dst[k:k + 1, :, :], self.bias_parts[:, k, :]).then_inc(self.rows_in, 16)

    def split_biases(self, dve):
        core, v = self.core, self.core.nc.vector
        dve.wait_ge(self.small_in, self.small_all)
        parts, rest = self.bias_parts, self.bias_rest
        v.tensor_copy(parts[:, 0, :], self.bias_wide[:, :]).then_inc(self.parts_in, 1)
        dve.wait_ge(self.parts_in, 1)
        core.vstep(v.tensor_tensor(rest[:, :], self.bias_wide[:, :], parts[:, 0, :], ALU.subtract))
        v.tensor_copy(parts[:, 1, :], rest[:, :]).then_inc(self.parts_in, 1)
        dve.wait_ge(self.parts_in, 2)
        v.tensor_tensor(parts[:, 2, :], rest[:, :], parts[:, 1, :], ALU.subtract).then_inc(self.parts_in, 1)


class Experts:

    def __init__(self, core, w, ew, name, top, func, fresh=True, meanwhile=None):
        self.meanwhile = meanwhile
        self.core, self.w, self.ew, self.top, self.func, self.fresh = core, w, ew, top, func, fresh
        self.tiles = tiles = N * top // P + NE - 1
        assert tiles % 2 == 1
        s, sb = core.sem, core.sb
        self.normed = s(name + "_normed")
        self.shifted = s(name + "_shifted")
        self.exps = s(name + "_exps")
        self.chosen = s(name + "_chosen")
        self.tables_in = s(name + "_tables")
        self.rounded = s(name + "_rounded")
        self.parts_in = s(name + "_parts_in")
        self.tokens_in = s(name + "_tokens_in")
        self.in_tile = s(name + "_in_tile")
        self.weight_in_tile = s(name + "_weight_in_tile")
        self.in_row = s(name + "_in_row")
        self.places_in = s(name + "_places")
        self.tile_in = [s(f"{name}_tile_in{i}") for i in range(2)]
        self.back_before = w.back_before
        w.back_before += 16 * top
        at = 0
        c = carve
        self.probs, at = c(core, at, [T, NE])
        self.top_p, at = c(core, at, [2, T])
        self.tmp, at = c(core, at, [T, NE])
        self.hot, at = c(core, at, [2, T, NE])
        self.both, at = c(core, at, [T, NE])
        self.r1, at = c(core, at, [T])
        self.tot, at = c(core, at, [NE, T])
        self.incl, at = c(core, at, [NE, T])
        self.cnt, at = c(core, at, [4, NE])
        self.cnt_i, at = c(core, at, [NE], I32)
        self.pos, at = c(core, at, [T, NE])
        self.slot, at = c(core, at, [top, T])
        self.slot_int, at = c(core, at, [2, top * T], I32)
        self.slot_row, at = c(core, at, [top * T])
        self.slot_tile, at = c(core, at, [top * T])
        self.places, at = c(core, at, [3, tiles])
        self.padding_row, at = c(core, at, [tiles])
        self.place_int, at = c(core, at, [2, tiles], I32)
        self.over, at = c(core, at, [40, NE])
        self.tile_w, at = c(core, at, [40])
        self.tile_at, at = c(core, at, [2, 40], I32)
        self.xgT, at = c(core, at, [2, 2, P], F16)
        self.hT, at = c(core, at, [2, FC, P])
        self.split, _ = c(core, at, [T, D])
        self.split16, at = c(core, at, [T, 2 * D], F16)
        self.sorted, _ = c(core, at, [tiles, D])
        self.sorted16, at = c(core, at, [tiles, 2 * D], F16)
        self.row_hot, mid = c(core, at, [top * T, P])
        self.tile_hot, end = c(core, mid, [top * T, 3, tiles])
        self.y, at = c(core, at, [tiles, D])
        self.yg, at = c(core, at, [top, T, D])
        assert max(at, end) <= ARENA - NE * FF
        self.xT = core.turns(4)
        (self.logits,) = core.turns(1)
        (self.ranks,) = core.turns(1)
        (self.inverse,) = core.turns(1)
        if meanwhile:
            meanwhile.take_banks()
        self.base = list(core.uses)
        assert min(self.base) > 0
        for i in range(6):
            core.uses[i] += (tiles + 1 - i % 2) // 2
        self.tokens, self.results = w.tokens, w.results
        self.results_before = list(w.results_before)
        for i in range(tiles):
            w.results_before[i % LANES] += 1

    def claim(self, eng, k, p, m):
        eng.wait_ge(self.core.emptied[2 * k + p], m + self.base[2 * k + p])

    def result(self, eng, k, p, m):
        eng.wait_ge(self.core.filled[2 * k + p], m + (self.base[2 * k + p] + 1))

    def moved(self, eng, k, p, m):
        eng.wait_ge(self.core.emptied[2 * k + p], m + (self.base[2 * k + p] + 1))

    def used_before(self, eng, k, p, m):
        eng.wait_ge(self.core.filled[2 * k + p], m + self.base[2 * k + p])

    def over_tiles(self, eng, step, lag):
        first = 2 * ((lag + 3) // 2)
        last = first + 2 * ((self.tiles - first) // 2)
        for s in range(first):
            step(s, s % 2, s // 2)
        with eng.Fori(first // 2, last // 2) as m:
            for p in range(2):
                step(None, p, m)
        for s in range(last, self.tiles + lag):
            step(s, s % 2, s // 2)

    def sync(self, sp):
        if self.fresh and self.ew is self.w.e1:
            sp.wait_ge(self.normed, 1)
            self.ew.load_w1(sp)
        for b in range(B):
            ts = slice(b * TB, (b + 1) * TB)
            sp.wait_ge(self.parts_in, b + 1)
            sp.dma_start(self.tokens[b * S:(b + 1) * S, :].rearrange("(t p) d -> p t d", p=P), self.split[:, ts, :]
                         ).then_inc(self.tokens_in, 16)
        for s in range(self.tiles - LANES, self.tiles):
            sp.wait_ge(self.w.result_out[s % LANES], self.result_count(s))
        rows = self.results[0:self.top * N, :].rearrange("(k t p) d -> p k t d", p=P, t=T)
        for g in range(4):
            for k in range(self.top):
                sp.dma_start(self.yg[:, k, 4 * g:4 * g + 4, :], rows[:, k, 4 * g:4 * g + 4, :]
                             ).then_inc(self.w.back[g], 16)

    def gpsimd(self, pool):
        core, w, g_ = self.core, self.w, self.core.nc.gpsimd
        for b in range(B):
            ts = slice(b * TB, (b + 1) * TB)
            pool.wait_ge(self.rounded, b + 1)
            g_.tensor_tensor(self.split16[:, ts, D:2 * D], core.xn[:, ts, :], self.split16[:, ts, 0:D],
                             ALU.subtract).then_inc(self.parts_in, 1)
        pool.wait_ge(self.in_tile, 1)
        g_.tensor_tensor(self.tile_hot[:, :, 1, :], self.tile_hot[:, :, 2, :], self.per_choice(self.top_p[:, 0:self.top, :]
                         .rearrange("p k t -> p (k t)"), self.tiles), ALU.mult).then_inc(self.weight_in_tile, 1)
        if self.fresh:
            self.ew.split_w1(g_, 1)
        pool.wait_ge(self.tokens_in, 16 * B)
        pool.wait_ge(self.places_in, 1)
        ahead = 6
        for s in range(self.tiles + ahead):
            if s < self.tiles:
                if s >= 2:
                    pool.wait_ge(self.tile_in[s % 2], 16 * (s // 2))
                pool.indirect_dma_start(out=self.sorted[:, s, :], out_offset=None, in_=self.tokens[:, :],
                                        in_offset=bass.IndirectOffsetOnAxis(ap=self.place_int[:, 0, s:s + 1], axis=0)
                                        ).then_inc(self.tile_in[s % 2], 16)
            if s >= ahead:
                t = s - ahead
                self.moved(pool, 2, t % 2, t // 2)
                if t >= LANES:
                    pool.wait_ge(w.result_out[t % LANES], self.result_count(t - LANES))
                pool.indirect_dma_start(out=self.results[:, :],
                                        out_offset=bass.IndirectOffsetOnAxis(ap=self.place_int[:, 1, t:t + 1], axis=0),
                                        in_=self.y[:, t, :], in_offset=None).then_inc(w.result_out[t % LANES], 16)

    def per_choice(self, a, n):
        return a.unsqueeze(2).to_broadcast([P, self.top * T, n])

    def result_count(self, s):
        return 16 * (self.results_before[s % LANES] + s // LANES + 1)

    def tensor(self, pe):
        core, w, nc = self.core, self.w, self.core.nc
        ps = core.psum
        for b in range(B):
            pe.wait_ge(self.normed, b + 1)
            for g in range(2 * b, 2 * b + 2):
                transpose_tiles(core, pe, self.xT[g], [core.xn[:, 4 * g + i, :] for i in range(4)], w.ident[:, :])
            if b == 0:
                pe.wait_ge(self.ew.small_in, self.ew.small_all)
                core.claim(pe, self.logits)
            for t in range(b * TB, (b + 1) * TB):
                if t % 4 == 0:
                    core.moved(pe, self.xT[t // 4])
                i = t % TB
                last = nc.tensor.matmul(ps[:, self.logits.bank, t * NE:(t + 1) * NE],
                                        core.xnT[:, b, 1 + i * P:1 + (i + 1) * P], self.ew.gate[:, :],
                                        start=True, stop=True)
        last.then_inc(core.filled[self.logits.bank], 1)
        pe.wait_ge(self.chosen, 1)
        core.claim(pe, self.ranks)
        both = self.both.rearrange("p t e -> p (t e)")
        nc.tensor.matmul(ps[:, self.ranks.bank, 0:P], w.before[:, :], both, start=True, stop=True)
        nc.tensor.matmul(ps[:, self.ranks.bank, P:2 * P], w.ones[:, :], both, start=True,
                         stop=True).then_inc(core.filled[self.ranks.bank], 1)
        core.claim(pe, self.inverse)
        pe.wait_ge(self.in_tile, 2)
        pe.wait_ge(self.weight_in_tile, 1)
        for i in range(self.top * T):
            if i % (self.top * 4) == 0:
                pe.wait_ge(self.in_row, i // (self.top * 4) + 1)
            last = nc.tensor.matmul(ps[:, self.inverse.bank, 0:3 * self.tiles], self.row_hot[:, i, :],
                                    self.tile_hot[:, i, :, :], start=(i == 0), stop=(i == self.top * T - 1))
        last.then_inc(core.filled[self.inverse.bank], 1)
        if self.meanwhile:
            self.meanwhile.tensor(pe)
        pe.wait_ge(self.ew.w1_split, 2)
        pe.wait_ge(self.ew.w2_in, 16)
        pe.wait_ge(self.ew.rows_in, self.ew.rows_all)
        pe.wait_ge(self.tables_in, 2)
        pe.wait_ge(w.ones_rows_in, 1)
        pe.wait_ge(w.ident16_in, 1)
        w1, w2, brows = self.ew.w1_parts, self.ew.w2, self.ew.bias_rows

        column = {}
        for s in range(self.tiles + 3):
            t = s - 1
            if 0 <= t < self.tiles:
                column[t] = self.tile_value(pe, 0, slice(t, t + 1), (NE - 1) * FF)
            t = s
            if t < self.tiles:
                p, m = t % 2, t // 2
                pe.wait_ge(self.tile_in[p], 16 * m + 16)
                if t < 2:
                    self.claim(pe, 0, p, m)
                for k in range(2):
                    last = nc.tensor.transpose(ps[:, p, k * 64:(k + 1) * 64].bitcast(F16),
                                               self.sorted16[:, t, k * D:(k + 1) * D], w.ident16[:, :])
                last.then_inc(core.filled[p], 1)
            t = s - 1
            if 0 <= t < self.tiles:
                p, m = t % 2, t // 2
                self.moved(pe, 0, p, m)
                self.claim(pe, 1, p, m)
                for c in range(FC):
                    for i, (of_w, of_x) in enumerate(((0, 0), (0, 1), (1, 0))):
                        last = nc.tensor.matmul(ps[:, 2 + p, c * P:(c + 1) * P],
                                                w1[:, of_w, c * P:][:, bass.ds(column[t], P)], self.xgT[:, p, of_x, :],
                                                start=(i == 0), stop=(i == 2))
                last.then_inc(core.filled[2 + p], 1)
            t = s - 3
            if t >= 0:
                p, m = t % 2, t // 2
                self.moved(pe, 1, p, m)
                self.claim(pe, 2, p, m)
                at = column.pop(t)
                for c in range(FC):
                    nc.tensor.matmul(ps[:, 4 + p, 0:D], self.hT[:, p, c, :], w2[:, c * D:][:, bass.ds(at, D)],
                                     start=(c == 0), stop=False)
                nc.tensor.matmul(ps[:, 4 + p, 0:D], w.ones_rows[:, :], brows[:, bass.ds(at, D)],
                                 start=False, stop=True).then_inc(core.filled[4 + p], 1)

    def tile_value(self, eng, which, tile, largest):
        return eng.value_load(self.tile_at[0:1, which, tile], min_val=0, max_val=largest)

    def scalar(self, act):
        core, nc = self.core, self.core.nc
        ps = core.psum
        for b in range(B):
            deviation(core, b)
        for g, turn in enumerate(self.xT):
            core.result(act, turn)
            nc.scalar.copy(core.xnT[:, g // 2, 1 + 512 * (g % 2):1 + 512 * (g % 2 + 1)],
                           ps[:, turn.bank, :]).then_inc(core.emptied[turn.bank], 1)
        for b in range(B):
            ts = slice(b * TB, (b + 1) * TB)
            act.wait_ge(self.normed, b + 1)
            nc.scalar.copy(self.split16[:, ts, 0:D], core.xn[:, ts, :]).then_inc(self.rounded, 1)
        act.wait_ge(self.shifted, 1)
        nc.scalar.activation(self.probs, self.probs, ACT.Exp).then_inc(self.exps, 1)
        if self.fresh:
            self.ew.round_w1(act)
        if self.meanwhile:
            self.meanwhile.scalar(act)
        act.wait_ge(self.tables_in, 2)

        def step(s, p, m):
            at = self.tile_value(act, 1, slice(s, s + 1) if s is not None else bass.ds(2 * m + p, 1), (NE - 1) * FC)
            if s is None or s >= 2:
                self.used_before(act, 2, p, m)
            self.result(act, 1, p, m)
            for c in range(FC):
                last = nc.scalar.activation(self.hT[:, p, c, :], ps[:, 2 + p, c * P:(c + 1) * P], self.func,
                                            bias=self.ew.b1[:, c:][:, bass.ds(at, 1)])
            last.then_inc(core.emptied[2 + p], 1)

        self.over_tiles(act, step, 0)

    def vector(self, dve):
        core, w, nc = self.core, self.w, self.core.nc
        ps, v = core.psum, self.core.nc.vector
        layer_norms(core, core.x, core.xn, self.normed)
        pr, tmp, r1 = self.probs, self.tmp, self.r1

        def per_tile(a):
            return a.unsqueeze(2).to_broadcast([P, T, NE])

        gate_b = self.ew.gate_b[:, :].unsqueeze(1).to_broadcast([P, T, NE])
        ids = w.expert_ids[:, :].unsqueeze(1).to_broadcast([P, T, NE])
        dve.wait_ge(self.ew.small_in, self.ew.small_all)
        core.result(dve, self.logits)
        v.tensor_tensor(pr, ps[:, self.logits.bank, 0:T * NE].rearrange("p (t e) -> p t e", e=NE), gate_b,
                        ALU.add).then_inc(core.emptied[self.logits.bank], 1)
        core.moved(dve, self.logits)
        core.vstep(v.tensor_reduce(r1, pr, AX.X, ALU.max))
        v.tensor_tensor(pr, pr, per_tile(r1), ALU.subtract).then_inc(self.shifted, 1)
        dve.wait_ge(self.exps, 1)
        core.vstep(v.tensor_reduce(r1, pr, AX.X, ALU.add))
        core.vstep(v.reciprocal(r1, r1))
        core.vstep(v.tensor_tensor(pr, pr, per_tile(r1), ALU.mult))
        for k in range(self.top):
            best, hot = self.top_p[:, k, :], self.hot[:, k, :, :]
            core.vstep(v.tensor_reduce(best, pr, AX.X, ALU.max))
            core.vstep(v.tensor_tensor(tmp, pr, per_tile(best), ALU.is_equal))
            core.vstep(v.tensor_tensor(tmp, tmp, ids, ALU.mult))
            core.vstep(v.tensor_reduce(r1, tmp, AX.X, ALU.min))
            core.vstep(v.tensor_tensor(hot, per_tile(r1), ids, ALU.is_equal))
            if k + 1 < self.top:
                core.vstep(v.scalar_tensor_tensor(out=pr, in0=hot, scalar=-2.0, in1=pr, op0=ALU.mult, op1=ALU.add))
        if self.top == 2:
            v.tensor_tensor(self.both, self.hot[:, 0, :, :], self.hot[:, 1, :, :], ALU.add).then_inc(self.chosen, 1)
            core.vstep(v.tensor_tensor(r1, self.top_p[:, 0, :], self.top_p[:, 1, :], ALU.add))
            core.vstep(v.reciprocal(r1, r1))
            core.vstep(v.tensor_tensor(self.top_p, self.top_p, r1.unsqueeze(1).to_broadcast([P, 2, T]), ALU.mult))
        else:
            v.tensor_copy(self.both, self.hot[:, 0, :, :]).then_inc(self.chosen, 1)
        totals = ps[:, self.ranks.bank, P:2 * P].rearrange("p (t e) -> p e t", e=NE)
        ranks = ps[:, self.ranks.bank, 0:P].rearrange("p (t e) -> p t e", e=NE)
        cnt = self.cnt
        core.result(dve, self.ranks)
        core.vstep(v.tensor_copy(self.tot, totals))
        flat = "p e t -> p (e t)"
        core.vstep(v.tensor_tensor_scan(self.incl.rearrange(flat), w.not_first[:, :], self.tot.rearrange(flat), 0.0,
                                        ALU.mult, ALU.add))
        core.vstep(v.tensor_scalar(self.cnt_i, self.incl[:, :, T - 1], float(P - 1), None, ALU.add))
        core.vstep(v.tensor_scalar(self.cnt_i, self.cnt_i, 7, 7, ALU.logical_shift_right, ALU.logical_shift_left))
        core.vstep(v.tensor_copy(cnt[:, 0, :], self.cnt_i))
        core.vstep(v.tensor_tensor_scan(cnt[:, 1, :], w.ones[:, 0:NE], cnt[:, 0, :], 0.0, ALU.mult, ALU.add))
        core.vstep(v.tensor_tensor(cnt[:, 2, :], cnt[:, 1, :], cnt[:, 0, :], ALU.subtract))
        core.vstep(v.tensor_tensor(self.incl, self.incl, self.tot, ALU.subtract))
        core.vstep(v.tensor_tensor(self.incl, self.incl, cnt[:, 2, :].unsqueeze(2).to_broadcast([P, NE, T]), ALU.add))
        v.tensor_tensor(self.pos, ranks, self.incl.rearrange("p e t -> p t e"),
                        ALU.add).then_inc(core.emptied[self.ranks.bank], 1)
        core.moved(dve, self.ranks)
        for k in range(self.top):
            core.vstep(v.tensor_tensor(tmp, self.hot[:, k, :, :], self.pos, ALU.mult))
            core.vstep(v.tensor_reduce(self.slot[:, k, :], tmp, AX.X, ALU.add))
        n, choices = self.tiles, self.top * T
        slot = self.slot.rearrange("p k t -> p (k t)")
        core.vstep(v.tensor_copy(self.slot_int[:, 0, :], slot))
        core.vstep(v.tensor_scalar(self.slot_int[:, 1, :], self.slot_int[:, 0, :], 7, None, ALU.logical_shift_right))
        core.vstep(v.tensor_copy(self.slot_tile, self.slot_int[:, 1, :]))
        core.vstep(v.scalar_tensor_tensor(out=self.slot_row, in0=self.slot_tile, scalar=float(-P), in1=slot,
                                          op0=ALU.mult, op1=ALU.add))
        v.tensor_tensor(self.tile_hot[:, :, 2, :], w.counting[:, 0:n].unsqueeze(1).to_broadcast([P, choices, n]),
                        self.per_choice(self.slot_tile, n), ALU.is_equal).then_inc(self.in_tile, 1)
        dve.wait_ge(self.in_tile, 1)
        v.tensor_tensor(self.tile_hot[:, :, 0, :], self.tile_hot[:, :, 2, :],
                        self.per_choice(w.choice_ids[:, 0:self.top, :].rearrange("p k t -> p (k t)"), n),
                        ALU.mult).then_inc(self.in_tile, 1)
        for g in range(4):
            part = slice(g * choices // 4, (g + 1) * choices // 4)
            shape = [P, choices // 4, P]
            v.tensor_tensor(self.row_hot[:, part, :], w.counting[:, :].unsqueeze(1).to_broadcast(shape),
                            self.slot_row[:, part].unsqueeze(2).to_broadcast(shape), ALU.is_equal).then_inc(self.in_row, 1)
        over, off = self.over[0:1, 0:n, :], self.tile_w[0:1, 0:n]
        core.vstep(v.tensor_tensor(over, w.tile_starts[0:1, 0:n].unsqueeze(2).to_broadcast([1, n, NE]),
                                   cnt[0:1, 1, :].unsqueeze(1).to_broadcast([1, n, NE]), ALU.is_ge))
        core.vstep(v.tensor_reduce(off, over, AX.X, ALU.add))
        core.vstep(v.tensor_scalar(off, off, float(NE - 1), None, ALU.min))
        for i, size in enumerate((FF, FC)):
            v.tensor_scalar(self.tile_at[0:1, i, 0:n], off, float(size), None, ALU.mult).then_inc(self.tables_in, 1)
        if self.fresh:
            self.ew.split_w1(v, 0)
        core.result(dve, self.inverse)
        v.tensor_copy(self.places, ps[:, self.inverse.bank, 0:3 * n].rearrange("p (i j) -> p i j", i=3)
                      ).then_inc(core.emptied[self.inverse.bank], 1)
        core.moved(dve, self.inverse)
        choice, there, own = self.places[:, 0, :], self.places[:, 2, :], self.padding_row
        core.vmark(v.tensor_copy(self.place_int[:, 0, :], choice))
        core.vstep(v.tensor_tensor(own, there, w.padding_rows[:, 0:n], ALU.mult))
        core.vmark(v.tensor_scalar(self.place_int[:, 0, :], self.place_int[:, 0, :], N - 1, None, ALU.bitwise_and))
        core.vstep(v.tensor_tensor(own, w.padding_rows[:, 0:n], own, ALU.subtract))
        core.vsync()
        v.tensor_tensor(self.place_int[:, 1, :], choice, own, ALU.add).then_inc(self.places_in, 1)
        if self.meanwhile:
            self.meanwhile.vector(dve)

        def step(s, p, m):
            def live(lag):
                return s is None or 0 <= s - lag < self.tiles
            q = 1 - p
            mq = m - q
            if live(0):
                if s is None or s >= 2:
                    self.used_before(dve, 1, p, m)
                self.result(dve, 0, p, m)
                v.tensor_copy(self.xgT[:, p, :, :].rearrange("p k t -> p (k t)"),
                              ps[:, p, 0:P].bitcast(F16)).then_inc(core.emptied[p], 1)
            if live(3):
                tile = 2 * (mq - 1) + q
                which = slice(tile, tile + 1) if s is not None else bass.ds(tile, 1)
                self.result(dve, 2, q, mq - 1)
                v.tensor_tensor(self.y[:, which, :], ps[:, 4 + q:5 + q, 0:D],
                                self.places[:, 1:2, which].rearrange("p o s -> p s o").to_broadcast([P, 1, D]), ALU.mult
                                ).then_inc(core.emptied[4 + q], 1)

        self.over_tiles(dve, step, 3)
        for g in range(4):
            ts = slice(4 * g, 4 * g + 4)
            dve.wait_ge(w.back[g], self.back_before + 16 * self.top)
            for k in range(self.top):
                core.vstep(v.tensor_tensor(core.x[:, ts, :], core.x[:, ts, :], self.yg[:, k, ts, :], ALU.add))


class SoftmaxAttention:

    SHIFT = 256.0

    def __init__(self, core, w):
        self.core, self.w = core, w
        s = core.sem
        self.normed = s("sa_normed")
        self.high_in = s("sa_high")
        self.again_in = s("sa_again")
        self.split_in = s("sa_split")
        self.pads = s("sa_pads")
        self.cleared = s("sa_cleared")
        self.masked_q = [s(f"sa_masked_q{i}") for i in range(2)]
        self.masked_k = [s(f"sa_masked_k{i}") for i in range(2)]
        self.ring_in = s("sa_ring_in")
        self.ring_out = s("sa_ring_out")
        self.max_in = s("sa_max_in")
        self.score_in = s("sa_score_in")
        self.prob_in = s("sa_prob_in")
        self.wave_in = s("sa_wave_in")
        self.sum_out = s("sa_sum_out")
        self.value_in = s("sa_value_in")
        self.att_in = s("sa_att")
        self.bias_in = s("sa_bias")
        self.x_in = s("sa_x")
        self.ln2 = s("sa_ln2")
        c, at = carve, 0
        self.qT, at = c(core, at, [NG, N], F16)
        self.kT, at = c(core, at, [NG, N], F16)
        self.qM, at = c(core, at, [2, HG, S], F16)
        self.kM, mid = c(core, at, [2, HG, S], F16)
        self.qs, _ = c(core, at, [T, H, 32], F16)
        self.prob, _ = c(core, mid, [2, HG, 512])
        self.ks, at = c(core, mid, [T, H, 32], F16)
        self.v, at = c(core, at, [T, D])
        self.vs, at = c(core, at, [2, TB, HG, 32])
        self.qT2, at = c(core, at, [2, S], F16)
        self.m4, at = c(core, at, [TB, P], F16)
        self.mx, at = c(core, at, [TB, HG])
        self.n1, _ = c(core, 0, [T, D])
        ew = core.expert_w
        self.qk = ew[:, 0:T * 256].rearrange("p (t c) -> p t c", t=T)
        self.rot = ew[:, T * 256:2 * T * 256].rearrange("p (t c) -> p t c", t=T)
        self.rtmp, _ = c(core, at, [2, TB * 2 * H * HD // 2])
        self.oT = ew[:, :].rearrange("p (g n) -> p g n", g=NG)
        at = 0
        self.att, at = c(core, at, [T, D])
        self.attT, at = c(core, at, [N])
        self.n2, at = c(core, at, [T, D])
        self.hid, at = c(core, at, [FC, N])
        self.den, at = c(core, at, [2, H])
        self.t = []
        for b in range(B):
            self.t.append({"xT": core.turns(2), "qkv": core.turns(8)})
        for b in range(B):
            self.t[b]["qkT"] = core.turns(8)
        self.before_units = list(core.uses)
        self.o_turns = core.turns(T)
        for b in range(B):
            self.t[b].update(attT=core.turns(2), wo=core.turns(2))
        for b in range(B):
            self.t[b].update(x2T=core.turns(2), up=core.turns(8), down=core.turns(2))

    RING = 34

    @staticmethod
    def ring_use(a):
        half, k = divmod(a, 17)
        return ("turn", half, 0) if k == 16 else ("max", 4 * half + k // 4, k % 4)

    def ring_fill(self, pe, a, g, b, m, second=False):
        core, nc = self.core, self.core.nc
        slot = a % 2
        kind, qt, j = self.ring_use(a)
        if not second:
            first_of_all = isinstance(m, int) and m == 0 and b == 0 and a < 2
            if not first_of_all:
                pe.wait_ge(self.ring_out, m * (2 * self.RING) + (b * self.RING + a - 1))
        if kind == "turn":
            pe.wait_ge(self.max_in, m * 4 + (2 * b + qt + 1))
            out = core.psum[:, 2 * slot, 0:256].bitcast(F16)
            for i in range(4):
                last = nc.tensor.transpose(out[:, i * P:(i + 1) * P], self.m4[:, 4 * qt + i, :], self.w.ident16[:, :])
            last.then_inc(self.ring_in, 1)
            return
        half = int(second)
        at = g * N + (b * S + 512 * half)
        keys = self.kT.rearrange("p g n -> p (g n)")
        keys = keys[:, at:at + 512] if isinstance(g, int) else keys[:, bass.ds(at, 512)]
        last = nc.tensor.matmul(core.psum[:, 2 * slot + half, :], self.qM[:, b, j, qt * P:(qt + 1) * P], keys,
                                start=True, stop=True)
        if second:
            last.then_inc(self.ring_in, 1)

    def ring_read(self, dve, a, g, b, m):
        core, v = self.core, self.core.nc.vector
        slot = a % 2
        kind, qt, j = self.ring_use(a)
        dve.wait_ge(self.ring_in, m * (2 * self.RING) + (b * self.RING + a + 1))
        if kind == "max":
            v.reduce_max(self.mx[:, qt, j:j + 1], core.psum[:, 2 * slot:2 * slot + 2, :].rearrange("p a n -> p (a n)"),
                         AX.X).then_inc(self.ring_out, 1)
            if a % 17 == 15:
                half = a // 17
                dve.wait_ge(self.ring_out, m * (2 * self.RING) + (b * self.RING + a + 1))
                rows = self.m4[:, 4 * half:4 * half + 4, :].rearrange("p t (j r) -> p t j r", r=32)[:, :, :, 24]
                v.tensor_scalar(rows, self.mx[:, 4 * half:4 * half + 4, :], -1.0 / self.SHIFT, None,
                                ALU.mult).then_inc(self.max_in, 1)
        else:
            at = g * N + (b * S + 512 * qt)
            queries = self.qT.rearrange("p g n -> p (g n)")
            queries = queries[:, at:at + 512] if isinstance(g, int) else queries[:, bass.ds(at, 512)]
            v.tensor_tensor(self.qT2[:, b, 512 * qt:512 * (qt + 1)], queries,
                            core.psum[:, 2 * slot, 0:256].bitcast(F16), ALU.add).then_inc(self.ring_out, 1)

    def move_sum(self, dve, half, g, b, m):
        dve.wait_ge(self.wave_in, m * 32 + (16 * b + 8 * half + 8))
        at = g * N + (b * S + 512 * half)
        out = self.oT.rearrange("p g n -> p (g n)")
        out = out[:, at:at + 512] if isinstance(g, int) else out[:, bass.ds(at, 512)]
        self.core.nc.vector.tensor_copy(out, self.core.psum[:, 6 + half, :]).then_inc(self.sum_out, 1)

    def wave(self, pe, k, g, b, m):
        core, nc = self.core, self.core.nc
        half, kt = divmod(k, 8)
        pe.wait_ge(self.prob_in, m * 128 + (64 * b + 4 * k + 4))
        if kt == 0 and not (isinstance(m, int) and m == 0 and b == 0):
            pe.wait_ge(self.sum_out, m * 4 + (2 * b + half - 1))
        for j in range(HG):
            last = nc.tensor.matmul(core.psum[32 * j:32 * j + 32, 6 + half, :], self.vs[:, b, kt, j, :],
                                    self.prob[:, k % 2, j, :], start=(kt == 0), stop=(kt == TB - 1))
        last.then_inc(self.wave_in, 1)

    def unit_tensor(self, pe, b, m, following=True):
        core, nc = self.core, self.core.nc
        nb, nm = 1 - b, m + b
        plan = list(range(self.RING)) if following else []
        pe.wait_ge(self.masked_k[b], 64 * m + 64)
        pe.wait_ge(self.value_in, m * 2 + (b + 1))
        if following:
            pe.wait_ge(self.masked_q[nb], 64 * nm + 64)
        for k in range(16):
            half, kt = divmod(k, 8)
            if kt == 0:
                pe.wait_ge(self.ring_out, m * (2 * self.RING) + (b * self.RING + 17 * (half + 1)))
            parts = []
            for _ in range(3 if k in (4, 12) else 2):
                if plan:
                    a = plan.pop(0)
                    parts.append((a, False))
                    if self.ring_use(a)[0] == "max":
                        parts.append((a, True))
            for j in range(HG):
                tile = 64 * b + 4 * k + j
                if not (isinstance(m, int) and m == 0 and tile < 2):
                    pe.wait_ge(self.prob_in, m * 128 + (tile - 1))
                nc.tensor.matmul(core.psum[:, 4 + j % 2, :], self.kM[:, b, j, kt * P:(kt + 1) * P],
                                 self.qT2[:, b, 512 * half:512 * (half + 1)], start=True,
                                 stop=True).then_inc(self.score_in, 1)
                take = (len(parts) + HG - 1 - j) // (HG - j)
                for _ in range(take):
                    a, second = parts.pop(0)
                    self.ring_fill(pe, a, nm, nb, nm, second)
            if k > 0:
                self.wave(pe, k - 1, m, b, m)
        self.wave(pe, 15, m, b, m)

    def unit_vector(self, dve, b, m, following=True):
        nb, nm = 1 - b, m + b
        for a in range(self.RING if following else 0):
            self.ring_read(dve, a, nm, nb, nm)
            if a == 3 and not (isinstance(m, int) and m == 0 and b == 0):
                self.move_sum(dve, 1, m - (1 - b), nb, m - (1 - b))
            if a == 20:
                self.move_sum(dve, 0, m, b, m)
        if not following:
            self.move_sum(dve, 1, m - (1 - b), nb, m - (1 - b))
            self.move_sum(dve, 0, m, b, m)
            self.move_sum(dve, 1, m, b, m)

    def unit_scalar(self, act, b, m):
        core, nc = self.core, self.core.nc
        for k in range(16):
            if not (isinstance(m, int) and m == 0 and b == 0 and k < 2):
                act.wait_ge(self.wave_in, m * 32 + (16 * b + k - 1))
            for j in range(HG):
                act.wait_ge(self.score_in, m * 128 + (64 * b + 4 * k + j + 1))
                nc.scalar.activation(self.prob[:, k % 2, j, :], core.psum[:, 4 + j % 2, :],
                                     ACT.Exp).then_inc(self.prob_in, 1)

    def tensor(self, pe):
        core, w, nc = self.core, self.w, self.core.nc
        ps = core.psum
        pe.wait_ge(w.sa_in, w.sa_all)
        for b in range(B):
            pe.wait_ge(self.normed, b + 1)
            for g, turn in enumerate(self.t[b]["xT"]):
                transpose_tiles(core, pe, turn, [self.n1[:, b * TB + 4 * g + i, :] for i in range(4)], w.ident[:, :])
            for i, turn in enumerate(self.t[b]["qkv"]):
                core.claim(pe, turn)
                core.moved(pe, self.t[b]["xT"][i // 4])
                nc.tensor.matmul(ps[:, turn.bank, 0:384], core.xnT[:, b, 1 + i * P:1 + (i + 1) * P],
                                 w.sa_wqkv[:, :], start=True, stop=True).then_inc(core.filled[turn.bank], 1)
        pe.wait_ge(self.pads, 2)
        pe.wait_ge(w.ident16_in, 1)
        for b in range(B):
            pe.wait_ge(self.again_in, b + 1)
            pe.wait_ge(self.split_in, b + 1)
            for i, turn in enumerate(self.t[b]["qkT"]):
                parts, g = (self.qs, self.ks)[i // NG], i % NG
                core.claim(pe, turn)
                out = ps[:, turn.bank, :].bitcast(F16)
                for t in range(TB):
                    last = nc.tensor.transpose(
                        out[:, t * P:(t + 1) * P],
                        parts[:, b * TB + t, HG * g:HG * g + HG, :].rearrange("p j r -> p (j r)"), w.ident16[:, :])
                last.then_inc(core.filled[turn.bank], 1)
        for i in range(8):
            pe.wait_ge(core.emptied[i], self.before_units[i])
        pe.wait_ge(self.masked_q[0], 64)
        for a in range(self.RING):
            self.ring_fill(pe, a, 0, 0, 0)
            if self.ring_use(a)[0] == "max":
                self.ring_fill(pe, a, 0, 0, 0, second=True)
        for b in range(B):
            self.unit_tensor(pe, b, 0)
        with pe.Fori(1, NG - 1) as g:
            for b in range(B):
                self.unit_tensor(pe, b, g)
        self.unit_tensor(pe, 0, NG - 1)
        self.unit_tensor(pe, 1, NG - 1, following=False)
        pe.wait_ge(self.sum_out, 2 * B * NG)
        for t, turn in enumerate(self.o_turns):
            transpose_tiles(core, pe, turn, [self.oT[:, g, t * P:(t + 1) * P] for g in range(NG)], w.ident[:, :])
        for b in range(B):
            tb = self.t[b]
            for g, turn in enumerate(tb["attT"]):
                t = b * TB + 4 * g
                for i in range(4):
                    core.moved(pe, self.o_turns[t + i])
                transpose_tiles(core, pe, turn, [self.att[:, t + i, :] for i in range(4)], w.ident[:, :])
            for g, turn in enumerate(tb["wo"]):
                core.claim(pe, turn)
                core.moved(pe, tb["attT"][g])
                for i in range(4):
                    t = b * TB + 4 * g + i
                    last = nc.tensor.matmul(ps[:, turn.bank, i * D:(i + 1) * D], self.attT[:, t * P:(t + 1) * P],
                                            w.sa_wo[:, :], start=True, stop=True)
                last.then_inc(core.filled[turn.bank], 1)
        for b in range(B):
            tb = self.t[b]
            pe.wait_ge(self.ln2, b + 1)
            for g, turn in enumerate(tb["x2T"]):
                transpose_tiles(core, pe, turn, [self.n2[:, b * TB + 4 * g + i, :] for i in range(4)], w.ident[:, :])
            for i, turn in enumerate(tb["up"]):
                c, half = i % FC, i // FC
                core.claim(pe, turn)
                core.moved(pe, tb["x2T"][half])
                nc.tensor.matmul(ps[:, turn.bank, :], w.sa_w1[:, c * P:(c + 1) * P],
                                 core.xnT[:, b, 1 + 512 * half:1 + 512 * (half + 1)],
                                 start=True, stop=True).then_inc(core.filled[turn.bank], 1)
            for g, turn in enumerate(tb["down"]):
                core.claim(pe, turn)
                for c in range(FC):
                    core.moved(pe, tb["up"][FC * g + c])
                for i in range(4):
                    t = b * TB + 4 * g + i
                    for c in range(FC):
                        last = nc.tensor.matmul(ps[:, turn.bank, i * D:(i + 1) * D], self.hid[:, c, t * P:(t + 1) * P],
                                                w.sa_w2[:, c, :], start=(c == 0), stop=(c == FC - 1))
                last.then_inc(core.filled[turn.bank], 1)

    def scalar(self, act):
        core, w, nc = self.core, self.w, self.core.nc
        ps = core.psum
        for b in range(B):
            deviation(core, b)
            deviation(core, b, var=5, root=6)
        act.wait_ge(w.sa_in, w.sa_all)
        for b in range(B):
            for g, turn in enumerate(self.t[b]["xT"]):
                core.result(act, turn)
                nc.scalar.activation(core.xnT[:, b, 1 + 512 * g:1 + 512 * (g + 1)], ps[:, turn.bank, :], ACT.Identity,
                                     scale=w.sa_affine[:, 0:1], bias=w.sa_affine[:, 1:2]
                                     ).then_inc(core.emptied[turn.bank], 1)
        for b in range(B):
            tiles = slice(b * TB, (b + 1) * TB)
            act.wait_ge(self.high_in, b + 1)
            nc.scalar.copy(self.qs[:, tiles, :, 8:16], self.qs[:, tiles, :, 0:8])
            nc.scalar.copy(self.ks[:, tiles, :, 16:24], self.ks[:, tiles, :, 0:8]).then_inc(self.again_in, 1)
            for i, turn in enumerate(self.t[b]["qkT"]):
                parts, g = (self.qT, self.kT)[i // NG], i % NG
                core.result(act, turn)
                nc.scalar.copy(parts[:, g, b * S:(b + 1) * S],
                               ps[:, turn.bank, :].bitcast(F16)).then_inc(core.emptied[turn.bank], 1)
        for b in range(B):
            self.unit_scalar(act, b, 0)
        with act.Fori(1, NG) as g:
            for b in range(B):
                self.unit_scalar(act, b, g)
        for b in range(B):
            for g, turn in enumerate(self.t[b]["attT"]):
                at = b * S + 512 * g
                core.result(act, turn)
                nc.scalar.copy(self.attT[:, at:at + 512], ps[:, turn.bank, :]).then_inc(core.emptied[turn.bank], 1)
        for b in range(B):
            deviation(core, b)
        for b in range(B):
            for g, turn in enumerate(self.t[b]["x2T"]):
                core.result(act, turn)
                nc.scalar.activation(core.xnT[:, b, 1 + 512 * g:1 + 512 * (g + 1)], ps[:, turn.bank, :], ACT.Identity,
                                     scale=w.sa_affine[:, 2:3], bias=w.sa_affine[:, 3:4]
                                     ).then_inc(core.emptied[turn.bank], 1)
            for i, turn in enumerate(self.t[b]["up"]):
                c, half = i % FC, i // FC
                at = b * S + 512 * half
                core.result(act, turn)
                nc.scalar.activation(self.hid[:, c, at:at + 512], ps[:, turn.bank, :], ACT.Relu,
                                     bias=w.sa_b1[:, c:c + 1]).then_inc(core.emptied[turn.bank], 1)

    def vector(self, dve):
        core, w, nc = self.core, self.w, self.core.nc
        ps, v = core.psum, self.core.nc.vector
        ln = core.ln
        for b in range(B):
            tiles = slice(b * TB, (b + 1) * TB)
            spread(core, core.x, b)
            inverse_root(core, 4, b)
            core.vstep(v.tensor_tensor(ln[:, 5, tiles], ln[:, 3, tiles], ln[:, 4, tiles], ALU.mult))
            v.tensor_tensor(ln[:, 5, tiles], ln[:, 5, tiles], ln[:, 4, tiles], ALU.mult).then_inc(core.variance, 1)
            inverse_root(core, 6, b)
            core.vstep(v.tensor_tensor(ln[:, 6, tiles], ln[:, 6, tiles], ln[:, 4, tiles], ALU.mult))
            center_and_scale(core, core.x, self.n1, 6, b, self.normed)
        dve.wait_ge(w.sa_in, w.sa_all)
        for b in range(B):
            tiles = slice(b * TB, (b + 1) * TB)
            for i, turn in enumerate(self.t[b]["qkv"]):
                core.result(dve, turn)
                core.vmark(v.tensor_tensor(self.qk[:, b * TB + i, :], ps[:, turn.bank, 0:256], w.sa_bqkv[:, 0:256],
                                           ALU.add))
                v.tensor_tensor(self.v[:, b * TB + i, :], ps[:, turn.bank, 256:384], w.sa_bqkv[:, 256:384],
                                ALU.add).then_inc(core.emptied[turn.bank], 1)
            core.vsync()
            qk = self.qk[:, tiles, :].rearrange("p t (h j e) -> p t h j e", h=2 * H, e=2)
            rot = self.rot[:, tiles, :].rearrange("p t (h j e) -> p t h j e", h=2 * H, e=2)
            cos, sin = (w.rope[:, i, :, :].unsqueeze(2).to_broadcast([P, TB, 2 * H, HD // 2]) for i in range(2))
            ta, tb_ = (self.rtmp[:, i, :].rearrange("p (t h j) -> p t h j", t=TB, h=2 * H) for i in range(2))
            core.vmark(v.tensor_tensor(ta, qk[:, :, :, :, 0], cos, ALU.mult))
            core.vstep(v.tensor_tensor(tb_, qk[:, :, :, :, 1], sin, ALU.mult))
            core.vstep(v.tensor_tensor(rot[:, :, :, :, 0], ta, tb_, ALU.subtract))
            core.vmark(v.tensor_tensor(ta, qk[:, :, :, :, 0], sin, ALU.mult))
            core.vstep(v.tensor_tensor(tb_, qk[:, :, :, :, 1], cos, ALU.mult))
            core.vstep(v.tensor_tensor(rot[:, :, :, :, 1], ta, tb_, ALU.add))
            if b == 0:
                dve.wait_ge(self.pads, 2)
            q = self.rot[:, tiles, 0:D].rearrange("p t (h d) -> p t h d", d=HD)
            k = self.rot[:, tiles, D:2 * D].rearrange("p t (h d) -> p t h d", d=HD)
            qs, ks = self.qs[:, tiles, :, :], self.ks[:, tiles, :, :]
            scale = float(HD) ** -0.5
            core.vmark(v.tensor_scalar(qs[:, :, :, 0:8], q, scale, None, ALU.mult))
            v.tensor_copy(ks[:, :, :, 0:8], k).then_inc(self.high_in, 1)
            core.vsync()
            dve.wait_ge(self.high_in, b + 1)
            for t in range(b * TB, (b + 1) * TB):
                qt = self.rot[:, t, 0:D].rearrange("p (h d) -> p h d", d=HD)
                core.vmark(v.scalar_tensor_tensor(out=self.qs[:, t, :, 16:24], in0=qt, scalar=scale,
                                                  in1=self.qs[:, t, :, 0:8], op0=ALU.mult, op1=ALU.subtract))
            core.vsync()
            v.tensor_tensor(ks[:, :, :, 8:16], k, ks[:, :, :, 0:8], ALU.subtract).then_inc(self.split_in, 1)
        for a in range(self.RING):
            self.ring_read(dve, a, 0, 0, 0)
        for b in range(B):
            self.unit_vector(dve, b, 0)
        with dve.Fori(1, NG - 1) as g:
            for b in range(B):
                self.unit_vector(dve, b, g)
        self.unit_vector(dve, 0, NG - 1)
        self.unit_vector(dve, 1, NG - 1, following=False)
        for t, turn in enumerate(self.o_turns):
            core.result(dve, turn)
            view = ps[:, turn.bank, :].rearrange("p (h r) -> p h r", r=32)
            den = self.den[:, t % 2, :]
            core.vstep(v.reciprocal(den, view[:, :, 8]))
            v.tensor_tensor(self.att[:, t, :].rearrange("p (h d) -> p h d", d=HD), view[:, :, 0:HD],
                            den.unsqueeze(2).to_broadcast([P, H, HD]), ALU.mult).then_inc(core.emptied[turn.bank], 1)
        u = core.xn
        for b in range(B):
            dve.wait_ge(self.bias_in, b + 1)
            for g, turn in enumerate(self.t[b]["wo"]):
                ts = slice(b * TB + 4 * g, b * TB + 4 * g + 4)
                core.result(dve, turn)
                v.tensor_tensor(u[:, ts, :], u[:, ts, :], ps[:, turn.bank, :].rearrange("p (t d) -> p t d", d=D),
                                ALU.add).then_inc(core.emptied[turn.bank], 1)
            for turn in self.t[b]["wo"]:
                core.moved(dve, turn)
            spread(core, u, b)
            inverse_root(core, 4, b)
            center_and_scale(core, u, self.n2, 4, b, self.ln2)
        for b in range(B):
            dve.wait_ge(self.x_in, b + 1)
            for g, turn in enumerate(self.t[b]["down"]):
                xs = core.x[:, b * TB + 4 * g:b * TB + 4 * g + 4, :]
                core.result(dve, turn)
                v.tensor_tensor(xs, xs, ps[:, turn.bank, :].rearrange("p (t d) -> p t d", d=D),
                                ALU.add).then_inc(core.emptied[turn.bank], 1)
        for b in range(B):
            for turn in self.t[b]["down"]:
                core.moved(dve, turn)

    def gpsimd(self, pool):
        core, w, g_ = self.core, self.w, self.core.nc.gpsimd
        pool.wait_ge(self.normed, 1)
        g_.memset(self.qM, 0.0).then_inc(self.cleared, 1)
        g_.memset(self.m4, 0.0).then_inc(self.cleared, 1)
        g_.memset(self.qs[:, :, :, 24:32], 0.0).then_inc(self.pads, 1)
        g_.memset(self.ks[:, :, :, 25:32], 0.0).then_inc(self.cleared, 1)
        g_.memset(self.ks[:, :, :, 24:25], self.SHIFT).then_inc(self.pads, 1)
        g_.memset(self.vs[:, :, :, :, 9:32], 0.0).then_inc(self.cleared, 1)
        g_.memset(self.vs[:, :, :, :, 8:9], 1.0).then_inc(self.cleared, 1)
        for b in range(B):
            ts = slice(b * TB, (b + 1) * TB)
            pool.wait_ge(self.normed, b + 1)
            mean, r = (core.ln[:, i, ts].unsqueeze(2).to_broadcast([P, TB, D]) for i in (0, 4))
            core.pstep(g_.tensor_tensor(core.xn[:, ts, :], core.x[:, ts, :], mean, ALU.subtract))
            core.pstep(g_.tensor_tensor(core.xn[:, ts, :], core.xn[:, ts, :], r, ALU.mult))
        for b in range(B):
            for turn in self.t[b]["qkT"]:
                core.moved(pool, turn)
            g_.memset(self.kM[:, b, :, :], 0.0).then_inc(self.cleared, 1)

        def values(g, b, m):
            if not isinstance(m, int) or m > 0:
                pool.wait_ge(self.wave_in, m * 32 + 16 * (b - 1))
            src = self.v[:, b * TB:(b + 1) * TB, :]
            at = g * (HG * HD)
            src = src[:, :, at:at + HG * HD] if isinstance(g, int) else src[:, :, bass.ds(at, HG * HD)]
            g_.tensor_copy(self.vs[:, b, :, :, 0:HD], src.rearrange("p t (j d) -> p t j d", d=HD)
                           ).then_inc(self.value_in, 1)

        for b in range(B):
            values(0, b, 0)
        with pool.Fori(1, NG) as g:
            for b in range(B):
                values(g, b, g)
        for b in range(B):
            us = core.xn[:, b * TB:(b + 1) * TB, :]
            g_.tensor_tensor(us, us, w.sa_bo[:, :].unsqueeze(1).to_broadcast([P, TB, D]),
                             ALU.add).then_inc(self.bias_in, 1)
        for b in range(B):
            pool.wait_ge(self.ln2, b + 1)
            xs, us = core.x[:, b * TB:(b + 1) * TB, :], core.xn[:, b * TB:(b + 1) * TB, :]
            core.pstep(g_.tensor_tensor(xs, xs, us, ALU.add))
            g_.tensor_tensor(xs, xs, w.sa_b2[:, :].unsqueeze(1).to_broadcast([P, TB, D]),
                             ALU.add).then_inc(self.x_in, 1)

    def sync(self, sp):
        core = self.core

        def masked(src_all, dst, sem, g, b):
            at = g * N + b * S
            src = src_all.rearrange("p g n -> p (g n)")
            for j in range(HG):
                rows = slice(32 * j, 32 * j + 32)
                s = src[rows, at:at + S] if isinstance(g, int) else src[rows, bass.ds(at, S)]
                sp.dma_start(dst[rows, b, j, :], s).then_inc(sem[b], 16)

        def unit(g, b, m):
            if not isinstance(m, int) or m > 0:
                sp.wait_ge(self.ring_in, m * (2 * self.RING) + ((b - 2) * self.RING + 33))
            masked(self.qT, self.qM, self.masked_q, g, b)
            if not isinstance(m, int) or m > 0:
                sp.wait_ge(self.score_in, m * 128 + 64 * (b - 1))
            masked(self.kT, self.kM, self.masked_k, g, b)

        for b in range(B):
            for turn in self.t[b]["qkT"]:
                core.moved(sp, turn)
            sp.wait_ge(self.cleared, 5)
            masked(self.qT, self.qM, self.masked_q, 0, b)
            sp.wait_ge(self.cleared, 6 + b)
            masked(self.kT, self.kM, self.masked_k, 0, b)
        with sp.Fori(1, NG) as g:
            for b in range(B):
                unit(g, b, g)
        for turn in self.o_turns[-8:]:
            core.result(sp, turn)
        self.w.e1.load_w2(sp)


class MemoryWeights:

    def __init__(self, core, w):
        self.core, self.w = core, w
        s, sb = core.sem, core.sb
        self.basisT, self.coeffT = sb("basisT", [64, P]), sb("coeffT", [64, 4, P])
        self.soft = sb("mw_soft", [P, 3, P])
        self.wqkv, self.owT = self.soft, sb("mw_owT", [P, P])
        self.small = sb("mw_small", [P, 2, 3])
        self.powers = sb("mw_powers", [P, 3, P])
        self.within, self.rise = self.powers[:, 0, :], self.powers[:, 1, :]
        self.scal = sb("mw_scal", [P, 8])
        self.loaded = s("mw_loaded")
        self.shifted, self.exps = s("mw_shifted"), s("mw_exps")
        self.normal = s("mw_normal")
        self.abs_in, self.ln_in = s("mw_abs"), s("mw_ln")
        self.lnd_in = s("mw_lnd")
        self.powers_in = s("mw_powers_in")
        self.within_in = s("mw_within_in")

    def take_banks(self):
        self.logits, self.back = self.core.turns(2)

    def load(self, sp):
        a = self.w.a
        for out, src in [(self.basisT[:, :], a["L1_attn_b_basisT"]), (self.coeffT[:, :, :], a["L1_attn_b_coeffT"]),
                         (self.powers[:, :, :], a["c_powers"]), (self.scal[:, 5:6], a["c_to_end"]),
                         (self.scal[:, 0:1], a["L1_attn_b_decay"].partition_broadcast(P)),
                         (self.scal[:, 1:2], a["L1_attn_b_out_scale"].partition_broadcast(P))]:
            sp.dma_start(out, src).then_inc(self.loaded, 16)

    def tensor(self, pe):
        core, nc, ps = self.core, self.core.nc, self.core.psum
        pe.wait_ge(self.loaded, 96)
        core.claim(pe, self.logits)
        for i in range(4):
            last = nc.tensor.matmul(ps[:, self.logits.bank, i * P:(i + 1) * P], self.coeffT[:, i, :], self.basisT[:, :],
                                    start=True, stop=True)
        last.then_inc(core.filled[self.logits.bank], 1)
        pe.wait_ge(self.normal, 1)
        transpose_tiles(core, pe, self.back, [self.soft[:, i, :] for i in range(3)], self.w.ident[:, :])

    def scalar(self, act):
        core, nc = self.core, self.core.nc
        c = self.scal
        act.wait_ge(self.abs_in, 1)
        nc.scalar.activation(c[:, 3:4], c[:, 2:3], ACT.Exp, scale=-1.0).then_inc(self.ln_in, 1)
        act.wait_ge(self.ln_in, 1)
        nc.scalar.activation(c[:, 3:4], c[:, 3:4], ACT.Ln, bias=self.w.ones[:, 0:1]).then_inc(self.ln_in, 1)
        act.wait_ge(self.shifted, 1)
        nc.scalar.activation(self.soft[:, :, :], self.soft[:, :, :], ACT.Exp).then_inc(self.exps, 1)
        act.wait_ge(self.lnd_in, 1)
        lnd = c[:, 4:5]
        nc.scalar.activation(self.within, self.powers[:, 0, :], ACT.Exp, scale=lnd).then_inc(self.powers_in, 1)
        nc.scalar.activation(self.rise, self.powers[:, 1, :], ACT.Exp, scale=lnd).then_inc(self.powers_in, 1)
        nc.scalar.activation(c[:, 6:7], c[:, 5:6], ACT.Exp, scale=lnd).then_inc(self.powers_in, 1)
        nc.scalar.activation(c[:, 7:8], lnd, ACT.Exp, scale=float(P)).then_inc(self.powers_in, 1)
        core.result(act, self.back)
        nc.scalar.copy(self.wqkv[:, :, :], core.psum[:, self.back.bank, 0:3 * P].rearrange("p (i c) -> p i c", i=3)
                       ).then_inc(core.emptied[self.back.bank], 1)

    def vector(self, dve):
        core, v = self.core, self.core.nc.vector
        c = self.scal
        dve.wait_ge(self.loaded, 96)
        core.vstep(v.tensor_scalar(c[:, 2:3], c[:, 0:1], -1.0, None, ALU.mult))
        v.tensor_tensor(c[:, 2:3], c[:, 2:3], c[:, 0:1], ALU.max).then_inc(self.abs_in, 1)
        dve.wait_ge(self.ln_in, 2)
        v.scalar_tensor_tensor(out=c[:, 4:5], in0=c[:, 0:1], scalar=0.0, in1=c[:, 3:4], op0=ALU.min,
                               op1=ALU.subtract).then_inc(self.lnd_in, 1)
        core.result(dve, self.logits)
        view = core.psum[:, self.logits.bank, :].rearrange("p (i c) -> p i c", i=4)
        top, total = self.small[:, 0, :], self.small[:, 1, :]
        core.vstep(v.tensor_reduce(top, view[:, 0:3, :], AX.X, ALU.max))
        core.vmark(v.tensor_copy(self.owT[:, :], view[:, 3, :]))
        v.tensor_tensor(self.soft[:, :, :], view[:, 0:3, :], top.unsqueeze(2).to_broadcast([P, 3, P]),
                        ALU.subtract).then_inc(core.emptied[self.logits.bank], 1)
        core.moved(dve, self.logits)
        dve.engine_nop().then_inc(self.shifted, 1)
        dve.wait_ge(self.exps, 1)
        core.vstep(v.tensor_reduce(total, self.soft[:, :, :], AX.X, ALU.add))
        core.vstep(v.reciprocal(total, total))
        v.tensor_tensor(self.soft[:, :, :], self.soft[:, :, :], total.unsqueeze(2).to_broadcast([P, 3, P]),
                        ALU.mult).then_inc(self.normal, 1)
        dve.wait_ge(self.powers_in, 4)
        v.tensor_tensor(self.within, self.within, self.powers[:, 2, :], ALU.mult).then_inc(self.within_in, 1)


class LinearMemory:

    def __init__(self, core, w, mw):
        self.core, self.w, self.mw = core, w, mw
        s = core.sem
        self.normed = s("lm_normed")
        self.qd_in = s("lm_qd")
        self.state_in = s("lm_state")
        c, at = carve, 0
        self.qT, at = c(core, at, [B, S])
        self.kT, at = c(core, at, [B, S])
        self.qd, at = c(core, at, [B, S])
        self.rT, at = c(core, at, [B, S])
        self.kd, at = c(core, at, [T, P])
        self.v, at = c(core, at, [T, P])
        self.att, at = c(core, at, [T, P])
        self.state, at = c(core, at, [B, TB, P])
        self.t = []
        for b in range(B):
            self.t.append({"xT": core.turns(2), "qT": core.turns(2), "kT": core.turns(2), "kv": core.turns(4)})
        for b in range(B):
            self.t[b].update(grow=core.turns(2), att=core.turns(2))
        for b in range(B):
            self.t[b].update(rT=core.turns(2), out=core.turns(2))

    def tensor(self, pe):
        core, nc, ps, mw = self.core, self.core.nc, self.core.psum, self.mw
        core.moved(pe, mw.back)
        for b in range(B):
            tb = self.t[b]
            pe.wait_ge(self.normed, b + 1)
            for g, turn in enumerate(tb["xT"]):
                transpose_tiles(core, pe, turn, [core.xn[:, b * TB + 4 * g + i, :] for i in range(4)], self.w.ident[:, :])
            for i, name in enumerate(("qT", "kT")):
                for g, turn in enumerate(tb[name]):
                    core.claim(pe, turn)
                    core.moved(pe, tb["xT"][g])
                    nc.tensor.matmul(ps[:, turn.bank, :], mw.wqkv[:, i, :],
                                     core.xnT[:, b, 1 + 512 * g:1 + 512 * (g + 1)],
                                     start=True, stop=True).then_inc(core.filled[turn.bank], 1)
            for r, turn in enumerate(tb["kv"]):
                core.claim(pe, turn)
                for j in range(2):
                    i = 2 * r + j
                    last = nc.tensor.matmul(ps[:, turn.bank, j * 256:(j + 1) * 256],
                                            core.xnT[:, b, 1 + i * P:1 + (i + 1) * P], mw.wqkv[:, 1:3, :],
                                            start=True, stop=True)
                last.then_inc(core.filled[turn.bank], 1)
        for b in range(B):
            tb = self.t[b]
            for g, turn in enumerate(tb["grow"]):
                core.claim(pe, turn)
                for i in range(4 - g):
                    core.moved(pe, tb["kv"][(4 * g + i) // 2])
                    t = b * TB + 4 * g + i
                    last = nc.tensor.matmul(ps[:, turn.bank, i * P:(i + 1) * P], self.kd[:, t, :], self.v[:, t, :],
                                            start=True, stop=True)
                last.then_inc(core.filled[turn.bank], 1)
            for g, turn in enumerate(tb["att"]):
                core.claim(pe, turn)
                core.moved(pe, tb["qT"][g])
                core.moved(pe, tb["kT"][g])
                for i in range(4):
                    at = (4 * g + i) * P
                    last = nc.tensor.matmul(ps[:, turn.bank, i * P:(i + 1) * P], self.kT[:, b, at:at + P],
                                            self.qT[:, b, at:at + P], start=True, stop=True)
                last.then_inc(core.filled[turn.bank], 1)
        for b in range(B):
            tb = self.t[b]
            for g, turn in enumerate(tb["rT"]):
                core.claim(pe, turn)
                core.moved(pe, tb["att"][g])
                for i in range(4):
                    n, t = 4 * g + i, b * TB + 4 * g + i
                    out = ps[:, turn.bank, i * P:(i + 1) * P]
                    last = nc.tensor.matmul(out, self.v[:, t, :], self.att[:, t, :], start=True, stop=(n == 0))
                    if n:
                        pe.wait_ge(self.state_in, (TB - 1) * b + n)
                        pe.wait_ge(self.qd_in, 2 * b + g + 1)
                        last = nc.tensor.matmul(out, self.state[:, b, n, :], self.qd[:, b, n * P:(n + 1) * P],
                                                start=False, stop=True)
                last.then_inc(core.filled[turn.bank], 1)
            for g, turn in enumerate(tb["out"]):
                core.claim(pe, turn)
                core.moved(pe, tb["rT"][g])
                for i in range(4):
                    at = (4 * g + i) * P
                    last = nc.tensor.matmul(ps[:, turn.bank, i * P:(i + 1) * P], self.rT[:, b, at:at + P],
                                            mw.owT[:, :], start=True, stop=True)
                last.then_inc(core.filled[turn.bank], 1)

    def scalar(self, act):
        core, nc, ps = self.core, self.core.nc, self.core.psum
        for b in range(B):
            deviation(core, b)
        for b in range(B):
            for name, to in (("xT", None), ("qT", self.qT), ("kT", self.kT)):
                for g, turn in enumerate(self.t[b][name]):
                    out = (core.xnT[:, b, 1 + 512 * g:1 + 512 * (g + 1)] if to is None
                           else to[:, b, 512 * g:512 * (g + 1)])
                    core.result(act, turn)
                    nc.scalar.copy(out, ps[:, turn.bank, :]).then_inc(core.emptied[turn.bank], 1)
        for b in range(B):
            for g, turn in enumerate(self.t[b]["rT"]):
                core.result(act, turn)
                nc.scalar.copy(self.rT[:, b, 512 * g:512 * (g + 1)],
                               ps[:, turn.bank, :]).then_inc(core.emptied[turn.bank], 1)

    def gpsimd(self, pool):
        core, mw = self.core, self.mw
        pool.wait_ge(mw.powers_in, 4)
        rise = mw.rise.unsqueeze(1).to_broadcast([P, 4, P])
        for b in range(B):
            for g, turn in enumerate(self.t[b]["qT"]):
                core.moved(pool, turn)
                view = "p (i t) -> p i t"
                core.nc.gpsimd.tensor_tensor(self.qd[:, b, 512 * g:512 * (g + 1)].rearrange(view, i=4),
                                             self.qT[:, b, 512 * g:512 * (g + 1)].rearrange(view, i=4), rise,
                                             ALU.mult).then_inc(self.qd_in, 1)

    def vector(self, dve):
        core, mw, ps, v = self.core, self.mw, self.core.psum, self.core.nc.vector
        layer_norms(core, core.x, core.xn, self.normed)
        to_end, whole = mw.scal[:, 6:7], mw.scal[:, 7:8]
        for b in range(B):
            for r, turn in enumerate(self.t[b]["kv"]):
                ts = slice(b * TB + 2 * r, b * TB + 2 * r + 2)
                core.result(dve, turn)
                view = ps[:, turn.bank, :].rearrange("p (j c) -> p j c", j=2)
                core.vmark(v.tensor_scalar(self.kd[:, ts, :], view[:, :, 0:P], to_end, None, ALU.mult))
                v.tensor_copy(self.v[:, ts, :], view[:, :, P:2 * P]).then_inc(core.emptied[turn.bank], 1)
        within = mw.within.unsqueeze(1).to_broadcast([P, 4, P])
        core.vsync()
        for b in range(B):
            for g, turn in enumerate(self.t[b]["grow"]):
                core.result(dve, turn)
                for i in range(4 - g):
                    n = 4 * g + i
                    grow = ps[:, turn.bank, i * P:(i + 1) * P]
                    if n == 0:
                        v.tensor_copy(self.state[:, b, 1, :], grow).then_inc(self.state_in, 1)
                    else:
                        dve.wait_ge(self.state_in, (TB - 1) * b + n)
                        v.scalar_tensor_tensor(out=self.state[:, b, n + 1, :], in0=self.state[:, b, n, :],
                                               scalar=whole, in1=grow, op0=ALU.mult,
                                               op1=ALU.add).then_inc(self.state_in, 1)
                dve.wait_ge(self.state_in, (TB - 1) * b + 4 * g + 4 - g)
                dve.engine_nop().then_inc(core.emptied[turn.bank], 1)
            for g, turn in enumerate(self.t[b]["att"]):
                ts = slice(b * TB + 4 * g, b * TB + 4 * g + 4)
                core.result(dve, turn)
                v.tensor_tensor(self.att[:, ts, :], ps[:, turn.bank, :].rearrange("p (i t) -> p i t", i=4), within,
                                ALU.mult).then_inc(core.emptied[turn.bank], 1)
        for b in range(B):
            for g, turn in enumerate(self.t[b]["out"]):
                xs = core.x[:, b * TB + 4 * g:b * TB + 4 * g + 4, :]
                core.result(dve, turn)
                v.scalar_tensor_tensor(out=xs, in0=ps[:, turn.bank, :].rearrange("p (t d) -> p t d", d=D),
                                       scalar=mw.scal[:, 1:2], in1=xs, op0=ALU.mult,
                                       op1=ALU.add).then_inc(core.emptied[turn.bank], 1)
        for b in range(B):
            for turn in self.t[b]["out"]:
                core.moved(dve, turn)


def program(nc, a, out):
    with ExitStack() as ctx:
        core = Core(nc, ctx)
        w = Weights(core, a)
        mw = MemoryWeights(core, w)
        blocks = [LinearAttention(core, w), ChannelMix(core, w, "cm1"),
                  Experts(core, w, w.e0, "top2", 2, ACT.Gelu_apprx_tanh, meanwhile=mw), ChannelMix(core, w, "cm2"),
                  SoftmaxAttention(core, w), Experts(core, w, w.e1, "top1a", 1, ACT.Silu),
                  LinearMemory(core, w, mw), Experts(core, w, w.e1, "top1b", 1, ACT.Silu, fresh=False)]
        w.arena_free = blocks[1].normed if len(blocks) > 1 else mw.loaded
        stored = core.sem("stored")
        final = core.sem("final")
        block = ctx.enter_context(nc.Block())

        @block.sync
        def _(sp):
            w.sync(sp, mw)
            for k in blocks:
                if isinstance(k, (Experts, SoftmaxAttention)):
                    k.sync(sp)
            sp.wait_ge(final, 1)
            sp.dma_start(out.rearrange("b (t p) d -> p b t d", p=P),
                         core.x[:, :, :].rearrange("p (b t) d -> p b t d", b=B)).then_inc(stored, 16)
            sp.wait_ge(stored, 16)

        @block.gpsimd
        def _(pool):
            w.gpsimd(pool)
            for k in blocks:
                if isinstance(k, (LinearAttention, Experts, SoftmaxAttention, LinearMemory)):
                    k.gpsimd(pool)

        @block.scalar
        def _(act):
            for k in blocks:
                k.scalar(act)

        @block.tensor
        def _(pe):
            for k in blocks:
                k.tensor(pe)

        @block.vector
        def _(dve):
            for k in blocks:
                k.vector(dve)
            dve.engine_nop().then_inc(final, 1)


def _constants():
    p = np.arange(P)
    freq = (1.0 / np.float32(10000.0) ** (np.arange(0, HD, 2, dtype=np.float32) / HD)).astype(np.float32)
    angle = (np.arange(S, dtype=np.float32)[:, None] * freq[None, :]).astype(np.float32)
    angle = angle.reshape(TB, P, HD // 2).transpose(1, 0, 2)
    head = 4 * np.arange(NG)[None, :] + (p // FEAT)[:, None]
    col_head = np.concatenate([np.arange(D) // HD, np.arange(H)])
    return {
        "c_before": (p[:, None] < p[None, :]).astype(np.float32),
        "c_choice_ids": np.arange(2 * N, dtype=np.float32).reshape(2, T, P).transpose(2, 0, 1),
        "c_counting": np.arange(P, dtype=np.float32),
        "c_padding_rows": (2 * N + P * (np.arange(40)[None, :] % LANES) + p[:, None]).astype(np.float32),
        "c_ones": np.ones((P, P), np.float32),
        "c_expert_ids": np.arange(NE, dtype=np.float32) - NE,
        "c_not_first": (np.arange(NE * T) % T != 0).astype(np.float32),
        "c_tile_starts": np.arange(40, dtype=np.float32) * P,
        "c_rope": np.stack([np.cos(angle), np.sin(angle)], 1).astype(np.float32),
        "c_powers": np.stack([np.maximum(p[None, :] - 1 - p[:, None], 0), np.broadcast_to(p[None, :], (P, P)),
                              p[:, None] < p[None, :]], 1).astype(np.float32),
        "c_to_end": (P - 1 - p[:, None]).astype(np.float32),
        "c_ident": np.eye(P, dtype=np.float32),
        "c_head_mask": (p[:, None] // HD == np.arange(H)[None, :]).astype(np.float32),
        "c_kv_mask": (head[:, :, None] == col_head[None, None, :]).astype(np.float32),
    }


def _layouts(i):
    d = {k: v for k, v in i.items()}
    for n in "rkv":
        d[f"L0_ffn_W_{n}T"] = i[f"L0_ffn_W_{n}"].T
    d["L0_attn_a_bqkv"] = np.concatenate([i["L0_attn_a_b" + n] for n in "qkv"])
    d["L1_attn_a_bqkv"] = np.concatenate([i["L1_attn_a_b" + n] for n in "qkv"])
    d["L1_attn_a_b1_cols"] = i["L1_attn_a_b1"].reshape(FC, P).T
    d["L0_attn_b_b1_cols"] = i["L0_attn_b_b1"].reshape(NE * FC, P).T
    d["L1_ffn_b1_cols"] = i["L1_ffn_b1"].reshape(NE * FC, P).T
    d["L1_attn_b_basisT"] = i["L1_attn_b_basis"].T
    d["L1_attn_b_coeffT"] = np.stack([i[f"L1_attn_b_{n}_coeffs"].T for n in "qkvo"], 1)
    d["L0_attn_a_proj"] = i["L0_attn_a_projection"].transpose(0, 2, 1).reshape(P, FEAT)
    return d


_UNUSED = {"L0_ffn_W_r", "L0_ffn_W_k", "L0_ffn_W_v", "L0_attn_a_bq", "L0_attn_a_bk", "L0_attn_a_bv",
           "L0_attn_a_projection", "L1_attn_a_bq", "L1_attn_a_bk", "L1_attn_a_bv", "L1_attn_a_b1", "L0_attn_b_b1", "L1_ffn_b1", "L1_attn_b_basis",
           "L1_attn_b_q_coeffs", "L1_attn_b_k_coeffs", "L1_attn_b_v_coeffs", "L1_attn_b_o_coeffs"}


def kernel(**inputs):
    import concourse.bacc as _bacc
    from concourse.bass_utils import run_bass_kernel_spmd as _run

    nc = _bacc.Bacc("TRN2", target_bir_lowering=False, num_devices=1)
    given = {k: np.asarray(v) for k, v in inputs.items()}
    data = {**_layouts(given), **_constants()}
    arrays, args = {}, {}
    for name in sorted(data):
        if name in _UNUSED:
            continue
        a = np.ascontiguousarray(data[name] if np.ndim(data[name]) else np.reshape(data[name], (1,)))
        arrays[f"in_{name}_dram"] = a
        args[name] = nc.dram_tensor(f"in_{name}_dram", a.shape, mybir.dt.from_np(a.dtype), kind="ExternalInput").ap()
    out = nc.dram_tensor("out_0_dram", (B, S, D), F32, kind="ExternalOutput").ap()
    program(nc, args, out)
    r = _run(nc, [arrays], core_ids=[0])
    return r.results[0]["out_0_dram"]
```
